# Optimizing a Trainium2 kernel written in Bass

```python
import numpy as np
import jax
import jax.numpy as jnp

def _softmax(x, axis=-1):
    return jax.nn.softmax(x, axis=axis)

def _gelu(x):
    return jax.nn.gelu(x, approximate=True)

def _silu(x):
    return jax.nn.silu(x)

def _sigmoid(x):
    return jax.nn.sigmoid(x)

def _layernorm(x, axis=-1, eps=1e-05):
    m = jnp.mean(x, axis=axis, keepdims=True)
    v = jnp.var(x, axis=axis, keepdims=True)
    return (x - m) / jnp.sqrt(v + eps)

def _scatter_add(tgt, idx, src, axis=0):
    return tgt.at[idx].add(src)

def _segment_sum(src, seg, n):
    return jax.ops.segment_sum(src, seg, n)
kernel_name = 'mk_decoder_postln_d1_seqx_r4_d3fbae'

def setup_inputs(seed: int=0):
    np.random.seed(seed)
    _w = jnp.asarray

    def _rec_inputs():
        import jax
        import jax.numpy as jnp
        _rk = jax.random.key(seed)
        x = 7.22e-05 + 1 * jax.random.normal(jax.random.fold_in(_rk, 1), (8, 112, 256), jnp.float32)
        _lenS = 112 - jax.random.randint(jax.random.fold_in(_rk, 7), (8,), 0, max(1, 112 // 4) + 1, jnp.int32)
        _lenS2 = 375 - jax.random.randint(jax.random.fold_in(_rk, 8), (8,), 0, max(1, 375 // 4) + 1, jnp.int32)
        _ctx_1024P = jax.random.normal(jax.random.fold_in(_rk, 11), (8, 16, 256), jnp.float32)
        _ctx_1024c = jax.random.dirichlet(jax.random.fold_in(_rk, 511), 0.3 * jnp.ones((16,), jnp.float32), (8, 375))
        _ctx_1024t = jnp.einsum('bsk,bkd->bsd', _ctx_1024c, _ctx_1024P)
        _ctx_1024t = _ctx_1024t * jax.lax.rsqrt(jnp.mean(jnp.square(_ctx_1024t)) + 1e-12) * 0.953939
        ctx_1024 = 4.13588e-05 + 0.999923 * (_ctx_1024t + 0.3 * jax.random.normal(jax.random.fold_in(_rk, 611), (8, 375, 256), jnp.float32))
        _validS = jnp.arange(112)[None, :] < _lenS[:, None]
        _validS2 = jnp.arange(375)[None, :] < _lenS2[:, None]
        _causal = jnp.tril(jnp.ones((112, 112), dtype=bool))
        mask_Bx1xS2_ik0 = jnp.where(jnp.broadcast_to(_validS2[:, None, :], (8, 1, 375)), 0, 1).astype(jnp.int32)
        return (x, ctx_1024, mask_Bx1xS2_ik0)
    x, ctx_1024, mask_Bx1xS2_ik0 = _rec_inputs()

    def _L0_attn_setup():
        import jax, jax.numpy as jnp
        import numpy as np
        B, L, DM = (2, 512, 256)
        DI, N, R, W = (512, 16, 64, 4)
        BETA, ALPHA, NS_STEPS = (0.9, 1.0, 1)

        def _newton_schulz(G):
            a, b, c = (3.4445, -4.775, 2.0315)
            X = G.T / (jnp.linalg.norm(G) + 1e-07)
            for _ in range(NS_STEPS):
                A = X @ X.T
                Bm = b * A + c * (A @ A)
                X = a * X + Bm @ X
            return X.T
        key = jax.random.key(seed)
        ks = jax.random.split(key, 8)
        s = 0.02
        return {'hidden_states': jax.random.normal(ks[0], (B, L, DM), jnp.float32), 'in_proj_w': jax.random.normal(ks[1], (2 * DI, DM), jnp.float32) * s, 'conv_w': jax.random.normal(ks[2], (DI, 1, W), jnp.float32) * s, 'conv_b': jnp.zeros((DI,), jnp.float32), 'x_proj_w': jax.random.normal(ks[3], (R + 2 * N, DI), jnp.float32) * s, 'dt_head_w': jax.random.normal(ks[4], (DI, R), jnp.float32) * s, 'dt_head_b': jax.random.normal(ks[5], (DI,), jnp.float32) * s, 'out_proj_w': jax.random.normal(ks[6], (DM, DI), jnp.float32) * s, 'D': jnp.ones((DI,), jnp.float32)}
    _L0_attn_all = _L0_attn_setup()
    _L0_attn_in = {k: v for k, v in _L0_attn_all.items() if k in ('in_proj_w', 'conv_w', 'conv_b', 'x_proj_w', 'dt_head_w', 'dt_head_b', 'out_proj_w', 'D')}
    del _L0_attn_all

    def _L0_xattn_setup():
        import jax, jax.numpy as jnp
        import numpy as np
        B, L, D, H = (4, 512, 256, 16)
        DK = D // H
        key = jax.random.key(seed)
        ks = jax.random.split(key, 12)
        s = 1.0 / np.sqrt(D)
        inp = {'query': jax.random.normal(ks[0], (B, L, D), jnp.float32), 'key': jax.random.normal(ks[1], (B, L, D), jnp.float32), 'value': jax.random.normal(ks[2], (B, L, D), jnp.float32), 'mask': jax.random.randint(ks[3], (B, 1, L), 0, 2, jnp.int32), 'Wq': jax.random.normal(ks[4], (D, D), jnp.float32) * s, 'bq': jnp.zeros((D,), jnp.float32), 'Wk': jax.random.normal(ks[5], (D, D), jnp.float32) * s, 'bk': jnp.zeros((D,), jnp.float32), 'Wv': jax.random.normal(ks[6], (D, D), jnp.float32) * s, 'bv': jnp.zeros((D,), jnp.float32), 'Wo': jax.random.normal(ks[7], (D, D), jnp.float32) * s, 'bo': jnp.zeros((D,), jnp.float32)}
        return inp
    _L0_xattn_all = _L0_xattn_setup()
    _L0_xattn_in = {k: v for k, v in _L0_xattn_all.items() if k in ('Wq', 'bq', 'Wk', 'bk', 'Wv', 'bv', 'Wo', 'bo')}
    del _L0_xattn_all

    def _L0_ffn_setup():
        import jax, jax.numpy as jnp
        import numpy as np
        B, S, H, F, E = (1, 512, 256, 512, 8)

        def _swiglu(x, wg, wu, wd):
            return jax.nn.silu(x @ wg.T) * (x @ wu.T) @ wd.T
        key = jax.random.key(seed)
        ks = jax.random.split(key, 8)
        sc = 1.0 / np.sqrt(H)
        scf = 1.0 / np.sqrt(F)
        return {'hidden_states': jax.random.normal(ks[0], (B, S, H), jnp.float32), 'gate_w': jax.random.normal(ks[1], (E, H), jnp.float32) * sc, 'shared_gate': jax.random.normal(ks[2], (F, H), jnp.float32) * sc, 'shared_up': jax.random.normal(ks[3], (F, H), jnp.float32) * sc, 'shared_down': jax.random.normal(ks[4], (H, F), jnp.float32) * scf, 'r_gate': jax.random.normal(ks[5], (E, F, H), jnp.float32) * sc, 'r_up': jax.random.normal(ks[6], (E, F, H), jnp.float32) * sc, 'r_down': jax.random.normal(ks[7], (E, H, F), jnp.float32) * scf}
    _L0_ffn_all = _L0_ffn_setup()
    _L0_ffn_in = {k: v for k, v in _L0_ffn_all.items() if k in ('gate_w', 'shared_gate', 'shared_up', 'shared_down', 'r_gate', 'r_up', 'r_down')}
    del _L0_ffn_all
    return {'x': x, 'ctx_1024': ctx_1024, 'mask_Bx1xS2_ik0': mask_Bx1xS2_ik0, 'L0_attn_in_proj_w': _L0_attn_in['in_proj_w'], 'L0_attn_conv_w': _L0_attn_in['conv_w'], 'L0_attn_conv_b': _L0_attn_in['conv_b'], 'L0_attn_x_proj_w': _L0_attn_in['x_proj_w'], 'L0_attn_dt_head_w': _L0_attn_in['dt_head_w'], 'L0_attn_dt_head_b': _L0_attn_in['dt_head_b'], 'L0_attn_out_proj_w': _L0_attn_in['out_proj_w'], 'L0_attn_D': _L0_attn_in['D'], 'L0_xattn_Wq': _L0_xattn_in['Wq'], 'L0_xattn_bq': _L0_xattn_in['bq'], 'L0_xattn_Wk': _L0_xattn_in['Wk'], 'L0_xattn_bk': _L0_xattn_in['bk'], 'L0_xattn_Wv': _L0_xattn_in['Wv'], 'L0_xattn_bv': _L0_xattn_in['bv'], 'L0_xattn_Wo': _L0_xattn_in['Wo'], 'L0_xattn_bo': _L0_xattn_in['bo'], 'L0_ffn_gate_w': _L0_ffn_in['gate_w'], 'L0_ffn_shared_gate': _L0_ffn_in['shared_gate'], 'L0_ffn_shared_up': _L0_ffn_in['shared_up'], 'L0_ffn_shared_down': _L0_ffn_in['shared_down'], 'L0_ffn_r_gate': _L0_ffn_in['r_gate'], 'L0_ffn_r_up': _L0_ffn_in['r_up'], 'L0_ffn_r_down': _L0_ffn_in['r_down']}

def reference(x, ctx_1024, mask_Bx1xS2_ik0, L0_attn_in_proj_w, L0_attn_conv_w, L0_attn_conv_b, L0_attn_x_proj_w, L0_attn_dt_head_w, L0_attn_dt_head_b, L0_attn_out_proj_w, L0_attn_D, L0_xattn_Wq, L0_xattn_bq, L0_xattn_Wk, L0_xattn_bk, L0_xattn_Wv, L0_xattn_bv, L0_xattn_Wo, L0_xattn_bo, L0_ffn_gate_w, L0_ffn_shared_gate, L0_ffn_shared_up, L0_ffn_shared_down, L0_ffn_r_gate, L0_ffn_r_up, L0_ffn_r_down):
    import jax
    import jax.numpy as jnp

    def _L0_attn_ref(hidden_states, in_proj_w, conv_w, conv_b, x_proj_w, dt_head_w, dt_head_b, out_proj_w, D):
        import jax, jax.numpy as jnp
        import numpy as np
        B, L, DM = (2, 512, 256)
        DI, N, R, W = (512, 16, 64, 4)
        BETA, ALPHA, NS_STEPS = (0.9, 1.0, 1)

        def _newton_schulz(G):
            a, b, c = (3.4445, -4.775, 2.0315)
            X = G.T / (jnp.linalg.norm(G) + 1e-07)
            for _ in range(NS_STEPS):
                A = X @ X.T
                Bm = b * A + c * (A @ A)
                X = a * X + Bm @ X
            return X.T
        b, l, _ = hidden_states.shape
        xz = jnp.einsum('bld,ed->bel', hidden_states, in_proj_w)
        x, z = jnp.split(xz, 2, axis=1)
        x = jax.lax.conv_general_dilated(x, conv_w, (1,), [(W - 1, 0)], dimension_numbers=('NCH', 'OIH', 'NCH'), feature_group_count=DI)
        x = x + conv_b[None, :, None]
        x = x * jax.nn.sigmoid(x)
        xt = x.transpose(0, 2, 1)
        x_dbl = xt @ x_proj_w.T
        dt_low, k, q = jnp.split(x_dbl, [R, R + N], axis=-1)
        dt = jax.nn.softplus(dt_low @ dt_head_w.T + dt_head_b)

        def step(carry, inp):
            S, m = carry
            xi, ki, qi, di = inp
            eps = di / (1.0 + di * jnp.sum(ki * ki, axis=-1, keepdims=True))
            err = jnp.einsum('bdn,bn->bd', S, ki) - xi
            grad = (eps * err)[..., None] * ki[:, None, :]
            m = BETA * m + grad
            S = S - ALPHA * jax.vmap(_newton_schulz)(m)
            y = jnp.einsum('bdn,bn->bd', S, qi)
            return ((S, m), y)
        S0 = jnp.zeros((b, DI, N), xt.dtype)
        m0 = jnp.zeros_like(S0)
        inps = (xt.transpose(1, 0, 2), k.transpose(1, 0, 2), q.transpose(1, 0, 2), dt.transpose(1, 0, 2))
        _, ys = jax.lax.scan(step, (S0, m0), inps)
        y = ys.transpose(1, 0, 2) + D * xt
        zt = z.transpose(0, 2, 1)
        y = y * (zt * jax.nn.sigmoid(zt))
        return y @ out_proj_w.T

    def _L0_xattn_ref(query, key, value, mask, Wq, bq, Wk, bk, Wv, bv, Wo, bo):
        import jax, jax.numpy as jnp
        import numpy as np
        B, L, D, H = (4, 512, 256, 16)
        DK = D // H
        nb = query.shape[0]

        def proj(x, W, b):
            return (x @ W.T + b).reshape(nb, -1, H, DK).transpose(0, 2, 1, 3)
        q = proj(query, Wq, bq)
        k = proj(key, Wk, bk)
        v = proj(value, Wv, bv)
        scale = 1.0 / jnp.sqrt(jnp.asarray(DK, q.dtype))
        score = jnp.einsum('bhqd,bhkd->bhqk', q, k) * scale
        m = mask[:, None, :, :]
        score = jnp.where(m == 0, jnp.asarray(-1000000000.0, score.dtype), score)
        p = jax.nn.softmax(score, axis=-1)
        x = jnp.einsum('bhqk,bhkd->bhqd', p, v)
        x = x.transpose(0, 2, 1, 3).reshape(nb, -1, H * DK)
        return x @ Wo.T + bo

    def _L0_ffn_ref(hidden_states, gate_w, shared_gate, shared_up, shared_down, r_gate, r_up, r_down):
        import jax, jax.numpy as jnp
        import numpy as np
        B, S, H, F, E = (1, 512, 256, 512, 8)

        def _swiglu(x, wg, wu, wd):
            return jax.nn.silu(x @ wg.T) * (x @ wu.T) @ wd.T
        b, s, h = hidden_states.shape
        x = hidden_states.reshape(-1, h)
        shared_out = _swiglu(x, shared_gate, shared_up, shared_down)
        logits = x @ gate_w.T
        top_id = jnp.argmax(logits, axis=-1)
        score = jax.nn.sigmoid(jnp.max(logits, axis=-1))
        xs = x * score[:, None]

        def body(acc, ws):
            wg, wu, wd, e = ws
            xe = jnp.where((top_id == e)[:, None], xs, 0.0)
            return (acc + _swiglu(xe, wg, wu, wd), None)
        acc0 = jnp.zeros_like(x)
        routed_out, _ = jax.lax.scan(body, acc0, (r_gate, r_up, r_down, jnp.arange(E)))
        return (shared_out + routed_out).reshape(b, s, h)
    x = _layernorm(x + _L0_attn_ref(x, L0_attn_in_proj_w, L0_attn_conv_w, L0_attn_conv_b, L0_attn_x_proj_w, L0_attn_dt_head_w, L0_attn_dt_head_b, L0_attn_out_proj_w, L0_attn_D), axis=-1)
    x = _layernorm(x + _L0_xattn_ref(x, ctx_1024, ctx_1024, mask_Bx1xS2_ik0, L0_xattn_Wq, L0_xattn_bq, L0_xattn_Wk, L0_xattn_bk, L0_xattn_Wv, L0_xattn_bv, L0_xattn_Wo, L0_xattn_bo), axis=-1)
    x = _layernorm(x + _L0_ffn_ref(x, L0_ffn_gate_w, L0_ffn_shared_gate, L0_ffn_shared_up, L0_ffn_shared_down, L0_ffn_r_gate, L0_ffn_r_up, L0_ffn_r_down), axis=-1)
    return x

_drawn_inputs = setup_inputs


def setup_inputs(seed=0):
    import zlib

    import numpy as np

    out = dict(_drawn_inputs(seed))
    spreads = {'L0_attn_conv_b': (0.0, 0.533),
     'L0_attn_D': (1.0, 0.6),
     'L0_xattn_bq': (0.0, 0.1),
     'L0_xattn_bk': (0.0, 0.8),
     'L0_xattn_bv': (0.0, 0.1),
     'L0_xattn_bo': (0.0, 0.1)}
    factors = {'L0_attn_in_proj_w': 4.308,
     'L0_attn_conv_w': 8.0,
     'L0_attn_x_proj_w': 4.804,
     'L0_attn_dt_head_w': 8.0,
     'L0_attn_dt_head_b': 8.0,
     'L0_attn_out_proj_w': 3.518}
    for name, (base, spread) in spreads.items():
        noise = np.random.default_rng([zlib.crc32(name.encode()), seed]).standard_normal(out[name].shape)
        drawn = base * np.exp(spread * noise) if base else spread * noise
        out[name] = jnp.asarray(drawn.astype(out[name].dtype))
    for name, factor in factors.items():
        out[name] = (out[name] * factor).astype(out[name].dtype)
    return out
```

```python
import numpy as np

import concourse.bass as bass
from concourse import mybir
from contextlib import ExitStack

B, L, DM = 8, 112, 256
DI, N, R, W = 512, 16, 64, 4
S2 = 375
H, DK = 16, 16
F, E = 512, 8
P = 128
C = DI // P
MC = DM // P
T = B * L
HT = T // 2
HL = L // 2
BN = B * N
KC = 3
KW = S2 // KC
LP = L + 2
BETA = 0.9
NS_A, NS_B, NS_C = 3.4445, -4.775, 2.0315
LEAD = 1
NEG = 1e9
TINY = 1e-7
EPS = 1e-5

F32 = mybir.dt.float32
I32 = mybir.dt.int32
ALU = mybir.AluOpType
ACT = mybir.ActivationFunctionType
AX = mybir.AxisListType


def spread(ap, axis, n):
    a = ap.unsqueeze(axis)
    shape = list(a.shape)
    shape[axis] = n
    return a.broadcast_to(shape)


def decoder_kernel(nc, io, out):
    with ExitStack() as ctx:
        def sb(name, shape, dt=F32):
            return ctx.enter_context(nc.sbuf_tensor(name, shape, dt))

        def sem(name):
            return ctx.enter_context(nc.semaphore(name))

        bank = [ctx.enter_context(nc.psum_tensor(f"bank{i}", [P, 512], F32)) for i in range(8)]

        ident = sb("ident", [P, P])
        neg_ident = sb("neg_ident", [P, P])
        ones = sb("ones", [P, P])
        block_ones = sb("block_ones", [P, P])
        block_mask = sb("block_mask", [P, B, N])
        small = sb("small", [P, 96])
        batch_mask, half_batch_mask = small[:, 0:8], small[:, 64:96]
        col_mask, scaled_eye = small[:, 16:32], small[:, 32:48]
        mask_gain, mask_base, eps_ln = small[:, 48:49], small[:, 49:50], small[:, 50:51]
        tie_rank = small[:, 52:60]
        step_gain = sb("step_gain", [P, L])

        conv_w = sb("conv_w", [P, C, W])
        vecs = sb("vecs", [P, 3, C])
        bias_qk = sb("bias_qk", [P, 2, 4])
        bias_rows = sb("bias_rows", [P, 2, DM])
        w_out = sb("w_out", [P, C, DM])

        x_a = sb("x_a", [P, LP, C, B])
        z_a = sb("z_a", [P, L, C, B])
        eps_a = sb("eps_a", [P, L, C, B])
        y_a = sb("y_a", [P, LP, C, B])
        kq = sb("kq", [P, LP, 2 * B])
        k_col = sb("k_col", [P, L])
        ks_col = sb("ks_col", [P, L])
        rec = sb("rec", [P, L, 2 + 3 * N + 1])
        F_COL, F_NEXT, F_ROW = slice(0, 1), slice(1, 1 + N), slice(1 + N, 1 + 2 * N)
        F_SPREAD, F_TINY = slice(1 + 2 * N, 2 + 3 * N), slice(2 + 3 * N, 3 + 3 * N)
        now = [sb(f"now{i}", [P, 2 + 3 * N + 1]) for i in range(2)]
        arena = sb("arena", [P, 23000])
        ks_all = arena[:, 0:L * BN].rearrange("p (t n) -> p t n", t=L)

        m_a = sb("m_a", [P, C, BN])
        m_b = sb("m_b", [P, C, P])
        s_b = sb("s_b", [P, C, P])
        outer = sb("outer", [P, C, BN])
        g_a = sb("g_a", [P, C, B])
        g_sq = sb("g_sq", [P, C, B])
        junk2 = sb("junk2", [P, C * B])
        gram = sb("gram", [P, N])
        gram1 = sb("gram1", [P, N])
        gram_bd = sb("gram_bd", [P, B, N])
        poly = sb("poly", [P, N])
        ns_p = sb("ns_p", [P, N])
        p_bd = sb("p_bd", [P, B, N])
        w_bd = sb("w_bd", [P, B])
        v_diag = sb("v_diag", [P, N + 1])
        junk = sb("junk", [P, 4, N])
        cols = sb("cols", [P, 16])
        u_col, v_col, w_col, trace = cols[:, 0:1], cols[:, 1:2], cols[:, 2:3], cols[:, 3:4]
        root, norm, rneg, r2b, r4c = (cols[:, i:i + 1] for i in range(4, 9))

        ks_dram = nc.dram_tensor("ks_dram", [L, BN], F32, kind="Internal").ap()

        at = [0]

        def take(n):
            at[0] += n
            assert at[0] <= 23000
            return arena[:, at[0] - n:at[0]]

        xt = take(MC * T).rearrange("p (m t) -> p m t", m=MC)
        w_in = take(MC * 2 * DI).rearrange("p (m e) -> p m e", m=MC)
        x_in = take(C * (L + W - 1) * B).rearrange("p (c t b) -> p c t b", c=C, b=B)
        conv = take(2 * T).rearrange("p (u t) -> p u t", u=2)
        w_dt_lo = take(C * R).rearrange("p (c r) -> p c r", c=C)
        w_k = take(C * BN).rearrange("p (c n) -> p c n", c=C)
        w_q = take(C * BN).rearrange("p (c n) -> p c n", c=C)
        w_dt = take(DI)[0:R, :]
        dt_lo = take(T)[0:R, :]
        k_sq = take(L * B).rearrange("p (t b) -> p t b", b=B)
        ks_t = take(P)[0:L, :]
        kd_row = y_a[:, 0:LP].rearrange("p t c b -> p (t c b)")[:, 0:L * N].rearrange("p (t n) -> p t n", n=N)
        sp_a = x_in.rearrange("p c t b -> p (c t b)")[:, 0:HL * C * B]
        sp_e = x_in.rearrange("p c t b -> p (c t b)")[:, HL * C * B:2 * HL * C * B]
        sp_u = xt.rearrange("p m t -> p (m t)")[:, 0:HL * C * B]
        sp_l = w_in.rearrange("p m t -> p (m t)")[:, 0:HL * C * B]

        at[0] = 0
        x2t = take(MC * T).rearrange("p (m t) -> p m t", m=MC)
        xst = take(MC * T).rearrange("p (m t) -> p m t", m=MC)
        x2 = take(B * DM).rearrange("p (b d) -> p b d", b=B)
        acc = take(B * DM).rearrange("p (b d) -> p b d", b=B)
        onehot = take(B * E).rearrange("p (b e) -> p b e", b=B)
        base = at[0]
        wq = take(MC * 512).rearrange("p (m e) -> p m e", m=MC)
        wk = take(MC * 512).rearrange("p (m e) -> p m e", m=MC)
        wv = take(MC * DM).rearrange("p (m e) -> p m e", m=MC)
        wo = take(MC * DM).rearrange("p (m e) -> p m e", m=MC)
        w_gate = take(MC * E).rearrange("p (m e) -> p m e", m=MC)
        ctx_t = take(MC * S2).rearrange("p (m s) -> p m s", m=MC)
        mask_f = take(S2)
        k_t = take(4 * S2).rearrange("p (g s) -> p g s", g=4)
        v_t = take(KC * DM).rearrange("p (k e) -> p k e", k=KC)
        q_t = take(4 * L).rearrange("p (g s) -> p g s", g=4)
        prob = take(2 * S2).rearrange("p (u s) -> p u s", u=2)
        prob_t = take(2 * KC * L).rearrange("p (u k s) -> p u k s", u=2, k=KC)
        y_b = take(C * L).rearrange("p (c t) -> p c t", c=C)
        y_tmp = take(C * L).rearrange("p (c t) -> p c t", c=C)
        xb = take(DM)
        x1 = take(DM)
        h1 = take(DM)
        att = take(DM)
        x1t = take(MC * L).rearrange("p (m t) -> p m t", m=MC)
        at_t = take(MC * L).rearrange("p (m t) -> p m t", m=MC)
        xs = take(DM)
        lg = take(E)
        lg2 = take(E)
        stat = take(64)
        row_max = take(H)
        row_sum = take(H)
        row_inv = take(H)
        mask_i = sb("mask_i", [P, S2], I32)
        at[0] = base
        wg = take(MC * F).rearrange("p (m f) -> p m f", m=MC)
        wu = take(MC * F).rearrange("p (m f) -> p m f", m=MC)
        hid = take(C * T).rearrange("p (c t) -> p c t", c=C)
        gate = take(2 * HT).rearrange("p (u t) -> p u t", u=2)
        wd = sb("wd", [P, 2, C, DM])
        wg2 = x_a[:, 0:32].rearrange("p t c b -> p (t c b)").rearrange("p (m f) -> p m f", m=MC)
        wu2 = x_a[:, 32:64].rearrange("p t c b -> p (t c b)").rearrange("p (m f) -> p m f", m=MC)
        wg_s, wu_s = [wg, wg2], [wu, wu2]
        fin = x_a[:, 64:72].rearrange("p t c b -> p (t c b)")
        stat3 = x_a[:, 80:82].rearrange("p t c b -> p (t c b)")

        const_in, pre_in, k_out, ks_in = sem("const_in"), sem("pre_in"), sem("k_out"), sem("ks_in")
        zeroed = sem("zeroed")
        xz_ready, x_moved, z_done = sem("xz_ready"), sem("x_moved"), sem("z_done")
        conv_ready, conv_step, x_ready = sem("conv_ready"), sem("conv_step"), sem("x_ready")
        lo_ready, lo_moved = sem("lo_ready"), sem("lo_moved")
        kq_ready, kq_moved = sem("kq_ready"), sem("kq_moved")
        dt_ready, sp_act, sp_dve = sem("dt_ready"), sem("sp_act"), sem("sp_dve")
        tab, row_done, row_moved = sem("tab"), sem("row_done"), sem("row_moved")
        kt_ready, kt_moved, sq_ready, sq_moved = sem("kt_ready"), sem("kt_moved"), sem("sq_ready"), sem("sq_moved")
        base_ready, err_ready, g_ready, y_saved = sem("base_ready"), sem("err_ready"), sem("g_ready"), sem("y_saved")
        gsq_ready = sem("gsq_ready")
        mg_ready, gg_ready, u_ready, v_ready = sem("mg_ready"), sem("gg_ready"), sem("u_ready"), sem("v_ready")
        vd_ready, gram1_ready, spread_ready = sem("vd_ready"), sem("gram1_ready"), sem("spread_ready")
        trace_ready, gram_ready, bd_ready = sem("trace_ready"), sem("gram_ready"), sem("bd_ready")
        root_ready, scal, gram2_ready = sem("root_ready"), sem("scal"), sem("gram2_ready")
        poly_ready, p_ready, w_ready, wbd_ready = sem("poly_ready"), sem("p_ready"), sem("w_ready"), sem("wbd_ready")
        pbd_ready, outer_ready, ma_ready = sem("pbd_ready"), sem("outer_ready"), sem("ma_ready")
        mt_ready, mb_ready, s_ready, sb_ready = sem("mt_ready"), sem("mb_ready"), sem("s_ready"), sem("sb_ready")
        now_ready = sem("now_ready")
        att_in, batch_in, ctx_in, ctx_free = sem("att_in"), sem("batch_in"), sem("ctx_in"), sem("ctx_free")
        yb_ready, y_step, proj_ready, ln = sem("yb_ready"), sem("y_step"), sem("proj_ready"), sem("ln")
        std_ready, x1_ready, x1t_ready, x1t_moved = sem("std_ready"), sem("x1_ready"), sem("x1t_ready"), sem("x1t_moved")
        kp_ready, kp_moved, vp_ready, vp_moved = sem("kp_ready"), sem("kp_moved"), sem("vp_ready"), sem("vp_moved")
        qp_ready, q_moved, msk = sem("qp_ready"), sem("q_moved"), sem("msk")
        sc_ready, max_ready, exp_ready = sem("sc_ready"), sem("max_ready"), sem("exp_ready")
        pt_ready, pt_moved, pv_ready = sem("pt_ready"), sem("pt_moved"), sem("pv_ready")
        inv_ready, att_ready, att_t_ready, att_moved = sem("inv_ready"), sem("att_ready"), sem("att_t_ready"), sem("att_moved")
        wo_ready, x2_ready, x2t_ready, x2t_moved = sem("wo_ready"), sem("x2_ready"), sem("x2t_ready"), sem("x2t_moved")
        lg_ready, top, score_ready, xs_ready = sem("lg_ready"), sem("top"), sem("score_ready"), sem("xs_ready")
        xst_ready, xst_moved = sem("xst_ready"), sem("xst_moved")
        ffn_in = [sem("ffn_in0"), sem("ffn_in1")]
        gate_ready, up_ready, silu_ready, hid_ready = sem("gate_ready"), sem("up_ready"), sem("silu_ready"), sem("hid_ready")
        down_ready, acc_ready, ln3, std3_ready = sem("down_ready"), sem("acc_ready"), sem("ln3"), sem("std3_ready")
        y_ready, y_out, fin_free = sem("y_ready"), sem("y_out"), sem("fin_free")

        block = ctx.enter_context(nc.Block())

        @block.sync
        def _(sp):
            for s in (mb_ready, wbd_ready, pbd_ready, sb_ready, y_saved, w_ready, vp_moved, kp_moved, xst_moved,
                      exp_ready, pt_moved, vp_ready, kp_ready, msk, x1_ready, down_ready, fin_free, hid_ready,
                      acc_ready, pt_ready):
                sp.sem_inc(s, LEAD)
            for dst, name in ((ident, "c_ident"), (neg_ident, "c_neg"), (ones, "c_ones"),
                              (block_ones, "c_block"), (small, "c_small"), (step_gain, "c_gain")):
                sp.dma_start(dst[:, :], io[name]).then_inc(const_in, 16)
            sp.dma_start(block_mask[:, :, :], io["c_bmask"]).then_inc(const_in, 16)
            sp.dma_start(xt, io["xt"]).then_inc(pre_in, 16)
            sp.dma_start(w_in, io["w_in"]).then_inc(pre_in, 16)
            sp.dma_start(conv_w[:, :, :], io["conv_w"]).then_inc(const_in, 16)
            sp.dma_start(vecs[:, :, :], io["vecs"]).then_inc(const_in, 16)
            sp.dma_start(w_dt_lo, io["w_lo"]).then_inc(const_in, 16)
            sp.dma_start(w_k, io["w_k"]).then_inc(const_in, 16)
            sp.dma_start(w_q, io["w_q"]).then_inc(const_in, 16)
            sp.dma_start(w_dt, io["w_dt"]).then_inc(const_in, 16)
            sp.dma_start(w_out[:, :, :], io["w_out"]).then_inc(const_in, 16)
            sp.dma_start(bias_qk[:, :, :], io["bias_qk"]).then_inc(const_in, 16)
            sp.dma_start(bias_rows[:, :, :], io["bias_rows"]).then_inc(const_in, 16)
            sp.wait_ge(kt_moved, 1)
            sp.dma_start(ks_dram, ks_t).then_inc(k_out, 16)
            sp.wait_ge(k_out, 16)
            sp.wait_ge(sp_dve, 2 * 6)
            sp.wait_ge(row_moved, 4)
            sp.wait_ge(sq_moved, 2)
            for q in range(4):
                n = L // 4
                sp.dma_start(ks_all[:, q * n:(q + 1) * n, :],
                             ks_dram[q * n:(q + 1) * n, :].partition_broadcast(P)).then_inc(ks_in, 16)
            sp.wait_ge(ma_ready, L)
            sp.dma_start(wq, io["wq"]).then_inc(att_in, 16)
            sp.dma_start(wk, io["wk"]).then_inc(att_in, 16)
            sp.dma_start(wv, io["wv"]).then_inc(att_in, 16)
            sp.dma_start(wo, io["wo"]).then_inc(att_in, 16)
            sp.dma_start(w_gate, io["w_gate"]).then_inc(att_in, 16)

        @block.tensor
        def _(pe):
            mm = nc.tensor.matmul

            pe.wait_ge(pre_in, 32)
            for ec in range(2 * C):
                for hf in range(2):
                    n = ec * 2 + hf
                    if n >= 4:
                        pe.wait_ge(x_moved if (n - 4) // 2 < C else z_done, n - 3 if (n - 4) // 2 < C else n - 4 - 2 * C + 1)
                    for m in range(MC):
                        last = mm(bank[n % 4][:, 0:HT], w_in[:, m, ec * P:(ec + 1) * P],
                                  xt[:, m, hf * HT:(hf + 1) * HT], start=(m == 0), stop=(m == MC - 1))
                    last.then_inc(xz_ready, 1)
            pe.wait_ge(const_in, 16 * 16)
            pe.wait_ge(x_ready, C)
            for hf in range(2):
                xs_h = x_a[:, hf * HL:(hf + 1) * HL]
                for c in range(C):
                    last = mm(bank[4 + hf][0:R, 0:HT], w_dt_lo[:, c, :], xs_h[:, :, c, :],
                              start=(c == 0), stop=(c == C - 1))
                last.then_inc(lo_ready, 1)
            for j, wt in enumerate((w_k, w_q)):
                for hf in range(2):
                    xs_h = x_a[:, hf * HL:(hf + 1) * HL]
                    if j == 1:
                        pe.wait_ge(kq_moved, hf + 1)
                    for c in range(C):
                        last = mm(bank[6 + hf][:, 0:HT], wt[:, c, :], xs_h[:, :, c, :],
                                  start=(c == 0), stop=(c == C - 1))
                    last.then_inc(kq_ready, 1)
            pe.wait_ge(lo_moved, 2)
            pe.wait_ge(z_done, 2 * C)
            for hf in range(2):
                for c in range(C):
                    n = hf * C + c
                    if n >= 4:
                        pe.wait_ge(sp_act, n - 3)
                    mm(bank[c][:, 0:HT], w_dt[:, c * P:(c + 1) * P], dt_lo[:, hf * HT:(hf + 1) * HT],
                       start=True, stop=True).then_inc(dt_ready, 1)
            pe.wait_ge(tab, 3)
            nc.tensor.transpose(bank[4][0:L, 0:P], ks_col[:, :], ident[:, :]).then_inc(kt_ready, 1)
            pe.wait_ge(tab, 5)
            pe.wait_ge(kq_moved, 4)
            for hf in range(2):
                mm(bank[6 + hf][:, 0:HT], ones[:, :], k_sq[:, hf * HL:(hf + 1) * HL, :].rearrange("p t b -> p (t b)"),
                   start=True, stop=True).then_inc(sq_ready, 1)
            pe.wait_ge(tab, 6)
            for n in range(4):
                if n == 0:
                    pe.wait_ge(kt_moved, 1)
                if n >= 2:
                    pe.wait_ge(row_moved, n - 1)
                q = L // 4
                mm(bank[4 + n % 2][:, 0:q * N], block_ones[:, :],
                   kd_row[:, n * q:(n + 1) * q, :].rearrange("p t n -> p (t n)"),
                   start=True, stop=True).then_inc(row_done, 1)

            e_bank, mg_bank, gg_bank, sp_bank = bank[0:2], bank[2], bank[3], bank[4]
            g2_bank, st_bank, mt_bank = bank[5], bank[6], bank[7]

            def base_terms(t1, par):
                mm(e_bank[par][:, 0:64].rearrange("p (c v) -> p c v", c=C)[:, :, 0:B], neg_ident[:, :],
                   x_a[:, bass.ds(t1, 1)].rearrange("p o c b -> p (o c) b"), start=True, stop=False,
                   skip_group_check=True)
                for c in range(C):
                    last = mm(e_bank[par][:, c * 16:(c + 1) * 16], s_b[:, c, :],
                              kq[:, bass.ds(t1, 1), :].rearrange("p o v -> p (o v)"), start=False, stop=False,
                              skip_group_check=True)
                last.then_inc(base_ready, 1)

            def s_update(cs):
                for c in cs:
                    last = mm(st_bank[:, c * P:(c + 1) * P], p_bd[:, :, :].rearrange("p b n -> p (b n)"),
                              m_b[:, c, :], start=False, stop=False, skip_group_check=True)
                return last

            pe.wait_ge(zeroed, 12)
            pe.wait_ge(sp_act, 7 + 4)
            pe.wait_ge(row_moved, 4)
            pe.wait_ge(sq_moved, 2)
            mm(st_bank[:, :], p_bd[:, :, :].rearrange("p b n -> p (b n)"), m_b[:, :, :].rearrange("p c n -> p (c n)"),
               start=True, stop=False, skip_group_check=True)
            base_terms(0, 0)
            with pe.Fori(0, L // 2) as i:
                for par in range(2):
                    t = i * 2 + par
                    pe.wait_ge(mb_ready, LEAD + t)
                    pe.wait_ge(wbd_ready, LEAD + t)
                    for c in range(C):
                        last = mm(e_bank[par][:, c * 16:c * 16 + B], m_b[:, c, :], w_bd[:, :],
                                  start=False, stop=True, skip_group_check=True)
                    last.then_inc(err_ready, 1)
                    pe.wait_ge(pbd_ready, LEAD + t)
                    pe.wait_ge(sb_ready, LEAD + t)
                    s_update((0, 1))
                    pe.wait_ge(g_ready, t + 1)
                    for c in range(C):
                        last = mm(mg_bank[:, 0:B], m_a[:, c, :], g_a[:, c, :], start=(c == 0), stop=(c == C - 1))
                    last.then_inc(mg_ready, 1)
                    pe.wait_ge(gsq_ready, t + 1)
                    mm(gg_bank[:, 0:C * B], ones[:, :], g_sq[:, :, :].rearrange("p c b -> p (c b)"),
                       start=True, stop=True).then_inc(gg_ready, 1)
                    s_update((2, 3)).then_inc(s_ready, 1)
                    pe.wait_ge(vd_ready, t + 1)
                    mm(sp_bank[:, 0:N + 1], block_ones[:, :], v_diag[:, :], start=True, stop=True).then_inc(spread_ready, 1)
                    pe.wait_ge(bd_ready, t + 1)
                    mm(g2_bank[:, 0:N], gram_bd[:, :, :].rearrange("p b n -> p (b n)"), gram[:, :],
                       start=True, stop=True).then_inc(gram2_ready, 1)
                    pe.wait_ge(sb_ready, LEAD + t + 1)
                    pe.wait_ge(y_saved, LEAD + t)
                    base_terms(t + 1, 1 - par)
                    pe.wait_ge(ma_ready, t + 1)
                    pe.wait_ge(mb_ready, LEAD + t)
                    for c in range(C):
                        last = nc.tensor.transpose(mt_bank[:, c * P:(c + 1) * P], m_a[:, c, :], ident[:, :])
                    last.then_inc(mt_ready, 1)
            pe.wait_ge(mb_ready, LEAD + L)
            pe.wait_ge(pbd_ready, LEAD + L)
            pe.wait_ge(sb_ready, LEAD + L)
            s_update(range(C)).then_inc(s_ready, 1)
            pe.wait_ge(sb_ready, LEAD + L + 1)
            pe.wait_ge(y_saved, LEAD + L)
            base_terms(L + 1, (L + 1) % 2)

            misc = bank[5]
            pe.wait_ge(att_in, 16 * 5)
            pe.wait_ge(y_saved, LEAD + LP)
            with pe.Fori(0, B) as b:
                pe.wait_ge(batch_in, (b + 1) * 48)
                for g in range(4):
                    if g < 2:
                        pe.wait_ge(vp_moved, LEAD + b * KC)
                        pe.wait_ge(kp_moved, LEAD + b * 4)
                    else:
                        pe.wait_ge(kp_moved, LEAD + b * 4 + (g - 1))
                    for m in range(MC):
                        last = mm(bank[6 + g % 2][:, 0:S2], wk[:, m, g * P:(g + 1) * P], ctx_t[:, m, :],
                                  start=(m == 0), stop=(m == MC - 1))
                    last.then_inc(kp_ready, 1)
                for k in range(KC):
                    if k < 2:
                        pe.wait_ge(kp_moved, LEAD + b * 4 + 3 + k)
                    else:
                        pe.wait_ge(vp_moved, LEAD + b * KC + 1)
                    for m in range(MC):
                        last = mm(bank[6 + k % 2][0:KW, 0:DM], ctx_t[:, m, k * KW:(k + 1) * KW], wv[:, m, :],
                                  start=(m == 0), stop=(m == MC - 1))
                    last.then_inc(vp_ready, 1)
                pe.wait_ge(yb_ready, b + 1)
                pe.wait_ge(xst_moved, LEAD + b)
                for c in range(C):
                    last = mm(misc[0:L, 0:DM], y_b[:, c, :], w_out[:, c, :], start=(c == 0), stop=(c == C - 1))
                last.then_inc(proj_ready, 1)
                pe.wait_ge(x1_ready, LEAD + b + 1)
                for m in range(MC):
                    last = nc.tensor.transpose(misc[:, m * L:(m + 1) * L], x1[0:L, m * P:(m + 1) * P], ident[0:L, 0:L])
                last.then_inc(x1t_ready, 1)
                pe.wait_ge(x1t_moved, b + 1)
                for g in range(4):
                    for m in range(MC):
                        last = mm(misc[:, g * L:(g + 1) * L], wq[:, m, g * P:(g + 1) * P], x1t[:, m, :],
                                  start=(m == 0), stop=(m == MC - 1))
                last.then_inc(qp_ready, 1)
                pe.wait_ge(q_moved, b + 1)
                pe.wait_ge(kp_moved, LEAD + b * 4 + 4)
                pe.wait_ge(vp_moved, LEAD + b * KC + KC)

                def scores(h):
                    if h < 2:
                        pe.wait_ge(exp_ready, LEAD + b * H)
                    else:
                        pe.wait_ge(exp_ready, LEAD + b * H + (h - 1))
                    r = 32 * (h % 4)
                    mm(bank[h % 2][0:L, 0:S2], q_t[r:r + 32, h // 4, :], k_t[r:r + 32, h // 4, :],
                       start=True, stop=True).then_inc(sc_ready, 1)

                def turn(h):
                    pe.wait_ge(exp_ready, LEAD + b * H + (h + 1))
                    if h < 2:
                        pe.wait_ge(pt_moved, LEAD + b * H)
                    else:
                        pe.wait_ge(pt_moved, LEAD + b * H + (h - 1))
                    for k in range(KC):
                        last = nc.tensor.transpose(bank[2 + h % 2][0:KW, k * L:(k + 1) * L],
                                                   prob[0:L, h % 2, k * KW:(k + 1) * KW], ident[0:L, 0:L])
                    last.then_inc(pt_ready, 1)

                def values(h):
                    pe.wait_ge(pt_moved, LEAD + b * H + (h + 1))
                    for k in range(KC):
                        last = mm(bank[4][0:L, h * DK:(h + 1) * DK], prob_t[0:KW, h % 2, k, :],
                                  v_t[0:KW, k, h * DK:(h + 1) * DK], start=(k == 0), stop=(k == KC - 1))
                    last.then_inc(pv_ready, 1)

                scores(0)
                for h in range(H):
                    if h + 1 < H:
                        scores(h + 1)
                    turn(h)
                    if h >= 1:
                        values(h - 1)
                values(H - 1)
                pe.wait_ge(att_ready, b + 1)
                for m in range(MC):
                    last = nc.tensor.transpose(misc[:, m * L:(m + 1) * L], att[0:L, m * P:(m + 1) * P], ident[0:L, 0:L])
                last.then_inc(att_t_ready, 1)
                pe.wait_ge(att_moved, b + 1)
                for m in range(MC):
                    last = mm(misc[0:L, 0:DM], at_t[:, m, :], wo[:, m, :], start=(m == 0), stop=(m == MC - 1))
                last.then_inc(wo_ready, 1)
                pe.wait_ge(x2_ready, b + 1)
                for m in range(MC):
                    last = nc.tensor.transpose(misc[:, m * L:(m + 1) * L], x1[0:L, m * P:(m + 1) * P], ident[0:L, 0:L])
                last.then_inc(x2t_ready, 1)
                pe.wait_ge(x2t_moved, b + 1)
                for m in range(MC):
                    last = mm(misc[0:L, 0:E], at_t[:, m, :], w_gate[:, m, :], start=(m == 0), stop=(m == MC - 1))
                last.then_inc(lg_ready, 1)
                pe.wait_ge(xs_ready, b + 1)
                for m in range(MC):
                    last = nc.tensor.transpose(misc[:, m * L:(m + 1) * L], xs[0:L, m * P:(m + 1) * P], ident[0:L, 0:L])
                last.then_inc(xst_ready, 1)

            def expert(n, s, src):
                for f in range(C):
                    for hf in range(2):
                        k = f * 2 + hf
                        if k < 2:
                            pe.wait_ge(hid_ready, LEAD + n * 8 + 0)
                        else:
                            pe.wait_ge(hid_ready, LEAD + n * 8 + (k - 1))
                        for m in range(MC):
                            last = mm(bank[k % 2][:, 0:HT], wg_s[s][:, m, f * P:(f + 1) * P],
                                      src[:, m, hf * HT:(hf + 1) * HT], start=(m == 0), stop=(m == MC - 1))
                        last.then_inc(gate_ready, 1)
                        for m in range(MC):
                            last = mm(bank[2 + k % 2][:, 0:HT], wu_s[s][:, m, f * P:(f + 1) * P],
                                      src[:, m, hf * HT:(hf + 1) * HT], start=(m == 0), stop=(m == MC - 1))
                        last.then_inc(up_ready, 1)
                pe.wait_ge(hid_ready, LEAD + n * 8 + 8)
                for b in range(B):
                    if b < 2:
                        pe.wait_ge(acc_ready, LEAD + n * 8 + 0)
                    else:
                        pe.wait_ge(acc_ready, LEAD + n * 8 + (b - 1))
                    for c in range(C):
                        last = mm(bank[4 + b % 2][0:L, 0:DM], hid[:, c, b * L:(b + 1) * L], wd[:, s, c, :],
                                  start=(c == 0), stop=(c == C - 1))
                    last.then_inc(down_ready, 1)

            pe.wait_ge(xst_moved, LEAD + B)
            pe.wait_ge(ffn_in[0], 48)
            expert(0, 0, x2t)
            with pe.Fori(0, E // 2) as i:
                pe.wait_ge(ffn_in[1], (i + 1) * 48)
                expert(i * 2 + 1, 1, xst)
                pe.wait_ge(ffn_in[0], (i + 2) * 48)
                expert(i * 2 + 2, 0, xst)

        @block.vector
        def _(dve):
            v = nc.vector
            dve.wait_ge(const_in, 16 * 16)
            v.memset(x_in[:, :, 0:W - 1, :], 0.0).then_inc(zeroed, 1)
            v.memset(x_a[:, L:LP], 0.0).then_inc(zeroed, 1)
            v.memset(kq[:, L:LP, 0:B], 0.0).then_inc(zeroed, 1)
            v.memset(kq[:, 0:2, B:2 * B], 0.0).then_inc(zeroed, 1)
            v.memset(rec[:, L - 1, F_NEXT], 0.0).then_inc(zeroed, 1)
            v.memset(m_a[:, :, :], 0.0).then_inc(zeroed, 1)
            v.memset(m_b[:, :, :], 0.0).then_inc(zeroed, 1)
            v.memset(s_b[:, :, :], 0.0).then_inc(zeroed, 1)
            v.memset(gram[:, :], 0.0).then_inc(zeroed, 1)
            v.memset(p_bd[:, :, :], 0.0).then_inc(zeroed, 1)
            v.memset(w_bd[:, :], 0.0).then_inc(zeroed, 1)
            v.memset(cols[:, :], 0.0).then_inc(zeroed, 1)
            dve.wait_ge(zeroed, 12)
            for c in range(C):
                for hf in range(2):
                    n = c * 2 + hf
                    dve.wait_ge(xz_ready, n + 1)
                    v.tensor_copy(x_in[:, c, W - 1 + hf * HL:W - 1 + (hf + 1) * HL, :].rearrange("p t b -> p (t b)"),
                                  bank[n % 4][:, 0:HT]).then_inc(x_moved, 1)
                dve.wait_ge(x_moved, 2 * c + 2)
                if c >= 2:
                    dve.wait_ge(x_ready, c - 1)
                acc_c = conv[:, c % 2, :]
                for w in range(W):
                    win = x_in[:, c, w:w + L, :].rearrange("p t b -> p (t b)")
                    if w == 0:
                        ins = v.tensor_scalar(acc_c, win, conv_w[:, c, 0:1], None, ALU.mult)
                    else:
                        dve.wait_ge(conv_step, c * W + w)
                        ins = v.scalar_tensor_tensor(acc_c, win, conv_w[:, c, w:w + 1], acc_c, ALU.mult, ALU.add)
                    ins.then_inc(conv_step, 1)
            for hf in range(2):
                dve.wait_ge(lo_ready, hf + 1)
                v.tensor_copy(dt_lo[:, hf * HT:(hf + 1) * HT], bank[4 + hf][0:R, 0:HT]).then_inc(lo_moved, 1)
            for j in range(2):
                for hf in range(2):
                    dve.wait_ge(kq_ready, j * 2 + hf + 1)
                    t0 = hf * HL + 2 * j
                    v.tensor_tensor(kq[:, t0:t0 + HL, j * B:(j + 1) * B],
                                    bank[6 + hf][:, 0:HT].rearrange("p (t b) -> p t b", b=B),
                                    spread(batch_mask, 1, HL), ALU.mult).then_inc(kq_moved, 1)
            dve.wait_ge(kq_moved, 4)
            v.tensor_reduce(k_col[:, :], kq[:, 0:L, 0:B], AX.X, ALU.add).then_inc(tab, 1)
            dve.wait_ge(tab, 1)
            v.tensor_tensor(ks_col[:, :], k_col[:, :], step_gain[:, :], ALU.mult).then_inc(tab, 1)
            dve.wait_ge(tab, 2)
            v.tensor_scalar(rec[:, :, 1 + 3 * N], ks_col[:, :], 2.0, None, ALU.mult).then_inc(tab, 1)
            v.tensor_copy(rec[:, :, 1 + 2 * N:1 + 3 * N], spread(col_mask, 1, L)).then_inc(tab, 1)
            v.tensor_tensor(k_sq, kq[:, 0:L, 0:B], kq[:, 0:L, 0:B], ALU.mult).then_inc(tab, 1)
            v.tensor_tensor(kd_row, spread(col_mask, 1, L), spread(k_col[:, :], 2, N), ALU.mult).then_inc(tab, 1)
            dve.wait_ge(kt_ready, 1)
            v.tensor_copy(ks_t, bank[4][0:L, 0:P]).then_inc(kt_moved, 1)
            for hf in range(2):
                dve.wait_ge(sq_ready, hf + 1)
                v.tensor_copy(k_sq[:, hf * HL:(hf + 1) * HL, :].rearrange("p t b -> p (t b)"),
                              bank[6 + hf][:, 0:HT]).then_inc(sq_moved, 1)
            for n in range(4):
                q = L // 4
                dve.wait_ge(row_done, n + 1)
                row = bank[4 + n % 2][:, 0:q * N].rearrange("p (t n) -> p t n", n=N)
                skip = 1 if n == 0 else 0
                v.tensor_copy(rec[:, n * q + skip - 1:(n + 1) * q - 1, F_NEXT], row[:, skip:, :])
                v.tensor_tensor(rec[:, n * q:(n + 1) * q, F_ROW], row,
                                spread(step_gain[:, n * q:(n + 1) * q], 2, N), ALU.mult).then_inc(row_moved, 1)
            v.tensor_copy(rec[:, :, 0], ks_col[:, :]).then_inc(tab, 1)
            v.tensor_scalar(rec[:, :, 2 + 3 * N], step_gain[:, :], TINY, None, ALU.mult).then_inc(tab, 1)
            for hf in range(2):
                k = 6 * hf
                dve.wait_ge(sp_act, 8 * 0 + 4 + 7 * hf + 2)
                v.tensor_scalar(sp_u, sp_e, 1.0, None, ALU.add).then_inc(sp_dve, 1)
                dve.wait_ge(sp_dve, k + 1)
                dve.wait_ge(sp_act, 7 * hf + 7)
                v.scalar_tensor_tensor(sp_e, sp_u, -1.0, sp_e, ALU.add, ALU.subtract).then_inc(sp_dve, 1)
                v.scalar_tensor_tensor(sp_a, sp_a, 0.0, sp_l, ALU.max, ALU.add).then_inc(sp_dve, 1)
                dve.wait_ge(sp_dve, k + 3)
                v.tensor_tensor(sp_a, sp_a, sp_e, ALU.subtract).then_inc(sp_dve, 1)
                dve.wait_ge(sp_dve, k + 4)
                dve.wait_ge(sq_moved, 2)
                dtv = sp_a.rearrange("p (t c b) -> p t c b", c=C, b=B)
                v.tensor_tensor(sp_u.rearrange("p (t c b) -> p t c b", c=C, b=B), dtv,
                                spread(k_sq[:, hf * HL:(hf + 1) * HL, :], 2, C), ALU.mult).then_inc(sp_dve, 1)
                dve.wait_ge(sp_dve, k + 5)
                v.tensor_scalar(sp_u, sp_u, 1.0, None, ALU.add).then_inc(tab, 1)
                dve.wait_ge(tab, 9 + 2 * hf)
                v.reciprocal(sp_u, sp_u).then_inc(tab, 1)
                dve.wait_ge(tab, 10 + 2 * hf)
                v.tensor_tensor(eps_a[:, hf * HL:(hf + 1) * HL].rearrange("p t c b -> p (t c b)"), sp_a, sp_u,
                                ALU.mult).then_inc(sp_dve, 1)
            dve.wait_ge(sp_dve, 12)
            dve.wait_ge(tab, 12)

            e_bank, mg_bank, gg_bank, sp_bank, g2_bank = bank[0:2], bank[2], bank[3], bank[4], bank[5]
            with dve.Fori(0, L // 2) as i:
                for par in range(2):
                    t = i * 2 + par
                    ev = e_bank[par][:, 0:64].rearrange("p (c w) -> p c w", c=C)
                    dve.wait_ge(err_ready, t + 1)
                    v.tensor_tensor(g_a[:, :, :], ev[:, :, 0:B],
                                    eps_a[:, bass.ds(t, 1)].rearrange("p o c b -> p (o c) b"), ALU.mult).then_inc(g_ready, 1)
                    dve.wait_ge(g_ready, t + 1)
                    v.tensor_tensor(g_sq[:, :, :], g_a[:, :, :], g_a[:, :, :], ALU.mult).then_inc(gsq_ready, 1)
                    v.tensor_copy(y_a[:, bass.ds(t, 1)].rearrange("p o c b -> p (o c) b"), ev[:, :, B:2 * B]).then_inc(y_saved, 1)
                    dve.wait_ge(mg_ready, t + 1)
                    v.tensor_tensor_reduce(junk[:, 0, 0:B], mg_bank[:, 0:B], batch_mask, 1.0, 0.0, ALU.mult,
                                           ALU.add, u_col).then_inc(u_ready, 1)
                    dve.wait_ge(gg_ready, t + 1)
                    dve.wait_ge(now_ready, t + 1)
                    dve.wait_ge(u_ready, t + 1)
                    v.tensor_tensor_reduce(junk2[:, :], gg_bank[:, 0:C * B], half_batch_mask,
                                           now[par][:, F_COL], u_col, ALU.mult, ALU.add, v_col).then_inc(v_ready, 1)
                    dve.wait_ge(v_ready, t + 1)
                    v.tensor_scalar(v_diag[:, :], now[par][:, F_SPREAD], v_col, None, ALU.mult).then_inc(vd_ready, 1)
                    v.scalar_tensor_tensor(gram1[:, :], now[par][:, F_ROW], v_col, gram[:, :], ALU.mult, ALU.add).then_inc(gram1_ready, 1)
                    dve.wait_ge(spread_ready, t + 1)
                    v.tensor_scalar(trace, sp_bank[:, N:N + 1], trace, 0.0, ALU.add, ALU.max).then_inc(trace_ready, 1)
                    dve.wait_ge(gram1_ready, t + 1)
                    v.scalar_tensor_tensor(gram[:, :], sp_bank[:, 0:N], now[par][:, F_COL], gram1[:, :],
                                           ALU.mult, ALU.add).then_inc(gram_ready, 1)
                    dve.wait_ge(gram_ready, t + 1)
                    v.tensor_tensor(gram_bd[:, :, :], spread(gram[:, :], 1, B), block_mask[:, :, :], ALU.mult).then_inc(bd_ready, 1)
                    dve.wait_ge(root_ready, t + 1)
                    v.tensor_scalar(norm, root, now[par][:, F_TINY], -1.0, ALU.add, ALU.mult).then_inc(scal, 1)
                    dve.wait_ge(scal, t * 4 + 1)
                    v.reciprocal(rneg, norm).then_inc(scal, 1)
                    dve.wait_ge(scal, t * 4 + 2)
                    v.tensor_scalar(r2b, rneg, rneg, NS_B, ALU.mult, ALU.mult).then_inc(scal, 1)
                    dve.wait_ge(scal, t * 4 + 3)
                    v.tensor_scalar(r4c, r2b, r2b, NS_C / NS_B ** 2, ALU.mult, ALU.mult).then_inc(scal, 1)
                    v.scalar_tensor_tensor(poly[:, :], gram[:, :], r2b, scaled_eye, ALU.mult, ALU.add).then_inc(poly_ready, 1)
                    dve.wait_ge(scal, t * 4 + 4)
                    dve.wait_ge(poly_ready, t + 1)
                    dve.wait_ge(gram2_ready, t + 1)
                    v.scalar_tensor_tensor(ns_p[:, :], g2_bank[:, 0:N], r4c, poly[:, :], ALU.mult, ALU.add).then_inc(p_ready, 1)
                    dve.wait_ge(p_ready, t + 1)
                    v.tensor_tensor_reduce(junk[:, 2, :], ns_p[:, :], now[par][:, F_NEXT], rneg, 0.0, ALU.mult, ALU.add, w_col).then_inc(w_ready, 1)
                    dve.wait_ge(w_ready, LEAD + t + 1)
                    v.tensor_scalar(w_bd[:, :], batch_mask, w_col, None, ALU.mult).then_inc(wbd_ready, 1)
                    dve.wait_ge(s_ready, t + 1)
                    v.scalar_tensor_tensor(p_bd[:, :, :], spread(ns_p[:, :], 1, B), rneg, block_mask[:, :, :],
                                           ALU.mult, ALU.mult).then_inc(pbd_ready, 1)
            for t in (L, L + 1):
                dve.wait_ge(base_ready, t + 1)
                ev = e_bank[t % 2][:, 0:64].rearrange("p (c w) -> p c w", c=C)
                v.tensor_copy(y_a[:, t], ev[:, :, B:2 * B]).then_inc(y_saved, 1)

            def layer_norm(src, dst, n, st, s_ln, s_std, done):
                v.bn_stats(st[0:L, 0:6], src).then_inc(s_ln, 1)
                dve.wait_ge(s_ln, n * 3 + 1)
                v.memset(st[0:L, 10:11], 0.0)
                v.bn_aggr(st[0:L, 6:8], st[0:L, 0:6]).then_inc(s_ln, 1)
                dve.wait_ge(s_std, n + 1)
                v.reciprocal(st[0:L, 9:10], st[0:L, 8:9]).then_inc(s_ln, 1)
                dve.wait_ge(s_ln, n * 3 + 3)
                v.tensor_scalar(dst, src, st[0:L, 6:7], st[0:L, 9:10], ALU.subtract, ALU.mult).then_inc(done, 1)

            dve.wait_ge(y_saved, LEAD + LP)
            dve.wait_ge(ma_ready, L)
            with dve.Fori(0, B) as b:
                for c in range(C):
                    v.scalar_tensor_tensor(y_tmp[:, c, :], x_a[:, 0:L, c, bass.ds(b, 1)].rearrange("p t o -> p (t o)"),
                                           vecs[:, 2, c:c + 1],
                                           y_a[:, 2:LP, c, bass.ds(b, 1)].rearrange("p t o -> p (t o)"),
                                           ALU.mult, ALU.add).then_inc(y_step, 1)
                dve.wait_ge(y_step, b * 4 + 4)
                for c in range(C):
                    ins = v.tensor_tensor(y_b[:, c, :], y_tmp[:, c, :], z_a[:, :, c, bass.ds(b, 1)].rearrange("p t o -> p (t o)"), ALU.mult)
                ins.then_inc(yb_ready, 1)
                dve.wait_ge(batch_in, (b + 1) * 48)
                v.tensor_copy(mask_f, mask_i[:, :]).then_inc(msk, 1)
                dve.wait_ge(msk, LEAD + b * 3 + 1)
                v.tensor_scalar(mask_f, mask_f, 0.0, None, ALU.not_equal).then_inc(msk, 1)
                dve.wait_ge(msk, LEAD + b * 3 + 2)
                v.tensor_scalar(mask_f, mask_f, mask_gain, mask_base, ALU.mult, ALU.add).then_inc(msk, 1)
                dve.wait_ge(msk, LEAD + b * 3 + 3)
                for g in range(4):
                    dve.wait_ge(kp_ready, LEAD + b * 4 + (g + 1))
                    v.scalar_tensor_tensor(k_t[:, g, :], bank[6 + g % 2][:, 0:S2], bias_qk[:, 1, g:g + 1], mask_f,
                                           ALU.add, ALU.mult).then_inc(kp_moved, 1)
                for k in range(KC):
                    dve.wait_ge(vp_ready, LEAD + b * KC + (k + 1))
                    v.tensor_tensor(v_t[0:KW, k, :], bank[6 + k % 2][0:KW, 0:DM], bias_rows[0:KW, 0, :], ALU.add).then_inc(vp_moved, 1)
                dve.wait_ge(proj_ready, b + 1)
                v.tensor_tensor(h1[0:L, :], bank[5][0:L, 0:DM], xb[0:L, :], ALU.add).then_inc(top, 1)
                dve.wait_ge(top, b * 8 + 1)
                layer_norm(h1[0:L, :], x1[0:L, :], b * 2, stat, ln, std_ready, x1_ready)
                dve.wait_ge(x1t_ready, b + 1)
                v.tensor_copy(x1t.rearrange("p m t -> p (m t)"), bank[5][:, 0:MC * L]).then_inc(x1t_moved, 1)
                dve.wait_ge(qp_ready, b + 1)
                for g in range(4):
                    ins = v.tensor_scalar(q_t[:, g, :], bank[5][:, g * L:(g + 1) * L], bias_qk[:, 0, g:g + 1],
                                          DK ** -0.5, ALU.add, ALU.mult)
                ins.then_inc(q_moved, 1)

                def head_max(h):
                    dve.wait_ge(sc_ready, b * H + (h + 1))
                    v.tensor_reduce(row_max[0:L, h:h + 1], bank[h % 2][0:L, 0:S2], AX.X, ALU.max, negate=True).then_inc(max_ready, 1)

                def head_turned(h):
                    dve.wait_ge(pt_ready, LEAD + b * H + (h + 1))
                    if h >= 2:
                        dve.wait_ge(pv_ready, b * H + (h - 1))
                    v.tensor_copy(prob_t[0:KW, h % 2].rearrange("p k s -> p (k s)"), bank[2 + h % 2][0:KW, 0:KC * L]).then_inc(pt_moved, 1)

                head_max(0)
                for h in range(H):
                    if h + 1 < H:
                        head_max(h + 1)
                    head_turned(h)
                v.reciprocal(row_inv[0:L, :], row_sum[0:L, :]).then_inc(inv_ready, 1)
                dve.wait_ge(inv_ready, b + 1)
                dve.wait_ge(pv_ready, b * H + H)
                v.tensor_tensor(att[0:L, :].rearrange("p (h d) -> p h d", h=H),
                                bank[4][0:L, 0:DM].rearrange("p (h d) -> p h d", h=H),
                                spread(row_inv[0:L, :], 2, DK), ALU.mult).then_inc(att_ready, 1)
                dve.wait_ge(att_t_ready, b + 1)
                v.tensor_copy(at_t.rearrange("p m t -> p (m t)"), bank[5][:, 0:MC * L]).then_inc(att_moved, 1)
                dve.wait_ge(wo_ready, b + 1)
                v.tensor_tensor(h1[0:L, :], bank[5][0:L, 0:DM], bias_rows[0:L, 1, :], ALU.add).then_inc(top, 1)
                dve.wait_ge(top, b * 8 + 2)
                v.tensor_tensor(h1[0:L, :], h1[0:L, :], x1[0:L, :], ALU.add).then_inc(top, 1)
                dve.wait_ge(top, b * 8 + 3)
                layer_norm(h1[0:L, :], x1[0:L, :], b * 2 + 1, stat, ln, std_ready, x2_ready)
                dve.wait_ge(x2_ready, b + 1)
                v.tensor_copy(x2[0:L, bass.ds(b, 1), :].rearrange("p o d -> p (o d)"), x1[0:L, :]).then_inc(top, 1)
                dve.wait_ge(x2t_ready, b + 1)
                v.tensor_copy(at_t.rearrange("p m t -> p (m t)"), bank[5][:, 0:MC * L])
                v.tensor_copy(x2t[:, :, bass.ds(b * L, L)], bank[5][:, 0:MC * L].rearrange("p (m t) -> p m t", m=MC)).then_inc(x2t_moved, 1)
                dve.wait_ge(lg_ready, b + 1)
                v.tensor_reduce(stat[0:L, 20:21], bank[5][0:L, 0:E], AX.X, ALU.max).then_inc(top, 1)
                dve.wait_ge(top, b * 8 + 5)
                v.scalar_tensor_tensor(lg[0:L, :], bank[5][0:L, 0:E], stat[0:L, 20:21], tie_rank[0:L, :], ALU.is_equal, ALU.mult).then_inc(top, 1)
                dve.wait_ge(top, b * 8 + 6)
                v.tensor_reduce(stat[0:L, 21:22], lg[0:L, :], AX.X, ALU.max).then_inc(top, 1)
                dve.wait_ge(top, b * 8 + 7)
                v.tensor_scalar(onehot[0:L, bass.ds(b, 1), :].rearrange("p o e -> p (o e)"), lg[0:L, :], stat[0:L, 21:22], None,
                                ALU.is_equal).then_inc(top, 1)
                dve.wait_ge(score_ready, b + 1)
                v.tensor_scalar(xs[0:L, :], x1[0:L, :], stat[0:L, 22:23], None, ALU.mult).then_inc(xs_ready, 1)
                dve.wait_ge(xst_ready, b + 1)
                v.tensor_copy(xst[:, :, bass.ds(b * L, L)], bank[5][:, 0:MC * L].rearrange("p (m t) -> p m t", m=MC)).then_inc(xst_moved, 1)

            def expert(n, shared):
                for k in range(8):
                    f, hf = k // 2, k % 2
                    dve.wait_ge(up_ready, n * 8 + (k + 1))
                    dve.wait_ge(silu_ready, n * 8 + (k + 1))
                    if k == 0:
                        dve.wait_ge(down_ready, LEAD + n * 8)
                    v.tensor_tensor(hid[:, f, hf * HT:(hf + 1) * HT], bank[2 + k % 2][:, 0:HT], gate[:, k % 2, :],
                                    ALU.mult).then_inc(hid_ready, 1)
                for b in range(B):
                    dve.wait_ge(down_ready, LEAD + n * 8 + (b + 1))
                    if shared:
                        ins = v.tensor_tensor(acc[0:L, b, :], bank[4 + b % 2][0:L, 0:DM], x2[0:L, b, :], ALU.add)
                    else:
                        dve.wait_ge(acc_ready, LEAD + n * 8 - (7 - b))
                        ins = v.scalar_tensor_tensor(acc[0:L, b, :], bank[4 + b % 2][0:L, 0:DM],
                                                     onehot[0:L, b, bass.ds(n - 1, 1)], acc[0:L, b, :], ALU.mult, ALU.add)
                    ins.then_inc(acc_ready, 1)

            dve.wait_ge(top, B * 8)
            dve.wait_ge(xst_moved, LEAD + B)
            expert(0, True)
            with dve.Fori(1, E + 1) as n:
                expert(n, False)
            with dve.Fori(0, B) as b:
                dve.wait_ge(acc_ready, LEAD + 9 * 8)
                dve.wait_ge(fin_free, LEAD + b)
                row = acc[0:L, bass.ds(b, 1), :].rearrange("p o d -> p (o d)")
                layer_norm(row, fin[0:L, :], b, stat3, ln3, std3_ready, y_ready)

        @block.scalar
        def _(act):
            a = nc.scalar.activation
            act.wait_ge(const_in, 16 * 16)
            for c in range(C):
                act.wait_ge(conv_step, (c + 1) * W)
                a(x_a[:, 0:L, c, :], conv[:, c % 2, :].rearrange("p (t b) -> p t b", b=B), ACT.Silu,
                  bias=vecs[:, 0, c:c + 1]).then_inc(x_ready, 1)
            for n in range(2 * C):
                c, hf = n // 2, n % 2
                act.wait_ge(xz_ready, 2 * C + n + 1)
                a(z_a[:, hf * HL:(hf + 1) * HL, c, :], bank[n % 4][:, 0:HT].rearrange("p (t b) -> p t b", b=B),
                  ACT.Silu).then_inc(z_done, 1)
            for hf in range(2):
                if hf == 1:
                    act.wait_ge(sp_dve, 6)
                for c in range(C):
                    act.wait_ge(dt_ready, hf * C + c + 1)
                    a(sp_a.rearrange("p (t c b) -> p t c b", c=C, b=B)[:, :, c, :],
                      bank[c][:, 0:HT].rearrange("p (t b) -> p t b", b=B), ACT.Identity,
                      bias=vecs[:, 1, c:c + 1]).then_inc(sp_act, 1)
                act.wait_ge(sp_act, 7 * hf + 4)
                a(sp_e, sp_a, ACT.Abs).then_inc(sp_act, 1)
                act.wait_ge(sp_act, 7 * hf + 5)
                a(sp_e, sp_e, ACT.Exp, scale=-1.0).then_inc(sp_act, 1)
                act.wait_ge(sp_dve, 6 * hf + 1)
                a(sp_l, sp_u, ACT.Ln).then_inc(sp_act, 1)

            act.wait_ge(zeroed, 12)
            act.wait_ge(base_ready, 1)
            with act.Fori(0, L) as t:
                act.wait_ge(s_ready, t + 1)
                act.wait_ge(base_ready, t + 1)
                nc.scalar.copy(s_b[:, :, :].rearrange("p c n -> p (c n)"), bank[6][:, :]).then_inc(sb_ready, 1)
                act.wait_ge(trace_ready, t + 1)
                a(root, trace, ACT.Sqrt).then_inc(root_ready, 1)
                act.wait_ge(mt_ready, t + 1)
                act.wait_ge(s_ready, t + 1)
                nc.scalar.copy(m_b[:, :, :].rearrange("p c n -> p (c n)"), bank[7][:, :]).then_inc(mb_ready, 1)
            act.wait_ge(s_ready, L + 1)
            act.wait_ge(base_ready, L + 1)
            nc.scalar.copy(s_b[:, :, :].rearrange("p c n -> p (c n)"), bank[6][:, :]).then_inc(sb_ready, 1)

            with act.Fori(0, B) as b:
                act.wait_ge(ln, b * 6 + 2)
                a(stat[0:L, 8:9], stat[0:L, 7:8], ACT.Sqrt, bias=eps_ln[0:L, :]).then_inc(std_ready, 1)
                for h in range(H):
                    act.wait_ge(max_ready, b * H + (h + 1))
                    if h >= 2:
                        act.wait_ge(pt_ready, LEAD + b * H + (h - 1))
                    else:
                        act.wait_ge(pt_ready, LEAD + b * H)
                    a(prob[0:L, h % 2, :], bank[h % 2][0:L, 0:S2], ACT.Exp, bias=row_max[0:L, h:h + 1],
                      accum_out=row_sum[0:L, h:h + 1]).then_inc(exp_ready, 1)
                act.wait_ge(ln, b * 6 + 5)
                a(stat[0:L, 8:9], stat[0:L, 7:8], ACT.Sqrt, bias=eps_ln[0:L, :]).then_inc(std_ready, 1)
                act.wait_ge(top, b * 8 + 5)
                a(stat[0:L, 22:23], stat[0:L, 20:21], ACT.Sigmoid).then_inc(score_ready, 1)

            with act.Fori(0, E + 1) as n:
                for k in range(8):
                    act.wait_ge(gate_ready, n * 8 + (k + 1))
                    if k >= 2:
                        act.wait_ge(hid_ready, LEAD + n * 8 + (k - 1))
                    else:
                        act.wait_ge(hid_ready, LEAD + n * 8)
                    a(gate[:, k % 2, :], bank[k % 2][:, 0:HT], ACT.Silu).then_inc(silu_ready, 1)
            with act.Fori(0, B) as b:
                act.wait_ge(ln3, b * 3 + 2)
                a(stat3[0:L, 8:9], stat3[0:L, 7:8], ACT.Sqrt, bias=eps_ln[0:L, :]).then_inc(std3_ready, 1)

        @block.gpsimd
        def _(pool):
            pool.wait_ge(zeroed, 12)
            pool.wait_ge(ks_in, 64)
            pool.wait_ge(row_moved, 4)
            pool.wait_ge(tab, 8)
            with pool.Fori(0, L // 2) as i:
                for par in range(2):
                    t = i * 2 + par
                    pool.wait_ge(w_ready, LEAD + i * 2)
                    nc.gpsimd.tensor_copy(now[par][:, :], rec[:, bass.ds(t, 1), :].rearrange("p o f -> p (o f)")).then_inc(now_ready, 1)
                    pool.wait_ge(g_ready, t + 1)
                    nc.gpsimd.tensor_tensor(outer[:, :, :].rearrange("p c (b n) -> p c b n", b=B),
                                            spread(g_a[:, :, :], 3, N),
                                            spread(ks_all[:, bass.ds(t, 1), :].rearrange("p o (b n) -> p (o b) n", b=B), 1, C),
                                            ALU.mult).then_inc(outer_ready, 1)
                    pool.wait_ge(outer_ready, t + 1)
                    pool.wait_ge(mg_ready, t + 1)
                    nc.gpsimd.tensor_tensor(m_a[:, :, :], m_a[:, :, :], outer[:, :, :], ALU.add).then_inc(ma_ready, 1)
            pool.wait_ge(ma_ready, L)
            with pool.Fori(0, B) as b:
                pool.wait_ge(vp_ready, LEAD + b * KC)
                pool.wait_ge(kp_ready, LEAD + b * 4)
                pool.wait_ge(msk, LEAD + b * 3)
                pool.wait_ge(x1_ready, LEAD + b)
                pool.dma_start(ctx_t, io["ctx_t"][bass.ds(b, 1)].rearrange("o p m s -> (o p) m s")).then_inc(batch_in, 16)
                pool.dma_start(mask_i[:, :], io["mask"][bass.ds(b, 1), :].partition_broadcast(P).rearrange("p o s -> p (o s)")).then_inc(batch_in, 16)
                pool.dma_start(xb[0:L, :], io["x"][bass.ds(b, 1)].rearrange("o t d -> (o t) d")).then_inc(batch_in, 16)
            pool.wait_ge(xst_moved, LEAD + B)
            pool.dma_start(wg_s[0], io["w_g"][0]).then_inc(ffn_in[0], 16)
            pool.dma_start(wu_s[0], io["w_u"][0]).then_inc(ffn_in[0], 16)
            pool.dma_start(wd[:, 0], io["w_d"][0]).then_inc(ffn_in[0], 16)
            with pool.Fori(0, E // 2) as i:
                for u in range(2):
                    s = (1 + u) % 2
                    if u == 0:
                        pool.wait_ge(down_ready, LEAD + i * 2 * B)
                    else:
                        pool.wait_ge(down_ready, LEAD + (i * 2 + 1) * B)
                    e = i * 2 + (1 + u)
                    pool.dma_start(wg_s[s], io["w_g"][bass.ds(e, 1)].rearrange("o p m f -> (o p) m f")).then_inc(ffn_in[s], 16)
                    pool.dma_start(wu_s[s], io["w_u"][bass.ds(e, 1)].rearrange("o p m f -> (o p) m f")).then_inc(ffn_in[s], 16)
                    pool.dma_start(wd[:, s], io["w_d"][bass.ds(e, 1)].rearrange("o p c d -> (o p) c d")).then_inc(ffn_in[s], 16)
            with pool.Fori(0, B) as b:
                pool.wait_ge(y_ready, b + 1)
                pool.dma_start(out[bass.ds(b, 1)].rearrange("o t d -> (o t) d"), fin[0:L, :]).then_inc(y_out, 16)
                pool.wait_ge(y_out, (b + 1) * 16)
                pool.sem_inc(fin_free, 1)


def _constants():
    f = np.float32
    p = np.arange(P)
    small = np.zeros((P, 96), f)
    small[:, 0:8] = (p[:, None] // N == np.arange(B))
    small[:, 64:96] = 0.5 * np.tile(small[:, 0:8], (1, C))
    small[:, 16:32] = (p[:, None] % N == np.arange(N))
    small[:, 32:48] = NS_A * small[:, 16:32]
    bias_row = p % 32 == DK
    small[:, 48] = np.where(bias_row, NEG, 1.0)
    small[:, 49] = np.where(bias_row, -NEG, 0.0)
    small[:, 50] = EPS
    small[:, 52:60] = E - np.arange(E)
    gain = np.float64(BETA) ** -np.arange(L)
    block = (p[:, None] // N == p[None, :] // N).astype(f)
    return {
        "c_ident": np.eye(P, dtype=f), "c_neg": -np.eye(P, dtype=f), "c_ones": np.ones((P, P), f),
        "c_block": block, "c_small": small, "c_bmask": block.reshape(P, B, N),
        "c_gain": np.broadcast_to(gain, (P, L)).astype(f),
    }


def _chunks(w, n=P):
    return w.reshape(-1, n, w.shape[-1]).transpose(1, 0, 2)


def _pad_heads(w):
    out = np.zeros((H, 32) + w.shape[1:], w.dtype)
    out[:, :DK] = w.reshape((H, DK) + w.shape[1:])
    return out.reshape((H * 32,) + w.shape[1:])


def kernel(**inputs):
    import concourse.bacc as bacc
    from concourse.bass_utils import run_bass_kernel_spmd as run

    i = {k.replace("L0_", ""): np.asarray(a) for k, a in inputs.items()}
    x = i["x"]
    xp = i["attn_x_proj_w"]
    bq, bk = _pad_heads(i["xattn_bq"]), _pad_heads(i["xattn_bk"])
    bq.reshape(H, 32)[:, DK] = DK ** 0.5
    bk.reshape(H, 32)[:, DK] = 1.0
    arrays = {
        "x": x,
        "xt": _chunks(x.transpose(2, 1, 0).reshape(DM, T)),
        "w_in": _chunks(i["attn_in_proj_w"].T),
        "conv_w": _chunks(i["attn_conv_w"].reshape(DI, W)),
        "vecs": np.stack([i[k].reshape(C, P).T for k in ("attn_conv_b", "attn_dt_head_b", "attn_D")], 1),
        "w_lo": _chunks(xp[0:R].T),
        "w_k": _chunks(np.tile(xp[R:R + N].T, (1, B))),
        "w_q": _chunks(np.tile(xp[R + N:].T, (1, B))),
        "w_dt": i["attn_dt_head_w"].T,
        "w_out": _chunks(i["attn_out_proj_w"].T),
        "bias_qk": np.stack([bq.reshape(4, P).T, bk.reshape(4, P).T], 1),
        "bias_rows": np.broadcast_to(np.stack([i["xattn_bv"], i["xattn_bo"]]), (P, 2, DM)),
        "wq": _chunks(_pad_heads(i["xattn_Wq"]).T),
        "wk": _chunks(_pad_heads(i["xattn_Wk"]).T),
        "wv": _chunks(i["xattn_Wv"].T),
        "wo": _chunks(i["xattn_Wo"].T),
        "w_gate": _chunks(i["ffn_gate_w"].T),
        "ctx_t": i["ctx_1024"].transpose(0, 2, 1).reshape(B, MC, P, S2).transpose(0, 2, 1, 3),
        "mask": i["mask_Bx1xS2_ik0"].reshape(B, S2),
        "w_g": np.stack([_chunks(w.T) for w in [i["ffn_shared_gate"], *i["ffn_r_gate"]]]),
        "w_u": np.stack([_chunks(w.T) for w in [i["ffn_shared_up"], *i["ffn_r_up"]]]),
        "w_d": np.stack([_chunks(w.T) for w in [i["ffn_shared_down"], *i["ffn_r_down"]]]),
        **_constants(),
    }
    nc = bacc.Bacc("TRN2", target_bir_lowering=False, num_devices=1)
    sent, io = {}, {}
    for name, a in arrays.items():
        a = np.ascontiguousarray(a)
        sent[f"in_{name}"] = a
        io[name] = nc.dram_tensor(f"in_{name}", a.shape, mybir.dt.from_np(a.dtype), kind="ExternalInput").ap()
    out = nc.dram_tensor("out_0", (B, L, DM), F32, kind="ExternalOutput").ap()
    decoder_kernel(nc, io, out)
    r = run(nc, [sent], core_ids=[0])
    return r.results[0]["out_0"]
```

```python
import numpy as np

import concourse.bass as bass
from concourse import mybir
from contextlib import ExitStack

B, L, DM = 8, 112, 256
DI, N, R, W = 512, 16, 64, 4
S2 = 375
H, DK = 16, 16
F, E = 512, 8
P = 128
C = DI // P
MC = DM // P
T = B * L
HT = T // 2
HL = L // 2
BN = B * N
KC = 3
KW = S2 // KC
NT = (T + E * (P - 1)) // P
EW = MC * 2 * F + C * DM
LP = L + 2
BETA = 0.9
NS_A, NS_B, NS_C = 3.4445, -4.775, 2.0315
ARENA = 21504
TURN = 8
LEAD = 2
NEG = 1e9
TINY = 1e-7
EPS = 1e-5

F32 = mybir.dt.float32
I32 = mybir.dt.int32
ALU = mybir.AluOpType
ACT = mybir.ActivationFunctionType
AX = mybir.AxisListType


def spread(ap, axis, n):
    a = ap.unsqueeze(axis)
    shape = list(a.shape)
    shape[axis] = n
    return a.broadcast_to(shape)


def decoder_kernel(nc, io, out):
    with ExitStack() as ctx:
        def sb(name, shape, dt=F32):
            return ctx.enter_context(nc.sbuf_tensor(name, shape, dt))

        def sem(name):
            return ctx.enter_context(nc.semaphore(name))

        bank = [ctx.enter_context(nc.psum_tensor(f"bank{i}", [P, 512], F32)) for i in range(8)]

        ident = sb("ident", [P, P])
        neg_ident = sb("neg_ident", [P, P])
        ones = sb("ones", [P, P])
        block_ones = sb("block_ones", [P, P])
        block_mask = sb("block_mask", [P, N, B])
        pick = sb("pick", [P, 2 * C * B])
        spread_u = sb("spread_u", [P, P])
        tile_mask = sb("tile_mask", [P, B])
        small = sb("small", [P, 64])
        batch_mask = small[:, 0:8]
        col_mask, scaled_eye = small[:, 16:32], small[:, 32:48]
        mask_gain, mask_base, eps_ln = small[:, 48:49], small[:, 49:50], small[:, 50:51]
        tie_rank = small[:, 52:60]
        head_rows = small[:, 8:12]
        step_gain = sb("step_gain", [P, L])

        conv_w = sb("conv_w", [P, C, W])
        vecs = sb("vecs", [P, 3, C])
        bias_qk = sb("bias_qk", [P, 2, 4])
        bias_rows = sb("bias_rows", [P, 2, DM])
        w_out = sb("w_out", [P, C, DM])

        tables = sb("tables", [P, E * EW])
        t_at = [0]

        def table(t, *dims):
            n = int(np.prod(dims))
            t_at[0] += t * n
            flat = tables[:, t_at[0] - t * n:t_at[0]]
            if len(dims) == 2:
                return flat.rearrange("p (t c b) -> p t c b", t=t, c=dims[0])
            return flat.rearrange("p (t n) -> p t n", t=t)

        y_a = table(LP, C, B)
        x_a = table(LP, C, B)
        z_a = table(L, C, B)
        kq = table(LP, 2 * B)
        assert t_at[0] >= E // 2 * EW
        eps_a = table(L, C, B)
        k_col = sb("k_col", [P, L])
        ks_col = sb("ks_col", [P, L])
        at_rec = [0]

        def field(n):
            at_rec[0] += n
            return slice(at_rec[0] - n, at_rec[0])

        MASKS = N
        F_COL, F_TRACE, F_ROW, F_NEXT = field(1), field(N + 1), field(N), field(N)
        F_AK, F_TINY, F_KQ = field(1), field(1), field(2 * B)
        REC = at_rec[0]
        rec = table(L, REC)
        assert t_at[0] <= E * EW
        now_all = [sb(f"now{i}", [P, MASKS + REC + 2 * B]) for i in range(2)]
        now = [x[:, MASKS:] for x in now_all]
        arena = sb("arena", [P, ARENA])
        ks_all = arena[:, 0:L * BN].rearrange("p (t n) -> p t n", t=L)

        m_g = sb("m_g", [P, C, N + 1, B])
        m_b = sb("m_b", [P, C, P])
        s_b = sb("s_b", [P, C, P])
        outer = sb("outer", [P, C, BN])
        g_a = m_g[:, :, N, :]
        m_a = [m_g[:, c, 0:N, :].rearrange("p n b -> p (n b)") for c in range(C)]
        eps = sb("eps", [P, C * B])
        e_c = sb("e_c", [P, P])
        mg_m = sb("mg_m", [P, N + 1, B])
        u_row = sb("u_row", [P, N + 1])
        gram = sb("gram", [P, N])
        gram1 = sb("gram1", [P, N])
        gram_bd = sb("gram_bd", [P, N, B])
        poly = sb("poly", [P, N])
        ns_p = sb("ns_p", [P, N])
        p_bd = sb("p_bd", [P, N, B])
        w_bd = sb("w_bd", [P, B])
        junk = sb("junk", [P, N + 1])
        junk2 = sb("junk2", [P, N + 1])
        junk3 = sb("junk3", [P, N])
        junk4 = sb("junk4", [P, N])
        cols = sb("cols", [P, 16])
        u_col, v_col, w_col, trace = cols[:, 0:1], cols[:, 1:2], cols[:, 2:3], cols[:, 3:4]
        dummy, gk_col, ak_col, r4 = (cols[:, i:i + 1] for i in (11, 10, 13, 14))
        root, norm, rneg, r2b, r2c, trace1 = (cols[:, i:i + 1] for i in range(4, 10))

        ks_dram = nc.dram_tensor("ks_dram", [L, BN], F32, kind="Internal").ap()

        at = [0]

        def take(n):
            at[0] += n
            assert at[0] <= ARENA, at[0]
            return arena[:, at[0] - n:at[0]]

        xt = take(MC * T).rearrange("p (m t) -> p m t", m=MC)
        w_in = take(MC * 2 * DI).rearrange("p (m e) -> p m e", m=MC)
        x_in = take(C * (L + W - 1) * B).rearrange("p (c t b) -> p c t b", c=C, b=B)
        conv = take(2 * T).rearrange("p (u t) -> p u t", u=2)
        w_dt_lo = take(C * R).rearrange("p (c r) -> p c r", c=C)
        w_k = take(C * BN).rearrange("p (c n) -> p c n", c=C)
        w_q = take(C * BN).rearrange("p (c n) -> p c n", c=C)
        at[0] = L * BN
        dt_lo = take(T)[0:R, :]
        k_sq = take(L * B).rearrange("p (t b) -> p t b", b=B)
        kd_row = take(L * N).rearrange("p (t n) -> p t n", n=N)
        sp_e, sp_l = take(HL * C * B), take(HL * C * B)
        w_dt = outer[0:R, :, :].rearrange("p c n -> p (c n)")
        ks_t = e_c[0:L, :]
        y_flat = y_a.rearrange("p t c b -> p (t c b)")
        den_flat = eps_a.rearrange("p t c b -> p (t c b)")
        half = HL * C * B
        sp_a_of = [y_flat[:, i * half:(i + 1) * half] for i in range(2)]
        sp_u_of = [den_flat[:, i * half:(i + 1) * half] for i in range(2)]

        at[0] = L * BN
        wo = take(MC * DM).rearrange("p (m e) -> p m e", m=MC)
        w_gate = take(MC * E).rearrange("p (m e) -> p m e", m=MC)
        xb = take(B * DM).rearrange("p (b d) -> p b d", b=B)
        shared_at = at[0]
        wq = take(MC * 512).rearrange("p (m e) -> p m e", m=MC)
        wk = take(MC * 512).rearrange("p (m e) -> p m e", m=MC)
        wv = take(MC * DM).rearrange("p (m e) -> p m e", m=MC)
        ctx_t = [take(MC * S2).rearrange("p (m s) -> p m s", m=MC) for _ in range(2)]
        stat = take(168)
        row_inv = take(H)
        at[0] = 0
        y_g = take(C * T).rearrange("p (c b t) -> p c b t", c=C, b=B)
        prob_t = [y_g.rearrange("p c b t -> p (c b t)")[:, i * KC * 4 * L:(i + 1) * KC * 4 * L]
                  .rearrange("p (k q) -> p k q", k=KC) for i in range(2)]
        x1t = take(MC * T).rearrange("p (m t) -> p m t", m=MC)
        x1 = take(B * DM).rearrange("p (b d) -> p b d", b=B)
        att = take(B * DM).rearrange("p (b d) -> p b d", b=B)
        h1 = take(B * DM).rearrange("p (b d) -> p b d", b=B)
        hid_at = at[0] - B * DM
        q_bd = [take(4 * L).rearrange("p (h q) -> p h q", h=4) for _ in range(2)]
        q_mx = [take(4 * L).rearrange("p (h q) -> p h q", h=4) for _ in range(2)]
        q_aug = [take(L) for _ in range(2)]
        row_max = [take(P) for _ in range(2)]
        o_raw = take(4 * L).rearrange("p (g q) -> p g q", g=4)
        assert at[0] <= L * BN
        rec_flat = rec[:, :, :].rearrange("p t f -> p (t f)")
        k_t = [rec_flat[:, i * 4 * S2:(i + 1) * 4 * S2].rearrange("p (g s) -> p g s", g=4) for i in range(2)]
        v_at, v_n = 2 * 4 * S2, KC * H * 32
        v_t = [rec_flat[:, v_at + i * v_n:v_at + (i + 1) * v_n].rearrange("p (k h e) -> p k h e", k=KC, h=H) for i in range(2)]
        mask_f = rec_flat[:, v_at + 2 * v_n:v_at + 2 * v_n + S2]
        q_s = eps_a[:, :, :, :].rearrange("p t c b -> p (t c b)").rearrange("p (g t) -> p g t", g=4)
        mask_i = [sb(f"mask_i{i}", [P, S2], I32) for i in range(2)]
        q_bias = small[:, 60:64]
        x2 = xb
        at_t = x1t
        x2t = arena[:, 0:MC * T].rearrange("p (m t) -> p m t", m=MC)
        xs = att
        acc = x1
        lg, top_logit, top_rank = stat[:, 96:160].rearrange("p (b e) -> p b e", b=B), stat[:, 80:88], stat[:, 88:96]
        score = stat[:, 72:80]
        onehot = sb("onehot", [P, B, E])
        shared = arena[:, shared_at:shared_at + EW]
        wg = shared[:, 0:MC * F].rearrange("p (m f) -> p m f", m=MC)
        wu = shared[:, MC * F:2 * MC * F].rearrange("p (m f) -> p m f", m=MC)
        wd = shared[:, 2 * MC * F:EW].rearrange("p (c d) -> p c d", c=C)
        hid = arena[:, hid_at:hid_at + C * T].rearrange("p (c t) -> p c t", c=C)
        gate = arena[:, MC * T:MC * T + 2 * HT].rearrange("p (u t) -> p u t", u=2)
        w_r = tables[:, :].rearrange("p (e w f) -> p e w f", e=E, f=F)
        rows_in = [arena[:, MC * T + 2 * HT + i * DM:MC * T + 2 * HT + (i + 1) * DM] for i in range(2)]
        x1t_flat = x1t.rearrange("p m t -> p (m t)")
        rows_t = [x1t_flat[:, i * DM:(i + 1) * DM] for i in range(2)]
        hid_t = [x1t_flat[:, 2 * DM + i * F:2 * DM + (i + 1) * F] for i in range(2)]
        silu_r = [m_b[:, :, :].rearrange("p c n -> p (c n)"), s_b[:, :, :].rearrange("p c n -> p (c n)")]
        hid_r = [outer[:, :, :].rearrange("p c n -> p (c n)"), w_out[:, 0:2, :].rearrange("p c n -> p (c n)")]
        y_r = [w_out[:, 2, :], w_out[:, 3, :]]
        route_c = sb("route_c", [P, 112])
        before_e, tile_start, tile_no, digit = (route_c[:, 0:64], route_c[:, 64:72], route_c[:, 72:72 + NT],
                                                route_c[:, 96:96 + NT])
        earlier = sb("earlier", [P, L])
        route = arena[:, hid_at + C * T:hid_at + C * T + 512]
        r_tot, r_pre, r_pos = route[:, 0:64], route[:, 64:128], route[:, 128:192]
        r_cmp, r_tri = route[:, 192:256], route[:, 256:320]
        r_end_cmp = route[:, 320:320 + NT * E]
        r_cnt, r_tiles, r_base, r_end, r_slot = (route[:, 432 + 8 * i:440 + 8 * i] for i in range(5))
        r_tile = route[:, 472:472 + NT]
        slot_i = sb("slot_i", [P, B], I32)
        expert_i = sb("expert_i", [P, 2], I32)
        rows_dram = nc.dram_tensor("rows_dram", [NT * P, DM], F32, kind="Internal").ap()
        out_dram = nc.dram_tensor("out_dram", [NT * P, DM], F32, kind="Internal").ap()

        const_in, pre_in, k_out, ks_in = sem("const_in"), sem("pre_in"), sem("k_out"), sem("ks_in")
        zeroed = sem("zeroed")
        xz_ready, x_moved, z_done = sem("xz_ready"), sem("x_moved"), sem("z_done")
        conv_ready, conv_step, x_ready = sem("conv_ready"), sem("conv_step"), sem("x_ready")
        lo_ready, lo_moved = sem("lo_ready"), sem("lo_moved")
        kq_ready, kq_moved = sem("kq_ready"), sem("kq_moved")
        dt_ready, sp_act, sp_dve = sem("dt_ready"), sem("sp_act"), sem("sp_dve")
        tab, row_done, row_moved = sem("tab"), sem("row_done"), sem("row_moved")
        kt_ready, kt_moved, sq_ready, sq_moved = sem("kt_ready"), sem("kt_moved"), sem("sq_ready"), sem("sq_moved")
        base_ready, err_ready, g_ready, y_saved = sem("base_ready"), sem("err_ready"), sem("g_ready"), sem("y_saved")
        e_copied, a_ready, mgm_ready = sem("e_copied"), sem("a_ready"), sem("mgm_ready")
        mg_ready, ur_ready, v_ready = sem("mg_ready"), sem("ur_ready"), sem("v_ready")
        trace1_ready, gram1_ready, spread_ready = sem("trace1_ready"), sem("gram1_ready"), sem("spread_ready")
        trace_ready, gram_ready, bd_ready = sem("trace_ready"), sem("gram_ready"), sem("bd_ready")
        root_ready, gram2_ready, norm_ready = sem("root_ready"), sem("gram2_ready"), sem("norm_ready")
        rneg_ready, gk_ready, r2b_ready, r2c_ready = sem("rneg_ready"), sem("gk_ready"), sem("r2b_ready"), sem("r2c_ready")
        ak_ready, r4_ready = sem("ak_ready"), sem("r4_ready")
        poly_ready, p_ready, w_ready, wbd_ready = sem("poly_ready"), sem("p_ready"), sem("w_ready"), sem("wbd_ready")
        pbd_ready, outer_ready, ma_ready = sem("pbd_ready"), sem("outer_ready"), sem("ma_ready")
        mt_ready, mb_ready, s_ready, sb_ready = sem("mt_ready"), sem("mb_ready"), sem("s_ready"), sem("sb_ready")
        now_ready, ma0_ready = sem("now_ready"), sem("ma0_ready")
        recip_ready, eps_ready = sem("recip_ready"), sem("eps_ready")
        att_in, ctx_in = sem("att_in"), [sem("ctx_in0"), sem("ctx_in1")]
        y_step, yb_half, yb_ready, proj_ready, qb_ready = sem("y_step"), sem("yb_half"), sem("yb_ready"), sem("proj_ready"), sem("qb_ready")
        h1_ready, h2_ready, ln, std_ready, x1_ready = sem("h1_ready"), sem("h2_ready"), sem("ln"), sem("std_ready"), sem("x1_ready")
        x1b_ready, x1t_ready, x1t_moved, x1t_copied = sem("x1b_ready"), sem("x1t_ready"), sem("x1t_moved"), sem("x1t_copied")
        kp_ready, kp_moved, vp_ready, vp_moved = sem("kp_ready"), sem("kp_moved"), sem("vp_ready"), sem("vp_moved")
        qp_ready, q_moved, q_copied, msk = sem("qp_ready"), sem("q_moved"), sem("q_copied"), sem("msk")
        qbd_ready, sc_ready, max_ready, mxt_ready = sem("qbd_ready"), sem("sc_ready"), sem("max_ready"), sem("mxt_ready")
        qa_ready, qmx_ready, st_ready, exp_ready = sem("qa_ready"), sem("qmx_ready"), sem("st_ready"), sem("exp_ready")
        pv_ready, o_copied, ot_ready, inv_ready, att_ready = sem("pv_ready"), sem("o_copied"), sem("ot_ready"), sem("inv_ready"), sem("att_ready")
        cleared = sem("cleared")
        att_t_ready, att_moved, att_copied = sem("att_t_ready"), sem("att_moved"), sem("att_copied")
        wo_ready, x2_ready, x2t_ready, x2t_moved, x2t_copied = sem("wo_ready"), sem("x2_ready"), sem("x2t_ready"), sem("x2t_moved"), sem("x2t_copied")
        lg_ready, top, score_ready, xs_ready = sem("lg_ready"), sem("top"), sem("score_ready"), sem("xs_ready")
        shared_in, routed_in, rows_zero, rows_out = sem("shared_in"), sem("routed_in"), sem("rows_zero"), sem("rows_out")
        count_ready, route_step, route_ready = sem("count_ready"), sem("route_step"), sem("route_ready")
        gate_ready, up_ready, silu_ready, hid_ready = sem("gate_ready"), sem("up_ready"), sem("silu_ready"), sem("hid_ready")
        down_ready, acc_ready = sem("down_ready"), sem("acc_ready")
        rows_in_ready = [sem("rows_in0"), sem("rows_in1")]
        turned, turned_moved, rg_ready, ru_ready = sem("turned"), sem("turned_moved"), sem("rg_ready"), sem("ru_ready")
        rsilu_ready, rhid_ready, rht_ready, rht_moved = sem("rsilu_ready"), sem("rhid_ready"), sem("rht_ready"), sem("rht_moved")
        ry_ready, ry_moved, tile_out, back_in = sem("ry_ready"), sem("ry_moved"), [sem("tile_out0"), sem("tile_out1")], [sem(f"back_in{b}") for b in range(B)]
        sum_ready, y_ready, y_out = sem("sum_ready"), sem("y_ready"), sem("y_out")

        block = ctx.enter_context(nc.Block())

        @block.sync
        def _(sp):
            for s in (mb_ready, wbd_ready, pbd_ready, sb_ready, y_saved, w_ready, ma0_ready,
                      kp_ready, kp_moved, vp_ready, vp_moved, msk, qbd_ready, sc_ready, max_ready, mxt_ready,
                      qa_ready, qmx_ready, st_ready, exp_ready, pv_ready, o_copied, ot_ready, inv_ready, att_ready,
                      turned, turned_moved, rsilu_ready, rhid_ready, rht_ready, rht_moved, ry_ready, ry_moved,
                      rg_ready, ru_ready):
                sp.sem_inc(s, LEAD)
            for dst, name in ((xt, "xt"), (w_in, "w_in"), (conv_w[:, :, :], "conv_w"), (vecs[:, :, :], "vecs")):
                sp.dma_start(dst, io[name]).then_inc(pre_in, 16)
            for dst, name in ((w_dt_lo, "w_lo"), (w_k, "w_k"), (w_q, "w_q"), (w_dt, "w_dt"), (small[:, :], "c_small"),
                              (ident[:, :], "c_ident"), (step_gain[:, :], "c_gain"), (ones[:, :], "c_ones"),
                              (block_ones[:, :], "c_block"), (neg_ident[:, :], "c_neg"),
                              (block_mask[:, :, :], "c_bmask"), (pick[:, :], "c_pick"), (spread_u[:, :], "c_spread"),
                              (tile_mask[:, :], "c_tile"), (w_out[:, :, :], "w_out"), (bias_qk[:, :, :], "bias_qk"),
                              (bias_rows[:, :, :], "bias_rows")):
                sp.dma_start(dst, io[name]).then_inc(const_in, 16)
            sp.wait_ge(kt_moved, 1)
            sp.dma_start(ks_dram, ks_t).then_inc(k_out, 16)
            sp.wait_ge(k_out, 16)
            sp.wait_ge(xz_ready, 4 * C)
            sp.wait_ge(conv_step, C * W)
            sp.wait_ge(x_ready, C)
            sp.wait_ge(kq_ready, 4)
            for q in range(4):
                n = L // 4
                sp.dma_start(ks_all[:, q * n:(q + 1) * n, :],
                             ks_dram[q * n:(q + 1) * n, :].partition_broadcast(P)).then_inc(ks_in, 16)
            sp.wait_ge(sp_dve, 2 * 5)
            sp.wait_ge(row_moved, 4)
            sp.wait_ge(sq_moved, 2)
            sp.wait_ge(tab, 8)
            sp.wait_ge(dt_ready, 2 * C)
            sp.dma_start(route_c[:, :], io["c_route"]).then_inc(att_in, 16)
            sp.dma_start(earlier[:, :], io["c_earlier"]).then_inc(att_in, 16)
            sp.dma_start(rows_dram, io["c_zero"]).then_inc(rows_zero, 16)
            for dst, name in ((wq, "wq"), (wk, "wk"), (wv, "wv"), (wo, "wo"), (w_gate, "w_gate")):
                sp.dma_start(dst, io[name]).then_inc(att_in, 16)
            sp.dma_start(xb[0:L], io["x"].rearrange("b t d -> t b d")).then_inc(att_in, 16)
            for b in range(2):
                sp.dma_start(ctx_t[b], io["ctx_t"][b]).then_inc(ctx_in[b], 16)
                sp.dma_start(mask_i[b][:, :], io["mask"][b].partition_broadcast(P)).then_inc(ctx_in[b], 16)
            sp.wait_ge(yb_half, 2)
            sp.wait_ge(yb_ready, 1)
            for e in range(E // 2):
                sp.dma_start(tables[:, e * EW:(e + 1) * EW], io["w_r"][e]).then_inc(routed_in, 16)
            for b in range(2, B):
                sp.wait_ge(kp_ready, LEAD + (b - 1) * 4)
                sp.wait_ge(vp_ready, LEAD + (b - 1) * KC)
                sp.wait_ge(msk, LEAD + (b - 1) * 3)
                sp.dma_start(ctx_t[b % 2], io["ctx_t"][b]).then_inc(ctx_in[b % 2], 16)
                sp.dma_start(mask_i[b % 2][:, :], io["mask"][b].partition_broadcast(P)).then_inc(ctx_in[b % 2], 16)
            sp.wait_ge(kp_ready, LEAD + B * 4)
            sp.wait_ge(vp_ready, LEAD + B * KC)
            sp.dma_start(shared, io["w_shared"]).then_inc(shared_in, 16)
            sp.wait_ge(pv_ready, LEAD + B * 4)
            sp.wait_ge(qa_ready, LEAD + B * 4)
            sp.wait_ge(qbd_ready, LEAD + B * 4)
            for e in range(E // 2, E):
                sp.dma_start(tables[:, e * EW:(e + 1) * EW], io["w_r"][e]).then_inc(routed_in, 16)
            for b in range(B):
                sp.wait_ge(y_ready, b + 1)
                sp.dma_start(out[b], h1[0:L, b, :]).then_inc(y_out, 16)
            sp.wait_ge(y_out, 16 * B)

        @block.tensor
        def _(pe):
            mm = nc.tensor.matmul

            def project(ec, hf):
                for m in range(MC):
                    last = mm(bank[(2 * ec + hf) % 4][:, 0:HT], w_in[:, m, ec * P:(ec + 1) * P],
                              xt[:, m, hf * HT:(hf + 1) * HT], start=(m == 0), stop=(m == MC - 1))
                last.then_inc(xz_ready, 1)

            pe.wait_ge(pre_in, 64)
            for ec in range(C):
                for hf in range(2):
                    if ec >= 2:
                        pe.wait_ge(x_moved, 2 * ec + hf - 3)
                    project(ec, hf)
            pe.wait_ge(const_in, 16 * 17)
            pe.wait_ge(x_ready, C)
            for hf in range(2):
                xs_h = x_a[:, hf * HL:(hf + 1) * HL]
                for c in range(C):
                    last = mm(bank[4 + hf][0:R, 0:HT], w_dt_lo[:, c, :], xs_h[:, :, c, :],
                              start=(c == 0), stop=(c == C - 1))
                last.then_inc(lo_ready, 1)
            for j, wt in enumerate((w_k, w_q)):
                for hf in range(2):
                    xs_h = x_a[:, hf * HL:(hf + 1) * HL]
                    if j == 1:
                        pe.wait_ge(kq_moved, hf + 1)
                    for c in range(C):
                        last = mm(bank[6 + hf][:, 0:HT], wt[:, c, :], xs_h[:, :, c, :],
                                  start=(c == 0), stop=(c == C - 1))
                    last.then_inc(kq_ready, 1)
            pe.wait_ge(lo_moved, 2)
            pe.wait_ge(x_moved, 2 * C)
            for hf in range(2):
                for c in range(C):
                    n = hf * C + c
                    if n >= 4:
                        pe.wait_ge(sp_act, n - 3)
                    mm(bank[c][:, 0:HT], w_dt[:, c * P:(c + 1) * P], dt_lo[:, hf * HT:(hf + 1) * HT],
                       start=True, stop=True).then_inc(dt_ready, 1)
            for ec in range(C, 2 * C):
                for hf in range(2):
                    n = 2 * (ec - C) + hf
                    if n < 4:
                        pe.wait_ge(sp_act, C + 1 + n)
                    else:
                        pe.wait_ge(z_done, n - 3)
                    project(ec, hf)
            pe.wait_ge(tab, 3)
            nc.tensor.transpose(bank[4][0:L, 0:P], ks_col[:, :], ident[:, :]).then_inc(kt_ready, 1)
            pe.wait_ge(tab, 5)
            pe.wait_ge(kq_moved, 4)
            for hf in range(2):
                mm(bank[6 + hf][:, 0:HT], ones[:, :], k_sq[:, hf * HL:(hf + 1) * HL, :].rearrange("p t b -> p (t b)"),
                   start=True, stop=True).then_inc(sq_ready, 1)
            pe.wait_ge(tab, 6)
            for n in range(4):
                if n == 0:
                    pe.wait_ge(kt_moved, 1)
                if n >= 2:
                    pe.wait_ge(row_moved, n - 1)
                q = L // 4
                mm(bank[4 + n % 2][:, 0:q * N], block_ones[:, :],
                   kd_row[:, n * q:(n + 1) * q, :].rearrange("p t n -> p (t n)"),
                   start=True, stop=True).then_inc(row_done, 1)

            e_bank, a_bank, mg_bank, sp_bank = bank[0], bank[1], bank[2], bank[4]
            g2_bank, st_bank, mt_bank = bank[5], bank[6], bank[7]
            flat_p = p_bd[:, :, :].rearrange("p n b -> p (n b)")

            def base_terms(kq_t):
                for c in range(C):
                    last = mm(e_bank[32 * c:32 * c + kq_t.shape[1], 0:P], kq_t, s_b[:, c, :], start=True, stop=False,
                              skip_group_check=True)
                last.then_inc(base_ready, 1)

            def minus_x(t):
                mm(a_bank[:, 0:C * B], neg_ident[:, :], x_a[:, bass.ds(t, 1)].rearrange("p o c b -> p (o c b)"),
                   start=True, stop=False, skip_group_check=True)

            def to_inner():
                mm(a_bank[:, 0:2 * C * B], e_c[:, :], pick[:, :], start=False, stop=True,
                   skip_group_check=True).then_inc(a_ready, 1)

            def s_update(cs):
                for c in cs:
                    last = mm(st_bank[:, c * P:(c + 1) * P], flat_p, m_b[:, c, :], start=False, stop=False,
                              skip_group_check=True)
                return last

            pe.wait_ge(zeroed, 12)
            pe.wait_ge(z_done, 2 * C)
            pe.wait_ge(row_moved, 4)
            pe.wait_ge(sq_moved, 2)
            pe.wait_ge(kt_moved, 1)
            zeros = m_b[:, :, :].rearrange("p c n -> p (c n)")
            mm(st_bank[:, :], flat_p, zeros, start=True, stop=False, skip_group_check=True)
            mm(e_bank[:, 0:P], flat_p, zeros[:, 0:P], start=True, stop=True, skip_group_check=True)
            mm(mg_bank[:, 0:P + B], flat_p, zeros[:, 0:P + B], start=True, stop=True, skip_group_check=True)
            base_terms(kq[:, 0, :])
            with pe.Fori(0, L // 2) as i:
                for par in range(2):
                    t = i * 2 + par
                    pe.wait_ge(mb_ready, LEAD + t)
                    pe.wait_ge(wbd_ready, LEAD + t)
                    for c in range(C):
                        last = mm(e_bank[32 * c:32 * c + B, 0:P], w_bd[:, :], m_b[:, c, :], start=False, stop=True,
                                  skip_group_check=True)
                    last.then_inc(err_ready, 1)
                    pe.wait_ge(y_saved, LEAD + t)
                    minus_x(t)
                    pe.wait_ge(e_copied, t + 1)
                    to_inner()
                    pe.wait_ge(pbd_ready, LEAD + t)
                    pe.wait_ge(sb_ready, LEAD + t)
                    s_update((0,))
                    pe.wait_ge(g_ready, t + 1)
                    for c in range(C):
                        last = mm(mg_bank[32 * c:32 * c + B, 0:P + B], m_g[:, c, N, :],
                                  m_g[:, c, :, :].rearrange("p n b -> p (n b)"), start=True, stop=True,
                                  skip_group_check=True)
                    last.then_inc(mg_ready, 1)
                    s_update((1, 2))
                    pe.wait_ge(ur_ready, t + 1)
                    mm(sp_bank[:, 0:N + 1], spread_u[:, :], u_row[:, :], start=True, stop=True).then_inc(spread_ready, 1)
                    s_update((3,)).then_inc(s_ready, 1)
                    pe.wait_ge(ma_ready, t + 1)
                    pe.wait_ge(ma0_ready, LEAD + t + 1)
                    for c in range(C):
                        last = nc.tensor.transpose(mt_bank[:, c * P:(c + 1) * P], m_a[c], ident[:, :])
                    last.then_inc(mt_ready, 1)
                    pe.wait_ge(bd_ready, t + 1)
                    mm(g2_bank[:, 0:N], gram_bd[:, :, :].rearrange("p n b -> p (n b)"), gram[:, :],
                       start=True, stop=True).then_inc(gram2_ready, 1)
                    pe.wait_ge(sb_ready, LEAD + t + 1)
                    pe.wait_ge(now_ready, t + 1)
                    base_terms(now[par][:, F_KQ.start:F_KQ.start + 32])
            pe.wait_ge(mb_ready, LEAD + L)
            pe.wait_ge(pbd_ready, LEAD + L)
            pe.wait_ge(sb_ready, LEAD + L)
            s_update(range(C)).then_inc(s_ready, 1)
            pe.wait_ge(y_saved, LEAD + L)
            minus_x(L)
            pe.wait_ge(e_copied, L + 1)
            to_inner()
            pe.wait_ge(sb_ready, LEAD + L + 1)
            base_terms(kq[:, L + 1, :])
            pe.wait_ge(y_saved, LEAD + L + 1)
            minus_x(L + 1)
            pe.wait_ge(e_copied, L + 2)
            to_inner()

            def k_project(b, par, g, to):
                for m in range(MC):
                    last = mm(to[:, 0:S2], wk[:, m, g * P:(g + 1) * P], ctx_t[par][:, m, :], start=(m == 0), stop=(m == MC - 1))
                last.then_inc(kp_ready, 1)

            def v_project(b, par, k, to):
                for m in range(MC):
                    last = mm(to[0:KW, 0:DM], ctx_t[par][:, m, k * KW:(k + 1) * KW], wv[:, m, :],
                              start=(m == 0), stop=(m == MC - 1))
                last.then_inc(vp_ready, 1)

            def scores(b, par, g):
                pe.wait_ge(qbd_ready, LEAD + b * 4 + (g + 1))
                pe.wait_ge(kp_moved, LEAD + b * 4 + (g + 1))
                for h in range(4):
                    hh = 4 * g + h
                    pe.wait_ge(max_ready, LEAD + b * H + max(hh - 2, 0))
                    mm(bank[hh % 3][0:L, 0:S2], q_bd[g % 2][:, h, :], k_t[par][:, g, :],
                       start=True, stop=True).then_inc(sc_ready, 1)

            def turn_max(b, g):
                pe.wait_ge(max_ready, LEAD + b * H + 4 * (g + 1))
                nc.tensor.transpose(bank[6][:, 0:L], row_max[g % 2][0:L, :], ident[0:L, 0:L]).then_inc(mxt_ready, 1)

            def turned_scores(b, par, g):
                pe.wait_ge(qmx_ready, LEAD + b * 4 + (g + 1))
                for k in range(KC):
                    n = KC * g + k
                    pe.wait_ge(exp_ready, LEAD + b * 4 * KC + (n - 1))
                    mm(bank[3 + n % 2][0:KW, 0:4 * L], k_t[par][:, g, k * KW:(k + 1) * KW],
                       q_mx[g % 2].rearrange("p h q -> p (h q)"), start=True, stop=True).then_inc(st_ready, 1)

            def values(b, par, g):
                pe.wait_ge(exp_ready, LEAD + b * 4 * KC + KC * (g + 1))
                pe.wait_ge(vp_moved, LEAD + b * KC + KC)
                if g == 0:
                    pe.wait_ge(o_copied, LEAD + b)
                for k in range(KC):
                    for h in range(4):
                        last = mm(bank[5][32 * h:32 * h + 32, g * L:(g + 1) * L], v_t[par][0:KW, k, 4 * g + h, :],
                                  prob_t[g % 2][0:KW, k, h * L:(h + 1) * L], start=(k == 0), stop=(k == KC - 1),
                                  skip_group_check=True)
                last.then_inc(pv_ready, 1)

            def turn_values(b):
                pe.wait_ge(o_copied, LEAD + b + 1)
                for g in range(4):
                    last = nc.tensor.transpose(bank[7][0:L, g * P:(g + 1) * P], o_raw[:, g, :], ident[:, :])
                last.then_inc(ot_ready, 1)

            def batch(b, par, loads, first=False, last=False):
                nxt = b + 1
                for g in range(4):
                    if g < 3:
                        scores(b, par, g + 1)
                    elif not last:
                        scores(nxt, 1 - par, 0)
                    if g == 1 and not first:
                        pe.wait_ge(vp_moved, LEAD + b * KC + KC)
                        turn_values(b - 1)
                    if not last:
                        pe.wait_ge(qa_ready, LEAD + b * 4 + (g + 1))
                        if g == 0:
                            pe.wait_ge(ctx_in[1 - par], loads * 32)
                        k_project(nxt, 1 - par, g, bank[6])
                    turned_scores(b, par, g)
                    if g > 0 and not last:
                        pe.wait_ge(att_ready, LEAD + b)
                        pe.wait_ge(vp_moved, LEAD + nxt * KC + (g - 1))
                        v_project(nxt, 1 - par, g - 1, bank[7])
                    if g > 0:
                        values(b, par, g - 1)
                    elif not first:
                        values(b - 1, 1 - par, 3)
                    if last:
                        pe.wait_ge(qa_ready, LEAD + b * 4 + (g + 1))
                    else:
                        pe.wait_ge(kp_moved, LEAD + nxt * 4 + (g + 1))
                    if g < 3:
                        turn_max(b, g + 1)
                    elif not last:
                        turn_max(nxt, 0)

            pe.wait_ge(y_saved, LEAD + LP)
            pe.wait_ge(att_in, 16 * 8)
            pe.wait_ge(ctx_in[0], 32)
            for g in range(4):
                k_project(0, 0, g, bank[4 + g])
            for k in range(KC):
                v_project(0, 0, k, bank[1 + k])
            pe.wait_ge(yb_ready, 1)
            pe.wait_ge(yb_half, 2)
            for b in range(B):
                if b % 2 == 0 and b > 0:
                    pe.wait_ge(vp_moved, LEAD + b // 2)
                for c in range(C):
                    last = mm(bank[b // 2][0:L, (b % 2) * DM:(b % 2 + 1) * DM], y_g[:, c, b, :], w_out[:, c, :],
                              start=(c == 0), stop=(c == C - 1))
                last.then_inc(proj_ready, 1)

            def turn_rows(src, ready, done, first_bank):
                for b in range(B):
                    if ready is not None:
                        pe.wait_ge(ready, b + 1)
                    for m in range(MC):
                        last = nc.tensor.transpose(bank[first_bank + 2 * m + b // 4][:, (b % 4) * L:(b % 4 + 1) * L],
                                                   src[0:L, b, m * P:(m + 1) * P], ident[0:L, 0:L])
                    last.then_inc(done, 1)

            pe.wait_ge(kp_moved, LEAD + 4)
            turn_rows(x1, x1_ready, x1t_ready, 4)
            for hf in range(2):
                pe.wait_ge(x1t_moved, hf + 1)
                pe.wait_ge(x1t_copied, hf + 1)
                for g in range(4):
                    for m in range(MC):
                        last = mm(bank[4 * hf + g][:, 0:HT], wq[:, m, g * P:(g + 1) * P], x1t[:, m, hf * HT:(hf + 1) * HT],
                                  start=(m == 0), stop=(m == MC - 1))
                    last.then_inc(qp_ready, 1)
            pe.wait_ge(q_moved, 4)
            pe.wait_ge(q_copied, 4)
            scores(0, 0, 0)
            turn_max(0, 0)
            batch(0, 0, 1, first=True)
            with pe.Fori(0, B // 2 - 1) as i:
                batch(i * 2 + 1, 1, i + 2)
                batch(i * 2 + 2, 0, i + 2)
            batch(B - 1, 1, None, last=True)
            values(B - 1, 1, 3)
            turn_values(B - 1)
            pe.wait_ge(att_ready, LEAD + B)
            turn_rows(att, None, att_t_ready, 0)
            pe.wait_ge(att_moved, 2)
            pe.wait_ge(att_copied, 2)
            for b in range(B):
                for m in range(MC):
                    last = mm(bank[4 + b // 2][0:L, (b % 2) * DM:(b % 2 + 1) * DM], at_t[:, m, b * L:(b + 1) * L], wo[:, m, :],
                              start=(m == 0), stop=(m == MC - 1))
                last.then_inc(wo_ready, 1)
            turn_rows(x2, x2_ready, x2t_ready, 0)
            pe.wait_ge(x2t_moved, 2)
            pe.wait_ge(x2t_copied, 2)
            for b in range(B):
                for m in range(MC):
                    last = mm(bank[4][0:L, b * E:(b + 1) * E], x2t[:, m, b * L:(b + 1) * L], w_gate[:, m, :],
                              start=(m == 0), stop=(m == MC - 1))
            last.then_inc(lg_ready, 1)
            pe.wait_ge(top, 5)
            one_hot = onehot[0:L].rearrange("p b e -> p (b e)")
            mm(bank[5][0:L, 0:B * E], earlier[0:L, :], one_hot, start=True, stop=True).then_inc(count_ready, 1)
            mm(bank[6][:, 0:B * E], ones[0:L, :], one_hot, start=True, stop=True).then_inc(count_ready, 1)

            pe.wait_ge(shared_in, 16)
            for f in range(C):
                for hf in range(2):
                    k = f * 2 + hf
                    if k >= 2:
                        pe.wait_ge(hid_ready, k - 1)
                    for weights, to, ready in ((wg, bank[k % 2], gate_ready), (wu, bank[2 + k % 2], up_ready)):
                        for m in range(MC):
                            last = mm(to[:, 0:HT], weights[:, m, f * P:(f + 1) * P],
                                      x2t[:, m, hf * HT:(hf + 1) * HT], start=(m == 0), stop=(m == MC - 1))
                        last.then_inc(ready, 1)
            pe.wait_ge(route_ready, 1)
            for b in range(B):
                if b == 0:
                    pe.wait_ge(hid_ready, 7)
                if b == B // 2 - 1:
                    pe.wait_ge(hid_ready, 8)
                if b >= 2:
                    pe.wait_ge(acc_ready, b - 1)
                for c in range(C):
                    last = mm(bank[4 + b % 2][0:L, 0:DM], hid[:, c, b * L:(b + 1) * L], wd[:, c, :],
                              start=(c == 0), stop=(c == C - 1))
                last.then_inc(down_ready, 1)

            def turn_in(par, j, loads):
                pe.wait_ge(rows_in_ready[par], 16 * loads)
                pe.wait_ge(turned_moved, LEAD + j)
                for m in range(MC):
                    last = nc.tensor.transpose(bank[7][:, m * P:(m + 1) * P], rows_in[par][:, m * P:(m + 1) * P], ident[:, :])
                last.then_inc(turned, 1)

            def gate_up(par, j, turn):
                pe.wait_ge(turned_moved, LEAD + j + 1)
                pe.wait_ge(rhid_ready, LEAD + j - 1)
                e = (experts[par] >> (turn * 3)) & (E - 1)
                for first_w, to, ready in ((0, bank[par], rg_ready), (MC, bank[2 + par], ru_ready)):
                    for m in range(MC):
                        last = mm(to[:, :], rows_t[par][:, m * P:(m + 1) * P],
                                  w_r[:, bass.ds(e, 1), first_w + m, :].rearrange("p o f -> p (o f)"),
                                  start=(m == 0), stop=(m == MC - 1))
                    last.then_inc(ready, 1)

            def turn_hidden(par, j):
                pe.wait_ge(rhid_ready, LEAD + j + 1)
                pe.wait_ge(rht_moved, LEAD + j)
                for c in range(C):
                    last = nc.tensor.transpose(bank[4][:, c * P:(c + 1) * P], hid_r[par][:, c * P:(c + 1) * P], ident[:, :])
                last.then_inc(rht_ready, 1)

            def down(par, j, turn):
                pe.wait_ge(rht_moved, LEAD + j + 1)
                pe.wait_ge(ry_moved, LEAD + j - 1)
                e = (experts[par] >> (turn * 3)) & (E - 1)
                for c in range(C):
                    last = mm(bank[5 + par][:, 0:DM], hid_t[par][:, c * P:(c + 1) * P],
                              w_r[:, bass.ds(e, 1), 2 * MC + c // 2, (c % 2) * DM:(c % 2 + 1) * DM].rearrange("p o f -> p (o f)"),
                              start=(c == 0), stop=(c == C - 1))
                last.then_inc(ry_ready, 1)

            def tile(par, j, turn, loads):
                gate_up(par, j, turn)
                turn_hidden(1 - par, j - 1)
                turn_in(1 - par, j + 1, loads)
                down(1 - par, j - 1, turn if par == 1 else turn - 1)

            pe.wait_ge(acc_ready, B)
            turn_in(0, 0, 1)
            pe.wait_ge(routed_in, 16 * E)
            pe.wait_ge(route_ready, 2)
            experts = [pe.value_load(expert_i[0:1, u:u + 1], min_val=0, max_val=E ** (NT // 2) - 1) for u in range(2)]
            gate_up(0, 0, 0)
            turn_in(1, 1, 1)
            with pe.Fori(0, NT // 2 - 1) as i:
                tile(1, i * 2 + 1, i, i + 2)
                tile(0, i * 2 + 2, i + 1, i + 2)
            gate_up(1, NT - 1, NT // 2 - 1)
            turn_hidden(0, NT - 2)
            down(0, NT - 2, NT // 2 - 1)
            turn_hidden(1, NT - 1)
            down(1, NT - 1, NT // 2 - 1)

        @block.vector
        def _(dve):
            v = nc.vector
            v.memset(x_in[:, :, 0:W - 1, :], 0.0).then_inc(zeroed, 1)
            v.memset(x_a[:, L:LP], 0.0).then_inc(zeroed, 1)
            v.memset(kq[:, L:LP, 0:B], 0.0).then_inc(zeroed, 1)
            v.memset(kq[:, 0:2, B:2 * B], 0.0).then_inc(zeroed, 1)
            v.memset(rec[:, L - 1, F_NEXT.start:F_TINY.start], 0.0).then_inc(zeroed, 1)
            v.memset(m_g[:, :, :, :], 0.0).then_inc(zeroed, 1)
            v.memset(m_b[:, :, :], 0.0).then_inc(zeroed, 1)
            v.memset(s_b[:, :, :], 0.0).then_inc(zeroed, 1)
            v.memset(gram[:, :], 0.0).then_inc(zeroed, 1)
            v.memset(p_bd[:, :, :], 0.0).then_inc(zeroed, 1)
            for buf in now:
                v.memset(buf[:, REC:], 0.0)
            v.memset(w_bd[:, :], 0.0).then_inc(zeroed, 1)
            v.memset(cols[:, :], 0.0).then_inc(zeroed, 1)
            dve.wait_ge(zeroed, 12)
            dve.wait_ge(pre_in, 64)
            for c in range(C):
                for hf in range(2):
                    n = c * 2 + hf
                    dve.wait_ge(xz_ready, n + 1)
                    v.tensor_copy(x_in[:, c, W - 1 + hf * HL:W - 1 + (hf + 1) * HL, :].rearrange("p t b -> p (t b)"),
                                  bank[n % 4][:, 0:HT]).then_inc(x_moved, 1)
                dve.wait_ge(x_moved, 2 * c + 2)
                if c >= 2:
                    dve.wait_ge(x_ready, c - 1)
                acc_c = conv[:, c % 2, :]
                for w in range(W):
                    win = x_in[:, c, w:w + L, :].rearrange("p t b -> p (t b)")
                    if w == 0:
                        ins = v.tensor_scalar(acc_c, win, conv_w[:, c, 0:1], None, ALU.mult)
                    else:
                        dve.wait_ge(conv_step, c * W + w)
                        ins = v.scalar_tensor_tensor(acc_c, win, conv_w[:, c, w:w + 1], acc_c, ALU.mult, ALU.add)
                    ins.then_inc(conv_step, 1)
            dve.wait_ge(const_in, 16 * 17)
            for hf in range(2):
                dve.wait_ge(lo_ready, hf + 1)
                v.tensor_copy(dt_lo[:, hf * HT:(hf + 1) * HT], bank[4 + hf][0:R, 0:HT]).then_inc(lo_moved, 1)
            for j in range(2):
                for hf in range(2):
                    dve.wait_ge(kq_ready, j * 2 + hf + 1)
                    t0 = hf * HL + 2 * j
                    v.tensor_tensor(kq[:, t0:t0 + HL, j * B:(j + 1) * B],
                                    bank[6 + hf][:, 0:HT].rearrange("p (t b) -> p t b", b=B),
                                    spread(batch_mask, 1, HL), ALU.mult).then_inc(kq_moved, 1)
            dve.wait_ge(kq_moved, 4)
            v.tensor_reduce(k_col[:, :], kq[:, 0:L, 0:B], AX.X, ALU.add).then_inc(tab, 1)
            dve.wait_ge(tab, 1)
            v.tensor_tensor(ks_col[:, :], k_col[:, :], step_gain[:, :], ALU.mult).then_inc(tab, 1)
            dve.wait_ge(tab, 2)
            v.tensor_copy(rec[:, :, F_KQ], kq[:, 1:L + 1, :]).then_inc(tab, 1)
            v.tensor_copy(rec[:, :, F_COL.start], ks_col[:, :]).then_inc(tab, 1)
            for buf in now_all:
                v.tensor_copy(buf[:, 0:MASKS], col_mask)
            v.tensor_scalar(rec[:, 0:L - 1, F_AK.start], k_col[:, 1:L], NS_A, None, ALU.mult)
            v.tensor_tensor(k_sq, kq[:, 0:L, 0:B], kq[:, 0:L, 0:B], ALU.mult).then_inc(tab, 1)
            v.tensor_tensor(kd_row, spread(col_mask, 1, L), spread(k_col[:, :], 2, N), ALU.mult).then_inc(tab, 1)
            dve.wait_ge(kt_ready, 1)
            v.tensor_copy(ks_t, bank[4][0:L, 0:P]).then_inc(kt_moved, 1)
            for hf in range(2):
                dve.wait_ge(sq_ready, hf + 1)
                v.tensor_copy(k_sq[:, hf * HL:(hf + 1) * HL, :].rearrange("p t b -> p (t b)"),
                              bank[6 + hf][:, 0:HT]).then_inc(sq_moved, 1)
            for n in range(4):
                q = L // 4
                dve.wait_ge(row_done, n + 1)
                row = bank[4 + n % 2][:, 0:q * N].rearrange("p (t n) -> p t n", n=N)
                skip = 1 if n == 0 else 0
                v.tensor_copy(rec[:, n * q + skip - 1:(n + 1) * q - 1, F_NEXT], row[:, skip:, :])
                v.tensor_tensor(rec[:, n * q:(n + 1) * q, F_ROW], row,
                                spread(step_gain[:, n * q:(n + 1) * q], 2, N), ALU.mult).then_inc(row_moved, 1)
            dve.wait_ge(row_moved, 4)
            v.tensor_scalar(rec[:, :, F_TRACE.start:F_TRACE.stop - 1], rec[:, :, F_ROW], 2.0, None, ALU.mult)
            v.tensor_tensor(kd_row, rec[:, :, F_ROW], rec[:, :, F_ROW], ALU.mult).then_inc(tab, 1)
            dve.wait_ge(tab, 7)
            v.tensor_reduce(rec[:, :, F_TRACE.stop - 1], kd_row, AX.X, ALU.add)
            v.tensor_scalar(rec[:, :, F_TINY.start], step_gain[:, :], TINY, None, ALU.mult).then_inc(tab, 1)
            for hf in range(2):
                k = 5 * hf
                sp_a, sp_u = sp_a_of[hf], sp_u_of[hf]
                dve.wait_ge(sp_act, 2 * C + 3 * hf + 2)
                v.tensor_scalar(sp_u, sp_e, 1.0, None, ALU.add).then_inc(sp_dve, 1)
                dve.wait_ge(sp_dve, k + 1)
                dve.wait_ge(sp_act, 2 * C + 3 * hf + 3)
                v.scalar_tensor_tensor(sp_e, sp_u, -1.0, sp_e, ALU.add, ALU.subtract).then_inc(sp_dve, 1)
                v.scalar_tensor_tensor(sp_a, sp_a, 0.0, sp_l, ALU.max, ALU.add).then_inc(sp_dve, 1)
                dve.wait_ge(sp_dve, k + 3)
                v.tensor_tensor(sp_a, sp_a, sp_e, ALU.subtract).then_inc(sp_dve, 1)
                dve.wait_ge(sp_dve, k + 4)
                dve.wait_ge(sq_moved, 2)
                dtv = sp_a.rearrange("p (t c b) -> p t c b", c=C, b=B)
                v.tensor_tensor(sp_u.rearrange("p (t c b) -> p t c b", c=C, b=B), dtv,
                                spread(k_sq[:, hf * HL:(hf + 1) * HL, :], 2, C), ALU.mult).then_inc(sp_dve, 1)
                dve.wait_ge(sp_dve, k + 5)
                v.tensor_scalar(sp_u, sp_u, 1.0, None, ALU.add).then_inc(tab, 1)
            dve.wait_ge(tab, 10)
            dve.wait_ge(k_out, 16)

            e_bank, a_bank, mg_bank, sp_bank, g2_bank = bank[0], bank[1], bank[2], bank[4], bank[5]
            a_view = a_bank[:, 0:2 * C * B].rearrange("p (e c b) -> p e c b", e=2, c=C)

            def save_y(t):
                v.tensor_copy(y_a[:, bass.ds(t, 1)].rearrange("p o c b -> p (o c) b"), a_view[:, 1]).then_inc(y_saved, 1)

            with dve.Fori(0, L // 2) as i:
                for par in range(2):
                    t = i * 2 + par
                    dve.wait_ge(err_ready, t + 1)
                    v.tensor_copy(e_c[:, :], e_bank[:, 0:P]).then_inc(e_copied, 1)
                    v.reciprocal(eps[:, :], eps_a[:, bass.ds(t, 1)].rearrange("p o c b -> p (o c b)")).then_inc(recip_ready, 1)
                    dve.wait_ge(recip_ready, t + 1)
                    v.tensor_tensor(eps[:, :], eps[:, :], y_a[:, bass.ds(t, 1)].rearrange("p o c b -> p (o c b)"),
                                    ALU.mult).then_inc(eps_ready, 1)
                    dve.wait_ge(eps_ready, t + 1)
                    dve.wait_ge(a_ready, t + 1)
                    v.tensor_tensor(g_a, a_view[:, 0], eps[:, :].rearrange("p (c b) -> p c b", b=B),
                                    ALU.mult).then_inc(g_ready, 1)
                    save_y(t)
                    dve.wait_ge(mg_ready, t + 1)
                    v.tensor_tensor(mg_m[:, :, :], mg_bank[:, 0:P + B].rearrange("p (n b) -> p n b", b=B),
                                    spread(tile_mask[:, :], 1, N + 1), ALU.mult).then_inc(mgm_ready, 1)
                    dve.wait_ge(mgm_ready, t + 1)
                    v.tensor_reduce(u_row[:, :], mg_m[:, :, :], AX.X, ALU.add).then_inc(ur_ready, 1)
                    dve.wait_ge(outer_ready, t + 1)
                    v.tensor_tensor(m_a[0], m_a[0], outer[:, 0, :], ALU.add).then_inc(ma0_ready, 1)
                    dve.wait_ge(spread_ready, t + 1)
                    dve.wait_ge(now_ready, t + 1)
                    v.tensor_tensor_reduce(junk2[:, :], sp_bank[:, 0:N + 1], now_all[par][:, 0:N + 1], 1.0, 0.0, ALU.mult,
                                           ALU.add, v_col).then_inc(v_ready, 1)
                    v.tensor_tensor_reduce(junk[:, :], sp_bank[:, 0:N + 1], now[par][:, F_TRACE], 1.0, trace,
                                           ALU.mult, ALU.add, trace1).then_inc(trace1_ready, 1)
                    v.scalar_tensor_tensor(gram1[:, :], sp_bank[:, 0:N], now[par][:, F_COL], gram[:, :], ALU.mult,
                                           ALU.add).then_inc(gram1_ready, 1)
                    dve.wait_ge(trace1_ready, t + 1)
                    v.tensor_scalar(trace, trace1, 0.0, None, ALU.max).then_inc(trace_ready, 1)
                    dve.wait_ge(v_ready, t + 1)
                    dve.wait_ge(gram1_ready, t + 1)
                    v.scalar_tensor_tensor(gram[:, :], now[par][:, F_ROW], v_col, gram1[:, :], ALU.mult,
                                           ALU.add).then_inc(gram_ready, 1)
                    dve.wait_ge(root_ready, t + 1)
                    v.tensor_scalar(norm, root, now[par][:, F_TINY], -1.0, ALU.add, ALU.mult).then_inc(norm_ready, 1)
                    dve.wait_ge(gram_ready, t + 1)
                    v.tensor_tensor(gram_bd[:, :, :], spread(gram[:, :], 2, B), block_mask[:, :, :], ALU.mult).then_inc(bd_ready, 1)
                    dve.wait_ge(norm_ready, t + 1)
                    v.reciprocal(rneg, norm).then_inc(rneg_ready, 1)
                    v.tensor_tensor_reduce(junk3[:, :], gram[:, :], now[par][:, F_NEXT], 1.0, 0.0, ALU.mult,
                                           ALU.add, gk_col).then_inc(gk_ready, 1)
                    dve.wait_ge(rneg_ready, t + 1)
                    v.tensor_scalar(r2b, rneg, rneg, NS_B, ALU.mult, ALU.mult).then_inc(r2b_ready, 1)
                    v.tensor_scalar(r2c, rneg, rneg, NS_C / NS_B, ALU.mult, ALU.mult).then_inc(r2c_ready, 1)
                    dve.wait_ge(r2b_ready, t + 1)
                    dve.wait_ge(gk_ready, t + 1)
                    v.scalar_tensor_tensor(ak_col, gk_col, r2b, now[par][:, F_AK], ALU.mult, ALU.add).then_inc(ak_ready, 1)
                    dve.wait_ge(r2c_ready, t + 1)
                    v.tensor_tensor(r4, r2b, r2c, ALU.mult).then_inc(r4_ready, 1)
                    dve.wait_ge(ak_ready, t + 1)
                    dve.wait_ge(r4_ready, t + 1)
                    dve.wait_ge(gram2_ready, t + 1)
                    v.tensor_tensor_reduce(junk4[:, :], g2_bank[:, 0:N], now[par][:, F_NEXT], r4, ak_col, ALU.mult,
                                           ALU.add, w_col).then_inc(w_ready, 1)
                    v.scalar_tensor_tensor(poly[:, :], g2_bank[:, 0:N], r2c, gram[:, :], ALU.mult, ALU.add).then_inc(poly_ready, 1)
                    dve.wait_ge(w_ready, LEAD + t + 1)
                    v.tensor_scalar(w_bd[:, :], batch_mask, w_col, rneg, ALU.mult, ALU.mult).then_inc(wbd_ready, 1)
                    dve.wait_ge(poly_ready, t + 1)
                    v.scalar_tensor_tensor(ns_p[:, :], poly[:, :], r2b, scaled_eye, ALU.mult, ALU.add).then_inc(p_ready, 1)
                    dve.wait_ge(p_ready, t + 1)
                    dve.wait_ge(s_ready, t + 1)
                    v.scalar_tensor_tensor(p_bd[:, :, :], spread(ns_p[:, :], 2, B), rneg, block_mask[:, :, :],
                                           ALU.mult, ALU.mult).then_inc(pbd_ready, 1)
            for t in (L, L + 1):
                dve.wait_ge(base_ready, t + 1)
                v.tensor_copy(e_c[:, :], e_bank[:, 0:P]).then_inc(e_copied, 1)
                dve.wait_ge(a_ready, t + 1)
                save_y(t)

            mean_var = stat[0:L, 48:64].rearrange("p (b v) -> p b v", b=B)

            def layer_norm(src, src_ready, rows_per, dst, n, done):
                for b in range(B):
                    dve.wait_ge(src_ready, b // rows_per + 1)
                    v.bn_stats(stat[0:L, 6 * b:6 * b + 6], src[0:L, b, :]).then_inc(ln, 1)
                for b in range(B):
                    dve.wait_ge(ln, n * 17 + b + 1)
                    v.bn_aggr(mean_var[:, b, :], stat[0:L, 6 * b:6 * b + 6]).then_inc(ln, 1)
                dve.wait_ge(std_ready, n + 1)
                v.reciprocal(stat[0:L, 160:168], stat[0:L, 64:72]).then_inc(ln, 1)
                dve.wait_ge(ln, n * 17 + 17)
                for b in range(B):
                    v.tensor_scalar(dst[0:L, b, :], src[0:L, b, :], mean_var[:, b, 0:1], stat[0:L, 160 + b:161 + b],
                                    ALU.subtract, ALU.mult).then_inc(done, 1)

            def prepare_mask(b, par, loads):
                dve.wait_ge(ctx_in[par], loads * 32)
                dve.wait_ge(kp_moved, LEAD + b * 4)
                v.tensor_copy(mask_f, mask_i[par][:, :]).then_inc(msk, 1)
                dve.wait_ge(msk, LEAD + b * 3 + 1)
                v.tensor_scalar(mask_f, mask_f, 0.0, None, ALU.not_equal).then_inc(msk, 1)
                dve.wait_ge(msk, LEAD + b * 3 + 2)
                v.tensor_scalar(mask_f, mask_f, mask_gain, mask_base, ALU.mult, ALU.add).then_inc(msk, 1)

            def move_k(b, par, g, src):
                dve.wait_ge(kp_ready, LEAD + b * 4 + (g + 1))
                if g == 0:
                    dve.wait_ge(msk, LEAD + b * 3 + 3)
                v.scalar_tensor_tensor(k_t[par][:, g, :], src[:, 0:S2], bias_qk[:, 1, g:g + 1], mask_f,
                                       ALU.add, ALU.mult).then_inc(kp_moved, 1)

            def move_v(b, par, k, src):
                dve.wait_ge(vp_ready, LEAD + b * KC + (k + 1))
                v.tensor_tensor(v_t[par][0:KW, k, :, 0:DK], src[0:KW, 0:DM].rearrange("p (h e) -> p h e", h=H),
                                bias_rows[0:KW, 0, :].rearrange("p (h e) -> p h e", h=H), ALU.add).then_inc(vp_moved, 1)

            def maxima(b, g):
                dve.wait_ge(mxt_ready, LEAD + b * 4 + (g - 1))
                for h in range(4):
                    hh = 4 * g + h
                    dve.wait_ge(sc_ready, LEAD + b * H + (hh + 1))
                    v.tensor_reduce(row_max[g % 2][0:L, 32 * h + DK + 1:32 * h + DK + 2], bank[hh % 3][0:L, 0:S2], AX.X,
                                    ALU.max, negate=True).then_inc(max_ready, 1)

            def add_max(b, g):
                dve.wait_ge(mxt_ready, LEAD + b * 4 + (g + 1))
                dve.wait_ge(qmx_ready, LEAD + b * 4 + (g - 1))
                v.tensor_tensor(q_aug[g % 2], q_s[:, g, L * b:L * (b + 1)] if isinstance(b, int) else
                                q_s[:, g, bass.ds(b * L, L)], bank[6][:, 0:L], ALU.add).then_inc(qa_ready, 1)

            def divide(b):
                dve.wait_ge(ot_ready, LEAD + b + 1)
                o_t = bank[7][0:L, :].rearrange("p (h e) -> p h e", h=H)
                v.reciprocal(row_inv[0:L, :], o_t[:, :, DK]).then_inc(inv_ready, 1)
                dve.wait_ge(inv_ready, LEAD + b + 1)
                v.tensor_tensor(att[0:L, bass.ds(b, 1), :].rearrange("p o (h e) -> p (o h) e", h=H), o_t[:, :, 0:DK],
                                spread(row_inv[0:L, :], 2, DK), ALU.mult).then_inc(att_ready, 1)

            def batch(b, par, loads, first=False, last=False):
                nxt = b + 1
                for g in range(4):
                    if g < 3:
                        maxima(b, g + 1)
                    elif not last:
                        maxima(nxt, 0)
                    if g == 1 and not first:
                        divide(b - 1)
                    if not last:
                        if g == 0:
                            prepare_mask(nxt, 1 - par, loads)
                        move_k(nxt, 1 - par, g, bank[6])
                        if g > 0:
                            move_v(nxt, 1 - par, g - 1, bank[7])
                    if g < 3:
                        add_max(b, g + 1)
                    elif not last:
                        add_max(nxt, 0)

            dve.wait_ge(y_saved, LEAD + LP)
            dve.wait_ge(ma_ready, L)
            for c in range(C):
                v.scalar_tensor_tensor(y_g[:, c], x_a[:, 0:L, c, :].rearrange("p t b -> p b t"), vecs[:, 2, c:c + 1],
                                       y_a[:, 2:LP, c, :].rearrange("p t b -> p b t"), ALU.mult, ALU.add).then_inc(y_step, 1)
            dve.wait_ge(y_step, C)
            for c in range(2, C):
                ins = v.tensor_tensor(y_g[:, c], y_g[:, c], z_a[:, :, c, :].rearrange("p t b -> p b t"), ALU.mult)
            ins.then_inc(yb_ready, 1)
            v.tensor_scalar(q_bias, bias_qk[:, 0, :], DK ** -0.5, None, ALU.mult).then_inc(qb_ready, 1)
            dve.wait_ge(cleared, 4)
            prepare_mask(0, 0, 1)
            for g in range(4):
                move_k(0, 0, g, bank[4 + g])
            for k in range(KC):
                move_v(0, 0, k, bank[1 + k])
            dve.wait_ge(att_in, 16 * 8)
            for j in range(B // 2):
                dve.wait_ge(proj_ready, 2 * j + 2)
                v.tensor_tensor(h1[0:L, 2 * j:2 * j + 2, :], bank[j][0:L, :].rearrange("p (b d) -> p b d", b=2),
                                xb[0:L, 2 * j:2 * j + 2, :], ALU.add).then_inc(h1_ready, 1)
            layer_norm(h1, h1_ready, 2, x1, 0, x1_ready)
            for hf in range(2):
                dve.wait_ge(x1t_ready, 4 * hf + 4)
                v.tensor_copy(x1t[:, 1, hf * HT:(hf + 1) * HT], bank[6 + hf][:, 0:HT]).then_inc(x1t_moved, 1)
            dve.wait_ge(qb_ready, 1)
            for hf in range(2):
                for g in range(2, 4):
                    dve.wait_ge(qp_ready, 4 * hf + g + 1)
                    v.tensor_scalar(q_s[:, g, hf * HT:(hf + 1) * HT], bank[4 * hf + g][:, 0:HT], DK ** -0.5,
                                    q_bias[:, g:g + 1], ALU.mult, ALU.add).then_inc(q_moved, 1)
            dve.wait_ge(q_moved, 4)
            dve.wait_ge(q_copied, 4)
            maxima(0, 0)
            add_max(0, 0)
            batch(0, 0, 1, first=True)
            with dve.Fori(0, B // 2 - 1) as i:
                batch(i * 2 + 1, 1, i + 2)
                batch(i * 2 + 2, 0, i + 2)
            batch(B - 1, 1, None, last=True)
            divide(B - 1)

            def move_turned(dst, ready, moved):
                for hf in range(2):
                    dve.wait_ge(ready, 4 * hf + 4)
                    v.tensor_copy(dst[:, 1, hf * HT:(hf + 1) * HT], bank[2 + hf][:, 0:HT]).then_inc(moved, 1)

            move_turned(at_t, att_t_ready, att_moved)
            dve.wait_ge(x1b_ready, 1)
            for j in range(B // 2):
                dve.wait_ge(wo_ready, 2 * j + 2)
                v.tensor_tensor(h1[0:L, 2 * j:2 * j + 2, :], bank[4 + j][0:L, :].rearrange("p (b d) -> p b d", b=2),
                                xb[0:L, 2 * j:2 * j + 2, :], ALU.add).then_inc(h2_ready, 1)
            layer_norm(h1, h2_ready, 2, x2, 1, x2_ready)
            move_turned(x2t, x2t_ready, x2t_moved)
            dve.wait_ge(lg_ready, 1)
            logits = bank[4][0:L, 0:B * E].rearrange("p (b e) -> p b e", b=B)
            v.tensor_reduce(top_logit[0:L, :], logits, AX.X, ALU.max).then_inc(top, 1)
            dve.wait_ge(top, 1)
            v.tensor_tensor(lg[0:L], logits, spread(top_logit[0:L, :], 2, E), ALU.is_equal).then_inc(top, 1)
            dve.wait_ge(top, 2)
            v.tensor_tensor(lg[0:L], lg[0:L], spread(tie_rank[0:L, :], 1, B), ALU.mult).then_inc(top, 1)
            dve.wait_ge(top, 3)
            v.tensor_reduce(top_rank[0:L, :], lg[0:L], AX.X, ALU.max).then_inc(top, 1)
            dve.wait_ge(top, 4)
            v.tensor_tensor(onehot[0:L], lg[0:L], spread(top_rank[0:L, :], 2, E), ALU.is_equal).then_inc(top, 1)
            def by(ap, n=B):
                return ap.rearrange("p (b e) -> p b e", b=n)

            step = [0]

            def after(ins):
                ins.then_inc(route_step, 1)
                step[0] += 1
                dve.wait_ge(route_step, step[0])

            dve.wait_ge(count_ready, 2)
            after(v.tensor_copy(r_tot, bank[6][:, 0:B * E]))
            v.tensor_reduce(r_cnt, by(r_tot).rearrange("p b e -> p e b"), AX.X, ALU.add).then_inc(route_step, 1)
            v.memset(r_pre[:, 0:E], 0.0).then_inc(route_step, 1)
            step[0] += 2
            dve.wait_ge(route_step, step[0])
            after(v.tensor_tensor(by(r_cmp, E), spread(r_cnt, 2, E), spread(tile_start, 1, E), ALU.is_gt))
            after(v.tensor_reduce(r_tiles, by(r_cmp, E), AX.X, ALU.add))
            after(v.tensor_tensor(by(r_tri, E), spread(r_tiles, 1, E), by(before_e, E), ALU.mult))
            after(v.tensor_reduce(r_base, by(r_tri, E), AX.X, ALU.add))
            for b in range(1, B):
                after(v.tensor_tensor(r_pre[:, b * E:(b + 1) * E], r_pre[:, (b - 1) * E:b * E], r_tot[:, (b - 1) * E:b * E], ALU.add))
            after(v.scalar_tensor_tensor(by(r_pre), spread(r_base, 1, B), float(P), by(r_pre), ALU.mult, ALU.add))
            after(v.tensor_tensor(r_pos[0:L, :], bank[5][0:L, 0:B * E], r_pre[0:L, :], ALU.add))
            after(v.tensor_tensor(by(r_pos)[0:L], by(r_pos)[0:L], onehot[0:L], ALU.mult))
            after(v.tensor_reduce(r_slot[0:L, :], by(r_pos)[0:L], AX.X, ALU.add))
            v.tensor_copy(slot_i[0:L, :], r_slot[0:L, :]).then_inc(route_ready, 1)
            after(v.tensor_tensor(r_end, r_base, r_tiles, ALU.add))
            after(v.tensor_tensor(by(r_end_cmp, NT), spread(r_end, 1, NT), spread(tile_no, 2, E), ALU.is_le))
            after(v.tensor_reduce(r_tile, by(r_end_cmp, NT), AX.X, ALU.add))
            after(v.tensor_scalar(r_tile, r_tile, float(E - 1), None, ALU.min))
            after(v.tensor_tensor(r_tile, r_tile, digit, ALU.mult))
            after(v.tensor_reduce(r_cnt[:, 0:2], r_tile.rearrange("p (k u) -> p u k", u=2), AX.X, ALU.add))
            v.tensor_copy(expert_i[:, :], r_cnt[:, 0:2]).then_inc(route_ready, 1)

            for k in range(8):
                f, hf = k // 2, k % 2
                dve.wait_ge(up_ready, k + 1)
                dve.wait_ge(silu_ready, k + 1)
                v.tensor_tensor(hid[:, f, hf * HT:(hf + 1) * HT], bank[2 + k % 2][:, 0:HT], gate[:, k % 2, :],
                                ALU.mult).then_inc(hid_ready, 1)
            for b in range(B):
                dve.wait_ge(down_ready, b + 1)
                v.tensor_tensor(acc[0:L, b, :], bank[4 + b % 2][0:L, 0:DM], x2[0:L, b, :], ALU.add).then_inc(acc_ready, 1)

            def routed_tile(par, j):
                dve.wait_ge(ru_ready, LEAD + j + 1)
                dve.wait_ge(rsilu_ready, LEAD + j + 1)
                dve.wait_ge(rht_ready, LEAD + j - 1)
                v.tensor_tensor(hid_r[par], bank[2 + par][:, :], silu_r[par], ALU.mult).then_inc(rhid_ready, 1)
                dve.wait_ge(rht_ready, LEAD + j + 1)
                dve.wait_ge(ry_ready, LEAD + j - 1)
                v.tensor_copy(hid_t[par], bank[4][:, :]).then_inc(rht_moved, 1)

            with dve.Fori(0, NT // 2) as i:
                routed_tile(0, i * 2)
                routed_tile(1, i * 2 + 1)
            for b in range(B):
                dve.wait_ge(back_in[b], 16)
                v.tensor_tensor(acc[0:L, b, :], acc[0:L, b, :], att[0:L, b, :], ALU.add).then_inc(sum_ready, 1)
            layer_norm(acc, sum_ready, 1, h1, 2, y_ready)

        @block.scalar
        def _(act):
            a = nc.scalar.activation
            act.wait_ge(pre_in, 64)
            for c in range(C):
                act.wait_ge(conv_step, (c + 1) * W)
                a(x_a[:, 0:L, c, :], conv[:, c % 2, :].rearrange("p (t b) -> p t b", b=B), ACT.Silu,
                  bias=vecs[:, 0, c:c + 1]).then_inc(x_ready, 1)
            for hf in range(2):
                for c in range(C):
                    act.wait_ge(dt_ready, hf * C + c + 1)
                    a(sp_a_of[hf].rearrange("p (t c b) -> p t c b", c=C, b=B)[:, :, c, :],
                      bank[c][:, 0:HT].rearrange("p (t b) -> p t b", b=B), ACT.Identity,
                      bias=vecs[:, 1, c:c + 1]).then_inc(sp_act, 1)
            for n in range(2 * C):
                c, hf = n // 2, n % 2
                act.wait_ge(xz_ready, 2 * C + n + 1)
                a(z_a[:, hf * HL:(hf + 1) * HL, c, :], bank[n % 4][:, 0:HT].rearrange("p (t b) -> p t b", b=B),
                  ACT.Silu).then_inc(z_done, 1)
            act.wait_ge(sp_act, 2 * C)
            for hf in range(2):
                if hf == 1:
                    act.wait_ge(sp_dve, 4)
                k = 2 * C + 3 * hf
                a(sp_e, sp_a_of[hf], ACT.Abs).then_inc(sp_act, 1)
                act.wait_ge(sp_act, k + 1)
                a(sp_e, sp_e, ACT.Exp, scale=-1.0).then_inc(sp_act, 1)
                act.wait_ge(sp_dve, 5 * hf + 1)
                a(sp_l, sp_u_of[hf], ACT.Ln).then_inc(sp_act, 1)

            act.wait_ge(zeroed, 12)
            act.wait_ge(base_ready, 1)
            with act.Fori(0, L // TURN) as i:
                a(dummy, cols[:, 12:13], ACT.Sqrt)
                for u in range(TURN):
                    t = i * TURN + u
                    act.wait_ge(trace_ready, t + 1)
                    a(root, trace, ACT.Sqrt).then_inc(root_ready, 1)
                    act.wait_ge(s_ready, t + 1)
                    act.wait_ge(base_ready, t + 1)
                    nc.scalar.copy(s_b[:, :, :].rearrange("p c n -> p (c n)"), bank[6][:, :]).then_inc(sb_ready, 1)
                    act.wait_ge(mt_ready, t + 1)
                    nc.scalar.copy(m_b[:, :, :].rearrange("p c n -> p (c n)"), bank[7][:, :]).then_inc(mb_ready, 1)
            act.wait_ge(s_ready, L + 1)
            act.wait_ge(base_ready, L + 1)
            nc.scalar.copy(s_b[:, :, :].rearrange("p c n -> p (c n)"), bank[6][:, :]).then_inc(sb_ready, 1)

            def deviation(n):
                act.wait_ge(ln, n * 17 + 16)
                a(stat[0:L, 64:72], stat[0:L, 48:64].rearrange("p (b v) -> p b v", b=B)[:, :, 1], ACT.Sqrt,
                  bias=eps_ln[0:L, :]).then_inc(std_ready, 1)

            def move_turned(dst, ready, moved, first_bank):
                for hf in range(2):
                    act.wait_ge(ready, 4 * hf + 4)
                    nc.scalar.copy(dst[:, 0, hf * HT:(hf + 1) * HT], bank[first_bank + hf][:, 0:HT]).then_inc(moved, 1)

            def copy_values(b):
                act.wait_ge(pv_ready, LEAD + b * 4 + 4)
                act.wait_ge(ot_ready, LEAD + b)
                nc.scalar.copy(o_raw.rearrange("p g q -> p (g q)"), bank[5][:, 0:4 * L]).then_inc(o_copied, 1)

            def batch(b, first=False):
                for g in range(4):
                    act.wait_ge(pv_ready, LEAD + b * 4 + (g - 1))
                    for k in range(KC):
                        n = KC * g + k
                        act.wait_ge(st_ready, LEAD + b * 4 * KC + (n + 1))
                        a(prob_t[g % 2][0:KW, k, :], bank[3 + n % 2][0:KW, 0:4 * L], ACT.Exp).then_inc(exp_ready, 1)
                    if g == 0 and not first:
                        copy_values(b - 1)

            deviation(0)
            move_turned(x1t, x1t_ready, x1t_copied, 4)
            act.wait_ge(qb_ready, 1)
            for hf in range(2):
                for g in range(2):
                    act.wait_ge(qp_ready, 4 * hf + g + 1)
                    a(q_s[:, g, hf * HT:(hf + 1) * HT], bank[4 * hf + g][:, 0:HT], ACT.Identity,
                      bias=q_bias[:, g:g + 1], scale=DK ** -0.5).then_inc(q_copied, 1)
            batch(0, first=True)
            with act.Fori(1, B) as b:
                batch(b)
            copy_values(B - 1)
            move_turned(at_t, att_t_ready, att_copied, 0)
            deviation(1)
            move_turned(x2t, x2t_ready, x2t_copied, 0)
            act.wait_ge(top, 1)
            a(score[0:L, :], top_logit[0:L, :], ACT.Sigmoid).then_inc(score_ready, 1)
            act.wait_ge(x2_ready, B)
            act.wait_ge(score_ready, 1)
            for b in range(B):
                a(xs[0:L, b, :], x2[0:L, b, :], ACT.Copy, scale=score[0:L, b:b + 1]).then_inc(xs_ready, 1)

            for k in range(8):
                act.wait_ge(gate_ready, k + 1)
                if k >= 2:
                    act.wait_ge(hid_ready, k - 1)
                a(gate[:, k % 2, :], bank[k % 2][:, 0:HT], ACT.Silu).then_inc(silu_ready, 1)

            def move_rows(par, j):
                act.wait_ge(turned, LEAD + j + 1)
                act.wait_ge(ru_ready, LEAD + j - 1)
                nc.scalar.copy(rows_t[par], bank[7][:, 0:DM]).then_inc(turned_moved, 1)

            def silu_rows(par, j):
                act.wait_ge(rg_ready, LEAD + j + 1)
                act.wait_ge(rhid_ready, LEAD + j - 1)
                a(silu_r[par], bank[par][:, :], ACT.Silu).then_inc(rsilu_ready, 1)

            def move_out(par, j, stored):
                act.wait_ge(ry_ready, LEAD + j + 1)
                if stored is not None:
                    act.wait_ge(tile_out[par], 16 * stored)
                nc.scalar.copy(y_r[par], bank[5 + par][:, 0:DM]).then_inc(ry_moved, 1)

            move_rows(0, 0)
            silu_rows(0, 0)
            move_rows(1, 1)
            silu_rows(1, 1)
            move_rows(0, 2)
            move_out(0, 0, None)
            silu_rows(0, 2)
            move_rows(1, 3)
            move_out(1, 1, None)
            with act.Fori(1, NT // 2 - 1) as i:
                silu_rows(1, i * 2 + 1)
                move_rows(0, i * 2 + 2)
                move_out(0, i * 2, i)
                silu_rows(0, i * 2 + 2)
                move_rows(1, i * 2 + 3)
                move_out(1, i * 2 + 1, i)
            silu_rows(1, NT - 1)
            move_out(0, NT - 2, NT // 2 - 1)
            move_out(1, NT - 1, NT // 2 - 1)
            deviation(2)

        @block.gpsimd
        def _(pool):
            pool.wait_ge(zeroed, 12)
            pool.wait_ge(ks_in, 64)
            pool.wait_ge(row_moved, 4)
            pool.wait_ge(tab, 8)
            with pool.Fori(0, L // 2) as i:
                for par in range(2):
                    t = i * 2 + par
                    pool.wait_ge(w_ready, LEAD + i * 2)
                    pool.wait_ge(base_ready, i * 2 + 1)
                    nc.gpsimd.tensor_copy(now[par][:, 0:REC], rec[:, bass.ds(t, 1), :].rearrange("p o f -> p (o f)")).then_inc(now_ready, 1)
                    pool.wait_ge(g_ready, t + 1)
                    pool.wait_ge(ma0_ready, LEAD + t)
                    nc.gpsimd.tensor_tensor(outer[:, :, :].rearrange("p c (n b) -> p c n b", b=B),
                                            spread(g_a, 2, N),
                                            spread(ks_all[:, bass.ds(t, 1), :].rearrange("p o (n b) -> p (o n) b", b=B), 1, C),
                                            ALU.mult).then_inc(outer_ready, 1)
                    pool.wait_ge(outer_ready, t + 1)
                    pool.wait_ge(mg_ready, t + 1)
                    flat_m = m_g[:, 1:C, 0:N, :].rearrange("p c n b -> p c (n b)")
                    nc.gpsimd.tensor_tensor(flat_m, flat_m, outer[:, 1:C, :], ALU.add).then_inc(ma_ready, 1)
            pool.wait_ge(now_ready, L)
            pool.wait_ge(ma_ready, L)
            for par in range(2):
                nc.gpsimd.memset(v_t[par][:, :, :, DK:], 1.0).then_inc(cleared, 1)
                nc.gpsimd.memset(row_max[par], 0.0).then_inc(cleared, 1)
            for c in range(2):
                pool.wait_ge(y_step, c + 1)
                nc.gpsimd.tensor_tensor(y_g[:, c], y_g[:, c], z_a[:, :, c, :].rearrange("p t b -> p b t"),
                                        ALU.mult).then_inc(yb_half, 1)
            def q_blocks(b, g, fresh=False):
                if not fresh:
                    pool.wait_ge(sc_ready, LEAD + b * H + 4 * (g - 1))
                nc.gpsimd.tensor_tensor(q_bd[g % 2], spread(q_s[:, g, bass.ds(b * L, L)], 1, 4),
                                        spread(head_rows, 2, L), ALU.mult).then_inc(qbd_ready, 1)

            def q_max_blocks(b, g, fresh=False):
                pool.wait_ge(qa_ready, LEAD + b * 4 + (g + 1))
                if not fresh:
                    pool.wait_ge(st_ready, LEAD + b * 4 * KC + KC * (g - 1))
                nc.gpsimd.tensor_tensor(q_mx[g % 2], spread(q_aug[g % 2], 1, 4), spread(head_rows, 2, L),
                                        ALU.mult).then_inc(qmx_ready, 1)

            def batch(b, first=False, last=False):
                for g in range(4):
                    if g < 2:
                        q_blocks(b, g + 2)
                    elif not last:
                        q_blocks(b + 1, g - 2)
                    if g < 3:
                        q_max_blocks(b, g + 1, fresh=first and g == 0)
                    elif not last:
                        q_max_blocks(b + 1, 0)

            pool.wait_ge(q_moved, 4)
            pool.wait_ge(q_copied, 4)
            q_blocks(0, 0, fresh=True)
            q_blocks(0, 1, fresh=True)
            pool.wait_ge(x1_ready, B)
            nc.gpsimd.tensor_tensor(xb[0:L], x1[0:L], spread(bias_rows[0:L, 1, :], 1, B), ALU.add).then_inc(x1b_ready, 1)
            q_max_blocks(0, 0, fresh=True)
            batch(0, first=True)
            with pool.Fori(1, B - 1) as b:
                batch(b)
            batch(B - 1, last=True)
            pool.wait_ge(rows_zero, 16)
            pool.wait_ge(route_ready, 1)
            for b in range(B):
                pool.wait_ge(xs_ready, b + 1)
                pool.indirect_dma_start(rows_dram, bass.IndirectOffsetOnAxis(ap=slot_i[0:L, b:b + 1], axis=0),
                                        xs[0:L, b, :], None).then_inc(rows_out, 16)
            pool.wait_ge(rows_out, 16 * B)

            def load_rows(par, j):
                pool.dma_start(rows_in[par], rows_dram[bass.ds(j * P, P), :]).then_inc(rows_in_ready[par], 16)

            def store_rows(par, j):
                pool.wait_ge(ry_moved, LEAD + j + 1)
                pool.dma_start(out_dram[bass.ds(j * P, P), :], y_r[par]).then_inc(tile_out[par], 16)

            load_rows(0, 0)
            load_rows(1, 1)
            with pool.Fori(0, NT // 2 - 1) as i:
                pool.wait_ge(turned, LEAD + i * 2 + 1)
                load_rows(0, i * 2 + 2)
                pool.wait_ge(turned, LEAD + i * 2 + 2)
                load_rows(1, i * 2 + 3)
                store_rows(0, i * 2)
                store_rows(1, i * 2 + 1)
            store_rows(0, NT - 2)
            store_rows(1, NT - 1)
            for par in range(2):
                pool.wait_ge(tile_out[par], 16 * (NT // 2))
            for b in range(B):
                pool.indirect_dma_start(att[0:L, b, :], None, out_dram,
                                        bass.IndirectOffsetOnAxis(ap=slot_i[0:L, b:b + 1], axis=0)).then_inc(back_in[b], 16)


def _constants():
    f = np.float32
    p = np.arange(P)
    small = np.zeros((P, 64), f)
    small[:, 0:8] = (p[:, None] % B == np.arange(B))
    small[:, 8:12] = (p[:, None] // 32 == np.arange(4))
    small[:, 16:32] = (p[:, None] // B == np.arange(N))
    small[:, 32:48] = NS_A * small[:, 16:32]
    mask_row, max_row = p % 32 == DK, p % 32 == DK + 1
    small[:, 48] = np.where(mask_row, NEG, np.where(max_row, 0.0, 1.0))
    small[:, 49] = np.where(mask_row, -NEG, np.where(max_row, 1.0, 0.0))
    small[:, 50] = EPS
    small[:, 52:60] = E - np.arange(E)
    route = np.zeros((P, 112), f)
    route[:, 96:96 + NT] = E ** (np.arange(NT) // 2)
    route[:, 0:64] = (np.arange(E)[None, :] < np.arange(E)[:, None]).reshape(-1)
    route[:, 64:72] = P * np.arange(E)
    route[:, 72:72 + NT] = np.arange(NT)
    gain = np.float64(BETA) ** -np.arange(L)
    block = (p[:, None] % B == p[None, :] % B).astype(f)
    used = p[:, None] % 32 < B
    row_of = 32 * (np.arange(C * B) // B) + np.arange(C * B) % B
    pick = np.concatenate([p[:, None] == row_of, p[:, None] == row_of + B], 1).astype(f)
    return {
        "c_ident": np.eye(P, dtype=f), "c_neg": -np.eye(P, dtype=f), "c_ones": np.ones((P, P), f),
        "c_block": block, "c_small": small, "c_bmask": block.reshape(P, N, B),
        "c_pick": pick, "c_spread": (used & (p[:, None] % 32 == p[None, :] % B)).astype(f),
        "c_tile": (used & (p[:, None] % 32 == np.arange(B))).astype(f),
        "c_route": route, "c_earlier": (p[:, None] < np.arange(L)).astype(f), "c_zero": np.zeros((NT * P, DM), f),
        "c_gain": np.broadcast_to(gain, (P, L)).astype(f),
    }


def _chunks(w, n=P):
    return w.reshape(-1, n, w.shape[-1]).transpose(1, 0, 2)


def _pad_heads(w):
    out = np.zeros((H, 32) + w.shape[1:], w.dtype)
    out[:, :DK] = w.reshape((H, DK) + w.shape[1:])
    return out.reshape((H * 32,) + w.shape[1:])


def _expert(gate, up, down):
    return np.concatenate([_chunks(w.T).reshape(P, -1) for w in (gate, up, down)], axis=1)


def kernel(**inputs):
    import concourse.bacc as bacc
    from concourse.bass_utils import run_bass_kernel_spmd as run

    i = {k.replace("L0_", ""): np.asarray(a) for k, a in inputs.items()}
    x = i["x"]
    xp = i["attn_x_proj_w"]
    bq, bk = _pad_heads(i["xattn_bq"]), _pad_heads(i["xattn_bk"])
    bq.reshape(H, 32)[:, DK] = DK ** 0.5
    bk.reshape(H, 32)[:, DK] = 1.0
    bk.reshape(H, 32)[:, DK + 1] = 1.0
    arrays = {
        "x": x,
        "xt": _chunks(x.transpose(2, 1, 0).reshape(DM, T)),
        "w_in": _chunks(i["attn_in_proj_w"].T),
        "conv_w": _chunks(i["attn_conv_w"].reshape(DI, W)),
        "vecs": np.stack([i[k].reshape(C, P).T for k in ("attn_conv_b", "attn_dt_head_b", "attn_D")], 1),
        "w_lo": _chunks(xp[0:R].T),
        "w_k": _chunks(np.repeat(xp[R:R + N].T, B, axis=1)),
        "w_q": _chunks(np.repeat(xp[R + N:].T, B, axis=1)),
        "w_dt": i["attn_dt_head_w"].T,
        "w_out": _chunks(i["attn_out_proj_w"].T),
        "bias_qk": np.stack([bq.reshape(4, P).T, bk.reshape(4, P).T], 1),
        "bias_rows": np.broadcast_to(np.stack([i["xattn_bv"], i["xattn_bo"]]), (P, 2, DM)),
        "wq": _chunks(_pad_heads(i["xattn_Wq"]).T),
        "wk": _chunks(_pad_heads(i["xattn_Wk"]).T),
        "wv": _chunks(i["xattn_Wv"].T),
        "wo": _chunks(i["xattn_Wo"].T),
        "w_gate": _chunks(i["ffn_gate_w"].T),
        "ctx_t": i["ctx_1024"].transpose(0, 2, 1).reshape(B, MC, P, S2).transpose(0, 2, 1, 3),
        "mask": i["mask_Bx1xS2_ik0"].reshape(B, S2),
        "w_shared": _expert(i["ffn_shared_gate"], i["ffn_shared_up"], i["ffn_shared_down"]),
        "w_r": np.stack([_expert(*w) for w in zip(i["ffn_r_gate"], i["ffn_r_up"], i["ffn_r_down"])]),
        **_constants(),
    }
    nc = bacc.Bacc("TRN2", target_bir_lowering=False, num_devices=1)
    sent, io = {}, {}
    for name, a in arrays.items():
        a = np.ascontiguousarray(a)
        sent[f"in_{name}"] = a
        io[name] = nc.dram_tensor(f"in_{name}", a.shape, mybir.dt.from_np(a.dtype), kind="ExternalInput").ap()
    out = nc.dram_tensor("out_0", (B, L, DM), F32, kind="ExternalOutput").ap()
    decoder_kernel(nc, io, out)
    r = run(nc, [sent], core_ids=[0])
    return r.results[0]["out_0"]
```

```python
import numpy as np

import concourse.bass as bass
from concourse import mybir
from contextlib import ExitStack

B, L, DM = 8, 112, 256
DI, N, R, W = 512, 16, 64, 4
S2 = 375
H, DK = 16, 16
F, E = 512, 8
P = 128
C = DI // P
MC = DM // P
T = B * L
HT = T // 2
HL = L // 2
BN = B * N
KC = 3
KW = S2 // KC
NT = (T + E * (P - 1)) // P
EW = MC * 2 * F + C * DM
LP = L + 2
BETA = 0.9
NS_A, NS_B, NS_C = 3.4445, -4.775, 2.0315
ARENA = 21504
TURN = 8
LEAD = 2
NEG = 1e9
TINY = 1e-7
EPS = 1e-5

F32 = mybir.dt.float32
I32 = mybir.dt.int32
ALU = mybir.AluOpType
ACT = mybir.ActivationFunctionType
AX = mybir.AxisListType


def spread(ap, axis, n):
    a = ap.unsqueeze(axis)
    shape = list(a.shape)
    shape[axis] = n
    return a.broadcast_to(shape)


def decoder_kernel(nc, io, out):
    with ExitStack() as ctx:
        def sb(name, shape, dt=F32):
            return ctx.enter_context(nc.sbuf_tensor(name, shape, dt))

        def sem(name):
            return ctx.enter_context(nc.semaphore(name))

        bank = [ctx.enter_context(nc.psum_tensor(f"bank{i}", [P, 512], F32)) for i in range(8)]

        ident = sb("ident", [P, P])
        neg_ident = sb("neg_ident", [P, P])
        ones = sb("ones", [P, P])
        block_ones = sb("block_ones", [P, P])
        block_mask = sb("block_mask", [P, N, B])
        pick = sb("pick", [P, 2 * C * B])
        spread_u = sb("spread_u", [P, P])
        tile_mask = sb("tile_mask", [P, B])
        small = sb("small", [P, 64])
        batch_mask = small[:, 0:8]
        col_mask, scaled_eye = small[:, 16:32], small[:, 32:48]
        mask_gain, mask_base, eps_ln = small[:, 48:49], small[:, 49:50], small[:, 50:51]
        tie_rank = small[:, 52:60]
        head_rows = small[:, 8:12]
        step_gain = sb("step_gain", [P, L])

        conv_w = sb("conv_w", [P, C, W])
        vecs = sb("vecs", [P, 3, C])
        bias_qk = sb("bias_qk", [P, 2, 4])
        bias_rows = sb("bias_rows", [P, 2, DM])
        w_out = sb("w_out", [P, C, DM])

        tables = sb("tables", [P, E * EW])
        t_at = [0]

        def table(t, *dims):
            n = int(np.prod(dims))
            t_at[0] += t * n
            flat = tables[:, t_at[0] - t * n:t_at[0]]
            if len(dims) == 2:
                return flat.rearrange("p (t c b) -> p t c b", t=t, c=dims[0])
            return flat.rearrange("p (t n) -> p t n", t=t)

        y_a = table(LP, C, B)
        x_a = table(LP, C, B)
        z_a = table(L, C, B)
        kq = table(LP, 2 * B)
        assert t_at[0] >= E // 2 * EW
        eps_a = table(L, C, B)
        k_col = sb("k_col", [P, L])
        ks_col = sb("ks_col", [P, L])
        at_rec = [0]

        def field(n):
            at_rec[0] += n
            return slice(at_rec[0] - n, at_rec[0])

        MASKS = N
        F_COL, F_TRACE, F_ROW, F_NEXT = field(1), field(N + 1), field(N), field(N)
        F_AK, F_TINY, F_KQ = field(1), field(1), field(2 * B)
        REC = at_rec[0]
        rec = table(L, REC)
        assert t_at[0] <= E * EW
        now_all = [sb(f"now{i}", [P, MASKS + REC + 2 * B]) for i in range(2)]
        now = [x[:, MASKS:] for x in now_all]
        arena = sb("arena", [P, ARENA])
        ks_all = arena[:, 0:L * BN].rearrange("p (t n) -> p t n", t=L)

        m_g = sb("m_g", [P, C, N + 1, B])
        m_b = sb("m_b", [P, C, P])
        s_b = sb("s_b", [P, C, P])
        outer = sb("outer", [P, C, BN])
        g_a = m_g[:, :, N, :]
        m_a = [m_g[:, c, 0:N, :].rearrange("p n b -> p (n b)") for c in range(C)]
        eps = sb("eps", [P, C * B])
        y_now = sb("y_now", [P, C, B])
        e_c = sb("e_c", [P, P])
        mg_m = sb("mg_m", [P, N + 1, B])
        u_row = sb("u_row", [P, N + 1])
        gram = sb("gram", [P, N])
        gram1 = sb("gram1", [P, N])
        gram_bd = sb("gram_bd", [P, N, B])
        poly = sb("poly", [P, N])
        ns_p = sb("ns_p", [P, N])
        p_bd = sb("p_bd", [P, N, B])
        w_bd = sb("w_bd", [P, B])
        junk = sb("junk", [P, N + 1])
        junk2 = sb("junk2", [P, N + 1])
        junk3 = sb("junk3", [P, N])
        junk4 = sb("junk4", [P, N])
        cols = sb("cols", [P, 16])
        v_col, w_col, trace = cols[:, 1:2], cols[:, 2:3], cols[:, 3:4]
        dummy, gk_col, ak_col, r4 = (cols[:, i:i + 1] for i in (11, 10, 13, 14))
        root, norm, rneg, r2b, r2c, trace1 = (cols[:, i:i + 1] for i in range(4, 10))

        ks_dram = nc.dram_tensor("ks_dram", [L, BN], F32, kind="Internal").ap()

        at = [0]

        def take(n):
            at[0] += n
            assert at[0] <= ARENA, at[0]
            return arena[:, at[0] - n:at[0]]

        xt = take(MC * T).rearrange("p (m t) -> p m t", m=MC)
        w_in = take(MC * 2 * DI).rearrange("p (m e) -> p m e", m=MC)
        x_in = take(C * (L + W - 1) * B).rearrange("p (c t b) -> p c t b", c=C, b=B)
        conv = take(2 * T).rearrange("p (u t) -> p u t", u=2)
        w_dt_lo = take(C * R).rearrange("p (c r) -> p c r", c=C)
        w_k = take(C * BN).rearrange("p (c n) -> p c n", c=C)
        w_q = take(C * BN).rearrange("p (c n) -> p c n", c=C)
        at[0] = L * BN
        dt_lo = take(T)[0:R, :]
        k_sq = take(L * B).rearrange("p (t b) -> p t b", b=B)
        kd_row = take(L * N).rearrange("p (t n) -> p t n", n=N)
        late = 3 * (L // 4) * BN
        sp_e = [take(HL * C * B), arena[:, late:late + HL * C * B]]
        sp_l = [take(HL * C * B), arena[:, late + HL * C * B:late + 2 * HL * C * B]]
        w_dt = outer[0:R, :, :].rearrange("p c n -> p (c n)")
        ks_t = e_c[0:L, :]
        y_flat = y_a.rearrange("p t c b -> p (t c b)")
        den_flat = eps_a.rearrange("p t c b -> p (t c b)")
        half = HL * C * B
        sp_a_of = [y_flat[:, i * half:(i + 1) * half] for i in range(2)]
        sp_u_of = [den_flat[:, i * half:(i + 1) * half] for i in range(2)]

        at[0] = L * BN
        wo = take(MC * DM).rearrange("p (m e) -> p m e", m=MC)
        w_gate = take(MC * E).rearrange("p (m e) -> p m e", m=MC)
        xb = take(B * DM).rearrange("p (b d) -> p b d", b=B)
        shared_at = at[0]
        wq = take(MC * 512).rearrange("p (m e) -> p m e", m=MC)
        wk = take(MC * 512).rearrange("p (m e) -> p m e", m=MC)
        wv = take(MC * DM).rearrange("p (m e) -> p m e", m=MC)
        ctx_t = [take(MC * S2).rearrange("p (m s) -> p m s", m=MC) for _ in range(2)]
        stat = take(168)
        row_inv = take(H)
        at[0] = 0
        prob_at = take(MC * T + 2 * HT + 2 * DM)
        prob_t = [prob_at[:, i * KC * 4 * L:(i + 1) * KC * 4 * L].rearrange("p (k q) -> p k q", k=KC) for i in range(2)]
        x1t = take(MC * T).rearrange("p (m t) -> p m t", m=MC)
        x1 = take(B * DM).rearrange("p (b d) -> p b d", b=B)
        att = take(B * DM).rearrange("p (b d) -> p b d", b=B)
        h1 = take(B * DM).rearrange("p (b d) -> p b d", b=B)
        hid_at = at[0] - B * DM
        q_bd = [take(4 * L).rearrange("p (h q) -> p h q", h=4) for _ in range(2)]
        prob = [take(S2) for _ in range(4)]
        row_max = [take(4) for _ in range(2)]
        o_raw = take(4 * L).rearrange("p (g q) -> p g q", g=4)
        assert at[0] <= L * BN
        rec_flat = rec[:, :, :].rearrange("p t f -> p (t f)")
        k_t = [rec_flat[:, i * 4 * S2:(i + 1) * 4 * S2].rearrange("p (g s) -> p g s", g=4) for i in range(2)]
        v_at, v_n = 2 * 4 * S2, KC * H * 32
        v_t = [rec_flat[:, v_at + i * v_n:v_at + (i + 1) * v_n].rearrange("p (k h e) -> p k h e", k=KC, h=H) for i in range(2)]
        mask_f = rec_flat[:, v_at + 2 * v_n:v_at + 2 * v_n + S2]
        q_s = eps_a[:, :, :, :].rearrange("p t c b -> p (t c b)").rearrange("p (g t) -> p g t", g=4)
        mask_i = [sb(f"mask_i{i}", [P, S2], I32) for i in range(2)]
        q_bias = small[:, 60:64]
        x2 = xb
        at_t = x1t
        x2t = arena[:, 0:MC * T].rearrange("p (m t) -> p m t", m=MC)
        xs = att
        acc = x1
        lg, top_logit, top_rank = stat[:, 96:160].rearrange("p (b e) -> p b e", b=B), stat[:, 80:88], stat[:, 88:96]
        score = stat[:, 72:80]
        onehot = sb("onehot", [P, B, E])
        shared = arena[:, shared_at:shared_at + EW]
        wg = shared[:, 0:MC * F].rearrange("p (m f) -> p m f", m=MC)
        wu = shared[:, MC * F:2 * MC * F].rearrange("p (m f) -> p m f", m=MC)
        wd = shared[:, 2 * MC * F:EW].rearrange("p (c d) -> p c d", c=C)
        hid = arena[:, hid_at:hid_at + C * T].rearrange("p (c t) -> p c t", c=C)
        gate = arena[:, MC * T:MC * T + 2 * HT].rearrange("p (u t) -> p u t", u=2)
        w_r = tables[:, :].rearrange("p (e w f) -> p e w f", e=E, f=F)
        rows_in = [arena[:, MC * T + 2 * HT + i * DM:MC * T + 2 * HT + (i + 1) * DM] for i in range(2)]
        x1t_flat = x1t.rearrange("p m t -> p (m t)")
        rows_t = [x1t_flat[:, i * DM:(i + 1) * DM] for i in range(2)]
        hid_t = [x1t_flat[:, 2 * DM + i * F:2 * DM + (i + 1) * F] for i in range(2)]
        silu_r = [m_b[:, :, :].rearrange("p c n -> p (c n)"), s_b[:, :, :].rearrange("p c n -> p (c n)")]
        hid_r = [outer[:, :, :].rearrange("p c n -> p (c n)"), w_out[:, 0:2, :].rearrange("p c n -> p (c n)")]
        y_r = [w_out[:, 2, :], w_out[:, 3, :]]
        route_c = sb("route_c", [P, 112])
        before_e, tile_start, tile_no, digit = (route_c[:, 0:64], route_c[:, 64:72], route_c[:, 72:72 + NT],
                                                route_c[:, 96:96 + NT])
        earlier = sb("earlier", [P, L])
        route = arena[:, hid_at + C * T:hid_at + C * T + 512]
        r_tot, r_pre, r_pos = route[:, 0:64], route[:, 64:128], route[:, 128:192]
        r_cmp, r_tri = route[:, 192:256], route[:, 256:320]
        r_end_cmp = route[:, 320:320 + NT * E]
        r_cnt, r_tiles, r_base, r_end, r_slot = (route[:, 432 + 8 * i:440 + 8 * i] for i in range(5))
        r_tile = route[:, 472:472 + NT]
        slot_i = sb("slot_i", [P, B], I32)
        expert_i = sb("expert_i", [P, 2], I32)
        rows_dram = nc.dram_tensor("rows_dram", [NT * P, DM], F32, kind="Internal").ap()
        out_dram = nc.dram_tensor("out_dram", [NT * P, DM], F32, kind="Internal").ap()

        const_in, pre_in, k_out, ks_in = sem("const_in"), sem("pre_in"), sem("k_out"), [sem("ks_in_first"), sem("ks_in_rest")]
        zeroed = sem("zeroed")
        xz_ready, x_moved, z_done = sem("xz_ready"), sem("x_moved"), sem("z_done")
        conv_step, x_ready = sem("conv_step"), sem("x_ready")
        lo_ready, lo_moved = sem("lo_ready"), sem("lo_moved")
        kq_ready, kq_moved = sem("kq_ready"), sem("kq_moved")
        dt_ready, sp_act, sp_dve = sem("dt_ready"), sem("sp_act"), sem("sp_dve")
        tab, row_done, row_moved = sem("tab"), sem("row_done"), sem("row_moved")
        kt_ready, kt_moved, sq_ready, sq_moved = sem("kt_ready"), sem("kt_moved"), sem("sq_ready"), sem("sq_moved")
        base_ready, err_ready, g_ready, y_saved = sem("base_ready"), sem("err_ready"), sem("g_ready"), sem("y_saved")
        e_copied, a_ready, mgm_ready = sem("e_copied"), sem("a_ready"), sem("mgm_ready")
        mg_ready, ur_ready, v_ready = sem("mg_ready"), sem("ur_ready"), sem("v_ready")
        trace1_ready, gram1_ready, spread_ready = sem("trace1_ready"), sem("gram1_ready"), sem("spread_ready")
        trace_ready, gram_ready, bd_ready = sem("trace_ready"), sem("gram_ready"), sem("bd_ready")
        root_ready, gram2_ready, norm_ready = sem("root_ready"), sem("gram2_ready"), sem("norm_ready")
        rneg_ready, gk_ready, r2b_ready, r2c_ready = sem("rneg_ready"), sem("gk_ready"), sem("r2b_ready"), sem("r2c_ready")
        ak_ready, r4_ready = sem("ak_ready"), sem("r4_ready")
        poly_ready, p_ready, w_ready, wbd_ready = sem("poly_ready"), sem("p_ready"), sem("w_ready"), sem("wbd_ready")
        pbd_ready, outer_ready, ma_ready = sem("pbd_ready"), sem("outer_ready"), sem("ma_ready")
        mt_ready, mb_ready, s_ready, sb_ready = sem("mt_ready"), sem("mb_ready"), sem("s_ready"), sem("sb_ready")
        now_ready, ma0_ready = sem("now_ready"), sem("ma0_ready")
        recip_ready, eps_ready = sem("recip_ready"), sem("eps_ready")
        dx_ready, ydx_ready, gated = sem("dx_ready"), sem("ydx_ready"), sem("gated")
        att_in, ctx_in = sem("att_in"), [sem("ctx_in0"), sem("ctx_in1")]
        proj_ready, qb_ready = sem("proj_ready"), sem("qb_ready")
        h1_ready, h2_ready, ln, std_ready, x1_ready = sem("h1_ready"), sem("h2_ready"), sem("ln"), sem("std_ready"), sem("x1_ready")
        x1b_ready, x1t_ready, x1t_moved, x1t_copied = sem("x1b_ready"), sem("x1t_ready"), sem("x1t_moved"), sem("x1t_copied")
        kp_ready, kp_moved, vp_ready, vp_moved = sem("kp_ready"), sem("kp_moved"), sem("vp_ready"), sem("vp_moved")
        qp_ready, q_moved, q_copied, msk = sem("qp_ready"), sem("q_moved"), sem("q_copied"), sem("msk")
        qbd_ready, sc_ready, max_ready = sem("qbd_ready"), sem("sc_ready"), sem("max_ready")
        exp_ready, pt_ready, pt_moved, pt_copied = sem("exp_ready"), sem("pt_ready"), sem("pt_moved"), sem("pt_copied")
        pv_ready, o_copied, ot_ready, inv_ready, att_ready = sem("pv_ready"), sem("o_copied"), sem("ot_ready"), sem("inv_ready"), sem("att_ready")
        cleared = sem("cleared")
        att_t_ready, att_moved, att_copied = sem("att_t_ready"), sem("att_moved"), sem("att_copied")
        wo_ready, x2_ready, x2t_ready, x2t_moved, x2t_copied = sem("wo_ready"), sem("x2_ready"), sem("x2t_ready"), sem("x2t_moved"), sem("x2t_copied")
        lg_ready, top, score_ready, xs_ready = sem("lg_ready"), sem("top"), sem("score_ready"), sem("xs_ready")
        shared_in, routed_in, rows_zero, rows_out = sem("shared_in"), sem("routed_in"), sem("rows_zero"), sem("rows_out")
        count_ready, route_step, route_ready = sem("count_ready"), sem("route_step"), sem("route_ready")
        gate_ready, up_ready, silu_ready, hid_ready = sem("gate_ready"), sem("up_ready"), sem("silu_ready"), sem("hid_ready")
        down_ready, acc_ready = sem("down_ready"), sem("acc_ready")
        rows_in_ready = [sem("rows_in0"), sem("rows_in1")]
        turned, turned_moved, rg_ready, ru_ready = sem("turned"), sem("turned_moved"), sem("rg_ready"), sem("ru_ready")
        rsilu_ready, rhid_ready, rht_ready, rht_moved = sem("rsilu_ready"), sem("rhid_ready"), sem("rht_ready"), sem("rht_moved")
        ry_ready, ry_moved, tile_out, back_in = sem("ry_ready"), sem("ry_moved"), [sem("tile_out0"), sem("tile_out1")], [sem(f"back_in{b}") for b in range(B)]
        stats_ready, var_ready, inv_std_ready = sem("stats_ready"), sem("var_ready"), sem("inv_std_ready")
        sum_ready, y_ready, y_out = sem("sum_ready"), sem("y_ready"), sem("y_out")

        block = ctx.enter_context(nc.Block())

        @block.sync
        def _(sp):
            for s in (mb_ready, wbd_ready, pbd_ready, sb_ready, y_saved, w_ready, ma0_ready, gated,
                      kp_ready, kp_moved, vp_ready, vp_moved, msk, qbd_ready, sc_ready, max_ready,
                      pt_ready, pt_moved, pt_copied, exp_ready, pv_ready, o_copied, ot_ready, inv_ready, att_ready,
                      turned, turned_moved, rsilu_ready, rhid_ready, rht_ready, rht_moved, ry_ready, ry_moved,
                      rg_ready, ru_ready):
                sp.sem_inc(s, LEAD)
            for dst, name in ((xt, "xt"), (w_in, "w_in"), (conv_w[:, :, :], "conv_w"), (vecs[:, :, :], "vecs")):
                sp.dma_start(dst, io[name]).then_inc(pre_in, 16)
            for dst, name in ((w_dt_lo, "w_lo"), (w_k, "w_k"), (w_q, "w_q"), (w_dt, "w_dt"), (small[:, :], "c_small"),
                              (ident[:, :], "c_ident"), (step_gain[:, :], "c_gain"), (ones[:, :], "c_ones"),
                              (block_ones[:, :], "c_block"), (neg_ident[:, :], "c_neg"),
                              (block_mask[:, :, :], "c_bmask"), (pick[:, :], "c_pick"), (spread_u[:, :], "c_spread"),
                              (tile_mask[:, :], "c_tile"), (w_out[:, :, :], "w_out"), (bias_qk[:, :, :], "bias_qk"),
                              (bias_rows[:, :, :], "bias_rows")):
                sp.dma_start(dst, io[name]).then_inc(const_in, 16)
            sp.wait_ge(kt_moved, 1)
            sp.dma_start(ks_dram, ks_t).then_inc(k_out, 16)
            sp.wait_ge(k_out, 16)
            sp.wait_ge(xz_ready, 4 * C)
            sp.wait_ge(conv_step, C * W)
            sp.wait_ge(x_ready, C)
            sp.wait_ge(kq_ready, 4)
            n = L // 4
            for q in range(4):
                if q == 3:
                    sp.wait_ge(sp_dve, 2 * 5)
                sp.dma_start(ks_all[:, q * n:(q + 1) * n, :],
                             ks_dram[q * n:(q + 1) * n, :].partition_broadcast(P)).then_inc(ks_in[min(q, 1)], 16)
            sp.wait_ge(row_moved, 4)
            sp.wait_ge(sq_moved, 2)
            sp.wait_ge(tab, 8)
            sp.wait_ge(dt_ready, 2 * C)
            sp.dma_start(route_c[:, :], io["c_route"]).then_inc(att_in, 16)
            sp.dma_start(earlier[:, :], io["c_earlier"]).then_inc(att_in, 16)
            sp.dma_start(rows_dram, io["c_zero"]).then_inc(rows_zero, 16)
            for dst, name in ((wq, "wq"), (wk, "wk"), (wv, "wv"), (wo, "wo"), (w_gate, "w_gate")):
                sp.dma_start(dst, io[name]).then_inc(att_in, 16)
            sp.dma_start(xb[0:L], io["x"].rearrange("b t d -> t b d")).then_inc(att_in, 16)
            for b in range(2):
                sp.dma_start(ctx_t[b], io["ctx_t"][b]).then_inc(ctx_in[b], 16)
                sp.dma_start(mask_i[b][:, :], io["mask"][b].partition_broadcast(P)).then_inc(ctx_in[b], 16)
            sp.wait_ge(proj_ready, B)
            sp.wait_ge(gated, LEAD + L)
            for e in range(E // 2):
                sp.dma_start(tables[:, e * EW:(e + 1) * EW], io["w_r"][e]).then_inc(routed_in, 16)
            for b in range(2, B):
                sp.wait_ge(kp_ready, LEAD + (b - 1) * 4)
                sp.wait_ge(vp_ready, LEAD + (b - 1) * KC)
                sp.wait_ge(msk, LEAD + (b - 1) * 3)
                sp.dma_start(ctx_t[b % 2], io["ctx_t"][b]).then_inc(ctx_in[b % 2], 16)
                sp.dma_start(mask_i[b % 2][:, :], io["mask"][b].partition_broadcast(P)).then_inc(ctx_in[b % 2], 16)
            sp.wait_ge(kp_ready, LEAD + B * 4)
            sp.wait_ge(vp_ready, LEAD + B * KC)
            sp.dma_start(shared, io["w_shared"]).then_inc(shared_in, 16)
            sp.wait_ge(pv_ready, LEAD + B * 4)
            sp.wait_ge(sc_ready, LEAD + B * H)
            sp.wait_ge(qbd_ready, LEAD + B * 4)
            for e in range(E // 2, E):
                sp.dma_start(tables[:, e * EW:(e + 1) * EW], io["w_r"][e]).then_inc(routed_in, 16)
            for b in range(B):
                sp.wait_ge(y_ready, b + 1)
                sp.dma_start(out[b], h1[0:L, b, :]).then_inc(y_out, 16)
            sp.wait_ge(y_out, 16 * B)

        @block.tensor
        def _(pe):
            mm = nc.tensor.matmul

            def project(ec, hf):
                for m in range(MC):
                    last = mm(bank[(2 * ec + hf) % 4][:, 0:HT], w_in[:, m, ec * P:(ec + 1) * P],
                              xt[:, m, hf * HT:(hf + 1) * HT], start=(m == 0), stop=(m == MC - 1))
                last.then_inc(xz_ready, 1)

            pe.wait_ge(pre_in, 64)
            for ec in range(C):
                for hf in range(2):
                    if ec >= 2:
                        pe.wait_ge(x_moved, 2 * ec + hf - 3)
                    project(ec, hf)
            pe.wait_ge(const_in, 16 * 17)
            pe.wait_ge(x_ready, C)
            for hf in range(2):
                xs_h = x_a[:, hf * HL:(hf + 1) * HL]
                for c in range(C):
                    last = mm(bank[4 + hf][0:R, 0:HT], w_dt_lo[:, c, :], xs_h[:, :, c, :],
                              start=(c == 0), stop=(c == C - 1))
                last.then_inc(lo_ready, 1)
            for j, wt in enumerate((w_k, w_q)):
                for hf in range(2):
                    xs_h = x_a[:, hf * HL:(hf + 1) * HL]
                    if j == 1:
                        pe.wait_ge(kq_moved, hf + 1)
                    for c in range(C):
                        last = mm(bank[6 + hf][:, 0:HT], wt[:, c, :], xs_h[:, :, c, :],
                                  start=(c == 0), stop=(c == C - 1))
                    last.then_inc(kq_ready, 1)
            pe.wait_ge(lo_moved, 2)
            pe.wait_ge(x_moved, 2 * C)
            for hf in range(2):
                for c in range(C):
                    n = hf * C + c
                    if n >= 4:
                        pe.wait_ge(sp_act, n - 3)
                    mm(bank[c][:, 0:HT], w_dt[:, c * P:(c + 1) * P], dt_lo[:, hf * HT:(hf + 1) * HT],
                       start=True, stop=True).then_inc(dt_ready, 1)
            pe.wait_ge(tab, 3)
            nc.tensor.transpose(bank[4][0:L, 0:P], ks_col[:, :], ident[:, :]).then_inc(kt_ready, 1)
            pe.wait_ge(tab, 5)
            pe.wait_ge(kq_moved, 4)
            for hf in range(2):
                mm(bank[6 + hf][:, 0:HT], ones[:, :], k_sq[:, hf * HL:(hf + 1) * HL, :].rearrange("p t b -> p (t b)"),
                   start=True, stop=True).then_inc(sq_ready, 1)
            pe.wait_ge(tab, 6)
            for n in range(4):
                if n == 0:
                    pe.wait_ge(kt_moved, 1)
                if n >= 2:
                    pe.wait_ge(row_moved, n - 1)
                q = L // 4
                mm(bank[4 + n % 2][:, 0:q * N], block_ones[:, :],
                   kd_row[:, n * q:(n + 1) * q, :].rearrange("p t n -> p (t n)"),
                   start=True, stop=True).then_inc(row_done, 1)

            for ec in range(C, 2 * C):
                for hf in range(2):
                    n = 2 * (ec - C) + hf
                    if n < 4:
                        pe.wait_ge(sp_act, C + 1 + n)
                    else:
                        pe.wait_ge(z_done, n - 3)
                    project(ec, hf)

            e_bank, a_bank, mg_bank, sp_bank = bank[0], bank[1], bank[2], bank[4]
            g2_bank, st_bank, mt_bank = bank[5], bank[6], bank[7]
            flat_p = p_bd[:, :, :].rearrange("p n b -> p (n b)")

            def base_terms(kq_t):
                for c in range(C):
                    last = mm(e_bank[32 * c:32 * c + kq_t.shape[1], 0:P], kq_t, s_b[:, c, :], start=True, stop=False,
                              skip_group_check=True)
                last.then_inc(base_ready, 1)

            def minus_x(t):
                mm(a_bank[:, 0:C * B], neg_ident[:, :], x_a[:, bass.ds(t, 1)].rearrange("p o c b -> p (o c b)"),
                   start=True, stop=False, skip_group_check=True)

            def to_inner():
                mm(a_bank[:, 0:2 * C * B], e_c[:, :], pick[:, :], start=False, stop=True,
                   skip_group_check=True).then_inc(a_ready, 1)

            def s_update(cs):
                for c in cs:
                    last = mm(st_bank[:, c * P:(c + 1) * P], flat_p, m_b[:, c, :], start=False, stop=False,
                              skip_group_check=True)
                return last

            pe.wait_ge(zeroed, 12)
            pe.wait_ge(z_done, 2 * C)
            pe.wait_ge(row_moved, 4)
            pe.wait_ge(sq_moved, 2)
            pe.wait_ge(kt_moved, 1)
            zeros = m_b[:, :, :].rearrange("p c n -> p (c n)")
            mm(st_bank[:, :], flat_p, zeros, start=True, stop=False, skip_group_check=True)
            mm(e_bank[:, 0:P], flat_p, zeros[:, 0:P], start=True, stop=True, skip_group_check=True)
            mm(mg_bank[:, 0:P + B], flat_p, zeros[:, 0:P + B], start=True, stop=True, skip_group_check=True)
            base_terms(kq[:, 0, :])
            with pe.Fori(0, L // 2) as i:
                for par in range(2):
                    t = i * 2 + par
                    pe.wait_ge(mb_ready, LEAD + t)
                    pe.wait_ge(wbd_ready, LEAD + t)
                    for c in range(C):
                        last = mm(e_bank[32 * c:32 * c + B, 0:P], w_bd[:, :], m_b[:, c, :], start=False, stop=True,
                                  skip_group_check=True)
                    last.then_inc(err_ready, 1)
                    pe.wait_ge(y_saved, LEAD + t)
                    minus_x(t)
                    pe.wait_ge(e_copied, t + 1)
                    to_inner()
                    pe.wait_ge(pbd_ready, LEAD + t)
                    pe.wait_ge(sb_ready, LEAD + t)
                    s_update((0,))
                    pe.wait_ge(g_ready, t + 1)
                    for c in range(C):
                        last = mm(mg_bank[32 * c:32 * c + B, 0:P + B], m_g[:, c, N, :],
                                  m_g[:, c, :, :].rearrange("p n b -> p (n b)"), start=True, stop=True,
                                  skip_group_check=True)
                    last.then_inc(mg_ready, 1)
                    s_update((1, 2))
                    pe.wait_ge(ur_ready, t + 1)
                    mm(sp_bank[:, 0:N + 1], spread_u[:, :], u_row[:, :], start=True, stop=True).then_inc(spread_ready, 1)
                    s_update((3,)).then_inc(s_ready, 1)
                    def turn_m(c):
                        return nc.tensor.transpose(mt_bank[:, c * P:(c + 1) * P], m_a[c], ident[:, :])

                    pe.wait_ge(ma0_ready, LEAD + t + 1)
                    turn_m(0)
                    pe.wait_ge(ma_ready, t + 1)
                    for c in range(1, C - 1):
                        turn_m(c)
                    pe.wait_ge(bd_ready, t + 1)
                    mm(g2_bank[:, 0:N], gram_bd[:, :, :].rearrange("p n b -> p (n b)"), gram[:, :],
                       start=True, stop=True).then_inc(gram2_ready, 1)
                    turn_m(C - 1).then_inc(mt_ready, 1)
                    pe.wait_ge(sb_ready, LEAD + t + 1)
                    pe.wait_ge(now_ready, t + 1)
                    base_terms(now[par][:, F_KQ.start:F_KQ.start + 32])
            pe.wait_ge(mb_ready, LEAD + L)
            pe.wait_ge(pbd_ready, LEAD + L)
            pe.wait_ge(sb_ready, LEAD + L)
            s_update(range(C)).then_inc(s_ready, 1)
            pe.wait_ge(y_saved, LEAD + L)
            minus_x(L)
            pe.wait_ge(e_copied, L + 1)
            to_inner()
            pe.wait_ge(sb_ready, LEAD + L + 1)
            base_terms(kq[:, L + 1, :])
            pe.wait_ge(y_saved, LEAD + L + 1)
            minus_x(L + 1)
            pe.wait_ge(e_copied, L + 2)
            to_inner()

            def k_project(b, par, g, to):
                for m in range(MC):
                    last = mm(to[:, 0:S2], wk[:, m, g * P:(g + 1) * P], ctx_t[par][:, m, :], start=(m == 0), stop=(m == MC - 1))
                last.then_inc(kp_ready, 1)

            def v_project(b, par, k, to):
                for m in range(MC):
                    last = mm(to[0:KW, 0:DM], ctx_t[par][:, m, k * KW:(k + 1) * KW], wv[:, m, :],
                              start=(m == 0), stop=(m == MC - 1))
                last.then_inc(vp_ready, 1)

            def score(b, par, g, h):
                hh = 4 * g + h
                if h == 0:
                    pe.wait_ge(qbd_ready, LEAD + b * 4 + (g + 1))
                    pe.wait_ge(kp_moved, LEAD + b * 4 + (g + 1))
                pe.wait_ge(exp_ready, LEAD + b * H + max(hh - 2, 0))
                mm(bank[hh % 3][0:L, 0:S2], q_bd[g % 2][:, h, :], k_t[par][:, g, :],
                   start=True, stop=True).then_inc(sc_ready, 1)

            def turn_probs(b, g, h):
                pe.wait_ge(exp_ready, LEAD + b * H + (4 * g + h + 1))
                pe.wait_ge(pt_moved if h % 2 == 0 else pt_copied, LEAD + b * 8 + (2 * g + h // 2))
                for k in range(KC):
                    last = nc.tensor.transpose(bank[3 + h % 2][0:KW, k * L:(k + 1) * L],
                                               prob[h][0:L, k * KW:(k + 1) * KW], ident[0:L, 0:L])
                last.then_inc(pt_ready, 1)

            def values(b, par, g):
                pe.wait_ge(pt_moved, LEAD + b * 8 + 2 * (g + 1))
                pe.wait_ge(pt_copied, LEAD + b * 8 + 2 * (g + 1))
                pe.wait_ge(vp_moved, LEAD + b * KC + KC)
                if g == 0:
                    pe.wait_ge(o_copied, LEAD + b)
                for k in range(KC):
                    for h in range(4):
                        last = mm(bank[5][32 * h:32 * h + 32, g * L:(g + 1) * L], v_t[par][0:KW, k, 4 * g + h, :],
                                  prob_t[g % 2][0:KW, k, h * L:(h + 1) * L], start=(k == 0), stop=(k == KC - 1),
                                  skip_group_check=True)
                last.then_inc(pv_ready, 1)

            def turn_values(b):
                pe.wait_ge(o_copied, LEAD + b + 1)
                for g in range(4):
                    last = nc.tensor.transpose(bank[7][0:L, g * P:(g + 1) * P], o_raw[:, g, :], ident[:, :])
                last.then_inc(ot_ready, 1)

            def batch(b, par, loads, first=False, last=False):
                nxt = b + 1
                for g in range(4):
                    for h in range(4):
                        if g < 3:
                            score(b, par, g + 1, h)
                        elif not last:
                            score(nxt, 1 - par, 0, h)
                        turn_probs(b, g, h)
                        if h == 0 and not last:
                            pe.wait_ge(kp_moved, LEAD + nxt * 4 + g)
                            if g == 0:
                                pe.wait_ge(ctx_in[1 - par], loads * 32)
                            k_project(nxt, 1 - par, g, bank[6])
                        if h == 0 and g == 1 and not first:
                            pe.wait_ge(vp_moved, LEAD + b * KC + KC)
                            turn_values(b - 1)
                        if h == 1 and g > 0:
                            values(b, par, g - 1)
                        elif h == 1 and not first:
                            values(b - 1, 1 - par, 3)
                        if h == 2 and g > 0 and not last:
                            pe.wait_ge(att_ready, LEAD + b)
                            pe.wait_ge(vp_moved, LEAD + nxt * KC + (g - 1))
                            v_project(nxt, 1 - par, g - 1, bank[7])

            pe.wait_ge(y_saved, LEAD + LP)
            pe.wait_ge(att_in, 16 * 8)
            pe.wait_ge(ctx_in[0], 32)
            for g in range(4):
                k_project(0, 0, g, bank[4 + g])
            for k in range(KC):
                v_project(0, 0, k, bank[1 + k])
            pe.wait_ge(gated, LEAD + L)
            for b in range(B):
                if b % 2 == 0 and b > 0:
                    pe.wait_ge(vp_moved, LEAD + b // 2)
                for c in range(C):
                    last = mm(bank[b // 2][0:L, (b % 2) * DM:(b % 2 + 1) * DM], z_a[:, :, c, b], w_out[:, c, :],
                              start=(c == 0), stop=(c == C - 1))
                last.then_inc(proj_ready, 1)

            def turn_rows(src, ready, done, first_bank):
                for b in range(B):
                    if ready is not None:
                        pe.wait_ge(ready, b + 1)
                    for m in range(MC):
                        last = nc.tensor.transpose(bank[first_bank + 2 * m + b // 4][:, (b % 4) * L:(b % 4 + 1) * L],
                                                   src[0:L, b, m * P:(m + 1) * P], ident[0:L, 0:L])
                    last.then_inc(done, 1)

            pe.wait_ge(kp_moved, LEAD + 4)
            turn_rows(x1, x1_ready, x1t_ready, 4)
            for hf in range(2):
                pe.wait_ge(x1t_moved, hf + 1)
                pe.wait_ge(x1t_copied, hf + 1)
                for g in range(4):
                    for m in range(MC):
                        last = mm(bank[4 * hf + g][:, 0:HT], wq[:, m, g * P:(g + 1) * P], x1t[:, m, hf * HT:(hf + 1) * HT],
                                  start=(m == 0), stop=(m == MC - 1))
                    last.then_inc(qp_ready, 1)
            pe.wait_ge(q_moved, 4)
            pe.wait_ge(q_copied, 4)
            pe.wait_ge(cleared, 2)
            for h in range(4):
                score(0, 0, 0, h)
            batch(0, 0, 1, first=True)
            with pe.Fori(0, B // 2 - 1) as i:
                batch(i * 2 + 1, 1, i + 2)
                batch(i * 2 + 2, 0, i + 2)
            batch(B - 1, 1, None, last=True)
            values(B - 1, 1, 3)
            turn_values(B - 1)
            pe.wait_ge(att_ready, LEAD + B)
            turn_rows(att, None, att_t_ready, 0)
            pe.wait_ge(att_moved, 2)
            pe.wait_ge(att_copied, 2)
            for b in range(B):
                for m in range(MC):
                    last = mm(bank[4 + b // 2][0:L, (b % 2) * DM:(b % 2 + 1) * DM], at_t[:, m, b * L:(b + 1) * L], wo[:, m, :],
                              start=(m == 0), stop=(m == MC - 1))
                last.then_inc(wo_ready, 1)
            turn_rows(x2, x2_ready, x2t_ready, 0)
            pe.wait_ge(x2t_moved, 2)
            pe.wait_ge(x2t_copied, 2)
            for b in range(B):
                for m in range(MC):
                    last = mm(bank[4][0:L, b * E:(b + 1) * E], x2t[:, m, b * L:(b + 1) * L], w_gate[:, m, :],
                              start=(m == 0), stop=(m == MC - 1))
            last.then_inc(lg_ready, 1)
            pe.wait_ge(shared_in, 16)
            for f in range(C):
                for hf in range(2):
                    k = f * 2 + hf
                    if k >= 2:
                        pe.wait_ge(hid_ready, k - 1)
                    for weights, to, ready in ((wg, bank[k % 2], gate_ready), (wu, bank[2 + k % 2], up_ready)):
                        for m in range(MC):
                            last = mm(to[:, 0:HT], weights[:, m, f * P:(f + 1) * P],
                                      x2t[:, m, hf * HT:(hf + 1) * HT], start=(m == 0), stop=(m == MC - 1))
                        last.then_inc(ready, 1)
                        if k == 0 and ready is gate_ready:
                            pe.wait_ge(top, 5)
                            one_hot = onehot[0:L].rearrange("p b e -> p (b e)")
                            mm(bank[5][0:L, 0:B * E], earlier[0:L, :], one_hot, start=True, stop=True).then_inc(count_ready, 1)
                            mm(bank[6][:, 0:B * E], ones[0:L, :], one_hot, start=True, stop=True).then_inc(count_ready, 1)
            pe.wait_ge(route_ready, 1)
            for b in range(B):
                if b == 0:
                    pe.wait_ge(hid_ready, 7)
                if b == B // 2 - 1:
                    pe.wait_ge(hid_ready, 8)
                if b >= 2:
                    pe.wait_ge(acc_ready, b - 1)
                for c in range(C):
                    last = mm(bank[4 + b % 2][0:L, 0:DM], hid[:, c, b * L:(b + 1) * L], wd[:, c, :],
                              start=(c == 0), stop=(c == C - 1))
                last.then_inc(down_ready, 1)

            def turn_in(par, j, loads):
                pe.wait_ge(rows_in_ready[par], 16 * loads)
                pe.wait_ge(turned_moved, LEAD + j)
                for m in range(MC):
                    last = nc.tensor.transpose(bank[7][:, m * P:(m + 1) * P], rows_in[par][:, m * P:(m + 1) * P], ident[:, :])
                last.then_inc(turned, 1)

            def widen(par, turn, first_w, to, ready):
                e = (experts[par] >> (turn * 3)) & (E - 1)
                for m in range(MC):
                    last = mm(to[:, :], rows_t[par][:, m * P:(m + 1) * P],
                              w_r[:, bass.ds(e, 1), first_w + m, :].rearrange("p o f -> p (o f)"),
                              start=(m == 0), stop=(m == MC - 1))
                last.then_inc(ready, 1)

            def gates(par, j, turn):
                pe.wait_ge(turned_moved, LEAD + j + 1)
                pe.wait_ge(rhid_ready, LEAD + j - 1)
                widen(par, turn, 0, bank[par], rg_ready)

            def ups(par, turn):
                widen(par, turn, MC, bank[2 + par], ru_ready)

            def turn_hidden(par, j):
                pe.wait_ge(rhid_ready, LEAD + j + 1)
                pe.wait_ge(rht_moved, LEAD + j)
                for c in range(C):
                    last = nc.tensor.transpose(bank[4][:, c * P:(c + 1) * P], hid_r[par][:, c * P:(c + 1) * P], ident[:, :])
                last.then_inc(rht_ready, 1)

            def down(par, j, turn):
                pe.wait_ge(rht_moved, LEAD + j + 1)
                pe.wait_ge(ry_moved, LEAD + j - 1)
                e = (experts[par] >> (turn * 3)) & (E - 1)
                for c in range(C):
                    last = mm(bank[5 + par][:, 0:DM], hid_t[par][:, c * P:(c + 1) * P],
                              w_r[:, bass.ds(e, 1), 2 * MC + c // 2, (c % 2) * DM:(c % 2 + 1) * DM].rearrange("p o f -> p (o f)"),
                              start=(c == 0), stop=(c == C - 1))
                last.then_inc(ry_ready, 1)

            def tile(par, j, turn, loads):
                gates(par, j, turn)
                turn_hidden(1 - par, j - 1)
                ups(par, turn)
                turn_in(1 - par, j + 1, loads)
                down(1 - par, j - 1, turn if par == 1 else turn - 1)

            pe.wait_ge(acc_ready, B)
            turn_in(0, 0, 1)
            pe.wait_ge(routed_in, 16 * E)
            pe.wait_ge(route_ready, 2)
            experts = [pe.value_load(expert_i[0:1, u:u + 1], min_val=0, max_val=E ** (NT // 2) - 1) for u in range(2)]
            gates(0, 0, 0)
            ups(0, 0)
            turn_in(1, 1, 1)
            with pe.Fori(0, NT // 2 - 1) as i:
                tile(1, i * 2 + 1, i, i + 2)
                tile(0, i * 2 + 2, i + 1, i + 2)
            gates(1, NT - 1, NT // 2 - 1)
            turn_hidden(0, NT - 2)
            ups(1, NT // 2 - 1)
            down(0, NT - 2, NT // 2 - 1)
            turn_hidden(1, NT - 1)
            down(1, NT - 1, NT // 2 - 1)

        @block.vector
        def _(dve):
            v = nc.vector
            v.memset(x_in[:, :, 0:W - 1, :], 0.0).then_inc(zeroed, 1)
            v.memset(x_a[:, L:LP], 0.0).then_inc(zeroed, 1)
            v.memset(kq[:, L:LP, 0:B], 0.0).then_inc(zeroed, 1)
            v.memset(kq[:, 0:2, B:2 * B], 0.0).then_inc(zeroed, 1)
            v.memset(rec[:, L - 1, F_NEXT.start:F_TINY.start], 0.0).then_inc(zeroed, 1)
            v.memset(m_g[:, :, :, :], 0.0).then_inc(zeroed, 1)
            v.memset(m_b[:, :, :], 0.0).then_inc(zeroed, 1)
            v.memset(s_b[:, :, :], 0.0).then_inc(zeroed, 1)
            v.memset(gram[:, :], 0.0).then_inc(zeroed, 1)
            v.memset(p_bd[:, :, :], 0.0).then_inc(zeroed, 1)
            for buf in now:
                v.memset(buf[:, REC:], 0.0)
            v.memset(w_bd[:, :], 0.0).then_inc(zeroed, 1)
            v.memset(cols[:, :], 0.0).then_inc(zeroed, 1)
            dve.wait_ge(zeroed, 12)
            dve.wait_ge(pre_in, 64)
            for c in range(C):
                for hf in range(2):
                    n = c * 2 + hf
                    dve.wait_ge(xz_ready, n + 1)
                    v.tensor_copy(x_in[:, c, W - 1 + hf * HL:W - 1 + (hf + 1) * HL, :].rearrange("p t b -> p (t b)"),
                                  bank[n % 4][:, 0:HT]).then_inc(x_moved, 1)
                dve.wait_ge(x_moved, 2 * c + 2)
                if c >= 2:
                    dve.wait_ge(x_ready, c - 1)
                acc_c = conv[:, c % 2, :]
                for w in range(W):
                    win = x_in[:, c, w:w + L, :].rearrange("p t b -> p (t b)")
                    if w == 0:
                        ins = v.tensor_scalar(acc_c, win, conv_w[:, c, 0:1], None, ALU.mult)
                    else:
                        dve.wait_ge(conv_step, c * W + w)
                        ins = v.scalar_tensor_tensor(acc_c, win, conv_w[:, c, w:w + 1], acc_c, ALU.mult, ALU.add)
                    ins.then_inc(conv_step, 1)
            dve.wait_ge(const_in, 16 * 17)
            for hf in range(2):
                dve.wait_ge(lo_ready, hf + 1)
                v.tensor_copy(dt_lo[:, hf * HT:(hf + 1) * HT], bank[4 + hf][0:R, 0:HT]).then_inc(lo_moved, 1)
            for j in range(2):
                for hf in range(2):
                    dve.wait_ge(kq_ready, j * 2 + hf + 1)
                    t0 = hf * HL + 2 * j
                    v.tensor_tensor(kq[:, t0:t0 + HL, j * B:(j + 1) * B],
                                    bank[6 + hf][:, 0:HT].rearrange("p (t b) -> p t b", b=B),
                                    spread(batch_mask, 1, HL), ALU.mult).then_inc(kq_moved, 1)
            dve.wait_ge(kq_moved, 4)
            v.tensor_reduce(k_col[:, :], kq[:, 0:L, 0:B], AX.X, ALU.add).then_inc(tab, 1)
            dve.wait_ge(tab, 1)
            v.tensor_tensor(ks_col[:, :], k_col[:, :], step_gain[:, :], ALU.mult).then_inc(tab, 1)
            dve.wait_ge(tab, 2)
            v.tensor_copy(rec[:, :, F_KQ], kq[:, 1:L + 1, :]).then_inc(tab, 1)
            v.tensor_copy(rec[:, :, F_COL.start], ks_col[:, :]).then_inc(tab, 1)
            for buf in now_all:
                v.tensor_copy(buf[:, 0:MASKS], col_mask)
            v.tensor_scalar(rec[:, 0:L - 1, F_AK.start], k_col[:, 1:L], NS_A, None, ALU.mult)
            v.tensor_tensor(k_sq, kq[:, 0:L, 0:B], kq[:, 0:L, 0:B], ALU.mult).then_inc(tab, 1)
            v.tensor_tensor(kd_row, spread(col_mask, 1, L), spread(k_col[:, :], 2, N), ALU.mult).then_inc(tab, 1)
            dve.wait_ge(kt_ready, 1)
            v.tensor_copy(ks_t, bank[4][0:L, 0:P]).then_inc(kt_moved, 1)
            for hf in range(2):
                dve.wait_ge(sq_ready, hf + 1)
                v.tensor_copy(k_sq[:, hf * HL:(hf + 1) * HL, :].rearrange("p t b -> p (t b)"),
                              bank[6 + hf][:, 0:HT]).then_inc(sq_moved, 1)
            for n in range(4):
                q = L // 4
                dve.wait_ge(row_done, n + 1)
                row = bank[4 + n % 2][:, 0:q * N].rearrange("p (t n) -> p t n", n=N)
                skip = 1 if n == 0 else 0
                v.tensor_copy(rec[:, n * q + skip - 1:(n + 1) * q - 1, F_NEXT], row[:, skip:, :])
                v.tensor_tensor(rec[:, n * q:(n + 1) * q, F_ROW], row,
                                spread(step_gain[:, n * q:(n + 1) * q], 2, N), ALU.mult).then_inc(row_moved, 1)
            dve.wait_ge(row_moved, 4)
            v.tensor_scalar(rec[:, :, F_TRACE.start:F_TRACE.stop - 1], rec[:, :, F_ROW], 2.0, None, ALU.mult)
            for hf in range(2):
                dve.wait_ge(sp_act, 2 * C + 3 + hf)
                v.tensor_scalar(sp_u_of[hf], sp_e[hf], 1.0, None, ALU.add).then_inc(sp_dve, 1)
            v.tensor_tensor(kd_row, rec[:, :, F_ROW], rec[:, :, F_ROW], ALU.mult).then_inc(tab, 1)
            dve.wait_ge(tab, 7)
            v.tensor_reduce(rec[:, :, F_TRACE.stop - 1], kd_row, AX.X, ALU.add)
            v.tensor_scalar(rec[:, :, F_TINY.start], step_gain[:, :], TINY, None, ALU.mult).then_inc(tab, 1)
            for hf in range(2):
                k = 2 + 4 * hf
                sp_a, sp_u = sp_a_of[hf], sp_u_of[hf]
                dve.wait_ge(sp_act, 2 * C + 5 + hf)
                dve.wait_ge(sp_dve, k)
                v.scalar_tensor_tensor(sp_e[hf], sp_u, -1.0, sp_e[hf], ALU.add, ALU.subtract).then_inc(sp_dve, 1)
                v.scalar_tensor_tensor(sp_a, sp_a, 0.0, sp_l[hf], ALU.max, ALU.add).then_inc(sp_dve, 1)
                dve.wait_ge(sp_dve, k + 2)
                v.tensor_tensor(sp_a, sp_a, sp_e[hf], ALU.subtract).then_inc(sp_dve, 1)
                dve.wait_ge(sp_dve, k + 3)
                dve.wait_ge(sq_moved, 2)
                dtv = sp_a.rearrange("p (t c b) -> p t c b", c=C, b=B)
                v.tensor_tensor(sp_u.rearrange("p (t c b) -> p t c b", c=C, b=B), dtv,
                                spread(k_sq[:, hf * HL:(hf + 1) * HL, :], 2, C), ALU.mult).then_inc(sp_dve, 1)
                dve.wait_ge(sp_dve, k + 4)
                v.tensor_scalar(sp_u, sp_u, 1.0, None, ALU.add).then_inc(tab, 1)
            dve.wait_ge(tab, 10)
            dve.wait_ge(k_out, 16)

            e_bank, a_bank, mg_bank, sp_bank, g2_bank = bank[0], bank[1], bank[2], bank[4], bank[5]
            a_view = a_bank[:, 0:2 * C * B].rearrange("p (e c b) -> p e c b", e=2, c=C)

            def save_y(t):
                v.tensor_copy(y_a[:, bass.ds(t, 1)].rearrange("p o c b -> p (o c) b"), a_view[:, 1]).then_inc(y_saved, 1)

            with dve.Fori(0, L // 2) as i:
                for par in range(2):
                    t = i * 2 + par
                    dve.wait_ge(err_ready, t + 1)
                    v.tensor_copy(e_c[:, :], e_bank[:, 0:P]).then_inc(e_copied, 1)
                    v.reciprocal(eps[:, :], eps_a[:, bass.ds(t, 1)].rearrange("p o c b -> p (o c b)")).then_inc(recip_ready, 1)
                    dve.wait_ge(recip_ready, t + 1)
                    v.tensor_tensor(eps[:, :], eps[:, :], y_a[:, bass.ds(t, 1)].rearrange("p o c b -> p (o c b)"),
                                    ALU.mult).then_inc(eps_ready, 1)
                    dve.wait_ge(eps_ready, t + 1)
                    dve.wait_ge(a_ready, t + 1)
                    v.tensor_tensor(g_a, a_view[:, 0], eps[:, :].rearrange("p (c b) -> p c b", b=B),
                                    ALU.mult).then_inc(g_ready, 1)
                    save_y(t)
                    dve.wait_ge(mg_ready, t + 1)
                    v.tensor_tensor(mg_m[:, :, :], mg_bank[:, 0:P + B].rearrange("p (n b) -> p n b", b=B),
                                    spread(tile_mask[:, :], 1, N + 1), ALU.mult).then_inc(mgm_ready, 1)
                    dve.wait_ge(mgm_ready, t + 1)
                    v.tensor_reduce(u_row[:, :], mg_m[:, :, :], AX.X, ALU.add).then_inc(ur_ready, 1)
                    dve.wait_ge(outer_ready, t + 1)
                    v.tensor_tensor(m_a[0], m_a[0], outer[:, 0, :], ALU.add).then_inc(ma0_ready, 1)
                    dve.wait_ge(spread_ready, t + 1)
                    dve.wait_ge(now_ready, t + 1)
                    v.tensor_tensor_reduce(junk2[:, :], sp_bank[:, 0:N + 1], now_all[par][:, 0:N + 1], 1.0, 0.0, ALU.mult,
                                           ALU.add, v_col).then_inc(v_ready, 1)
                    v.tensor_tensor_reduce(junk[:, :], sp_bank[:, 0:N + 1], now[par][:, F_TRACE], 1.0, trace,
                                           ALU.mult, ALU.add, trace1).then_inc(trace1_ready, 1)
                    v.scalar_tensor_tensor(gram1[:, :], sp_bank[:, 0:N], now[par][:, F_COL], gram[:, :], ALU.mult,
                                           ALU.add).then_inc(gram1_ready, 1)
                    dve.wait_ge(trace1_ready, t + 1)
                    v.tensor_scalar(trace, trace1, 0.0, None, ALU.max).then_inc(trace_ready, 1)
                    dve.wait_ge(gram1_ready, t + 1)
                    v.scalar_tensor_tensor(gram[:, :], now[par][:, F_ROW], v_col, gram1[:, :], ALU.mult,
                                           ALU.add).then_inc(gram_ready, 1)
                    dve.wait_ge(root_ready, t + 1)
                    v.tensor_scalar(norm, root, now[par][:, F_TINY], -1.0, ALU.add, ALU.mult).then_inc(norm_ready, 1)
                    dve.wait_ge(gram_ready, t + 1)
                    v.tensor_tensor(gram_bd[:, :, :], spread(gram[:, :], 2, B), block_mask[:, :, :], ALU.mult).then_inc(bd_ready, 1)
                    dve.wait_ge(norm_ready, t + 1)
                    v.reciprocal(rneg, norm).then_inc(rneg_ready, 1)
                    v.tensor_tensor_reduce(junk3[:, :], gram[:, :], now[par][:, F_NEXT], 1.0, 0.0, ALU.mult,
                                           ALU.add, gk_col).then_inc(gk_ready, 1)
                    dve.wait_ge(rneg_ready, t + 1)
                    v.tensor_scalar(r2b, rneg, rneg, NS_B, ALU.mult, ALU.mult).then_inc(r2b_ready, 1)
                    v.tensor_scalar(r2c, rneg, rneg, NS_C / NS_B, ALU.mult, ALU.mult).then_inc(r2c_ready, 1)
                    dve.wait_ge(r2b_ready, t + 1)
                    v.scalar_tensor_tensor(ak_col, gk_col, r2b, now[par][:, F_AK], ALU.mult, ALU.add).then_inc(ak_ready, 1)
                    dve.wait_ge(r2c_ready, t + 1)
                    v.tensor_tensor(r4, r2b, r2c, ALU.mult).then_inc(r4_ready, 1)
                    dve.wait_ge(r4_ready, t + 1)
                    dve.wait_ge(gram2_ready, t + 1)
                    v.tensor_tensor_reduce(junk4[:, :], g2_bank[:, 0:N], now[par][:, F_NEXT], r4, ak_col, ALU.mult,
                                           ALU.add, w_col).then_inc(w_ready, 1)
                    v.scalar_tensor_tensor(poly[:, :], g2_bank[:, 0:N], r2c, gram[:, :], ALU.mult, ALU.add).then_inc(poly_ready, 1)
                    dve.wait_ge(w_ready, LEAD + t + 1)
                    v.tensor_scalar(w_bd[:, :], batch_mask, w_col, rneg, ALU.mult, ALU.mult).then_inc(wbd_ready, 1)
                    dve.wait_ge(poly_ready, t + 1)
                    v.scalar_tensor_tensor(ns_p[:, :], poly[:, :], r2b, scaled_eye, ALU.mult, ALU.add).then_inc(p_ready, 1)
                    dve.wait_ge(p_ready, t + 1)
                    dve.wait_ge(s_ready, t + 1)
                    v.scalar_tensor_tensor(p_bd[:, :, :], spread(ns_p[:, :], 2, B), rneg, block_mask[:, :, :],
                                           ALU.mult, ALU.mult).then_inc(pbd_ready, 1)
            for t in (L, L + 1):
                dve.wait_ge(base_ready, t + 1)
                v.tensor_copy(e_c[:, :], e_bank[:, 0:P]).then_inc(e_copied, 1)
                dve.wait_ge(a_ready, t + 1)
                save_y(t)

            mean_var = stat[0:L, 48:64].rearrange("p (b v) -> p b v", b=B)

            def layer_norm(src, src_ready, rows_per, make, dst, n, done):
                for j in range(B // rows_per + 1):
                    if j < B // rows_per:
                        make(j)
                    if j > 0:
                        dve.wait_ge(src_ready, j)
                        for b in range((j - 1) * rows_per, j * rows_per):
                            v.bn_stats(stat[0:L, 6 * b:6 * b + 6], src[0:L, b, :]).then_inc(ln, 1)
                for b in range(B):
                    dve.wait_ge(ln, n * 17 + b + 1)
                    v.bn_aggr(mean_var[:, b, :], stat[0:L, 6 * b:6 * b + 6]).then_inc(ln, 1)
                dve.wait_ge(std_ready, n + 1)
                v.reciprocal(stat[0:L, 160:168], stat[0:L, 64:72]).then_inc(ln, 1)
                dve.wait_ge(ln, n * 17 + 17)
                for b in range(B):
                    v.tensor_scalar(dst[0:L, b, :], src[0:L, b, :], mean_var[:, b, 0:1], stat[0:L, 160 + b:161 + b],
                                    ALU.subtract, ALU.mult).then_inc(done, 1)

            def prepare_mask(b, par, loads):
                dve.wait_ge(ctx_in[par], loads * 32)
                dve.wait_ge(kp_moved, LEAD + b * 4)
                v.tensor_copy(mask_f, mask_i[par][:, :]).then_inc(msk, 1)
                dve.wait_ge(msk, LEAD + b * 3 + 1)
                v.tensor_scalar(mask_f, mask_f, 0.0, None, ALU.not_equal).then_inc(msk, 1)
                dve.wait_ge(msk, LEAD + b * 3 + 2)
                v.tensor_scalar(mask_f, mask_f, mask_gain, mask_base, ALU.mult, ALU.add).then_inc(msk, 1)

            def move_k(b, par, g, src):
                dve.wait_ge(kp_ready, LEAD + b * 4 + (g + 1))
                if g == 0:
                    dve.wait_ge(msk, LEAD + b * 3 + 3)
                v.scalar_tensor_tensor(k_t[par][:, g, :], src[:, 0:S2], bias_qk[:, 1, g:g + 1], mask_f,
                                       ALU.add, ALU.mult).then_inc(kp_moved, 1)

            def move_v(b, par, k, src):
                dve.wait_ge(vp_ready, LEAD + b * KC + (k + 1))
                v.tensor_tensor(v_t[par][0:KW, k, :, 0:DK], src[0:KW, 0:DM].rearrange("p (h e) -> p h e", h=H),
                                bias_rows[0:KW, 0, :].rearrange("p (h e) -> p h e", h=H), ALU.add).then_inc(vp_moved, 1)

            def maximum(b, g, h):
                hh = 4 * g + h
                dve.wait_ge(sc_ready, LEAD + b * H + (hh + 1))
                v.tensor_reduce(row_max[g % 2][0:L, h:h + 1], bank[hh % 3][0:L, 0:S2], AX.X,
                                ALU.max, negate=True).then_inc(max_ready, 1)

            def move_probs(b, g, h):
                dve.wait_ge(pt_ready, LEAD + b * H + (4 * g + h + 1))
                dve.wait_ge(pv_ready, LEAD + b * 4 + (g - 1))
                v.tensor_copy(prob_t[g % 2][0:KW, :, h * L:(h + 1) * L],
                              bank[3 + h % 2][0:KW, 0:KC * L].rearrange("p (k q) -> p k q", k=KC)).then_inc(pt_moved, 1)

            def divide(b):
                dve.wait_ge(ot_ready, LEAD + b + 1)
                o_t = bank[7][0:L, :].rearrange("p (h e) -> p h e", h=H)
                v.reciprocal(row_inv[0:L, :], o_t[:, :, DK]).then_inc(inv_ready, 1)
                dve.wait_ge(inv_ready, LEAD + b + 1)
                v.tensor_tensor(att[0:L, bass.ds(b, 1), :].rearrange("p o (h e) -> p (o h) e", h=H), o_t[:, :, 0:DK],
                                spread(row_inv[0:L, :], 2, DK), ALU.mult).then_inc(att_ready, 1)

            def batch(b, par, loads, first=False, last=False):
                nxt = b + 1
                for g in range(4):
                    for h in range(4):
                        if h == 3 and g > 0 and not last:
                            move_v(nxt, 1 - par, g - 1, bank[7])
                        if g < 3:
                            maximum(b, g + 1, h)
                        elif not last:
                            maximum(nxt, 0, h)
                        if h % 2 == 0:
                            move_probs(b, g, h)
                        if h == 1 and not last:
                            if g == 0:
                                prepare_mask(nxt, 1 - par, loads)
                            move_k(nxt, 1 - par, g, bank[6])
                        if h == 1 and g == 1 and not first:
                            divide(b - 1)

            dve.wait_ge(y_saved, LEAD + LP)
            dve.wait_ge(ma_ready, L)
            v.tensor_scalar(q_bias, bias_qk[:, 0, :], DK ** -0.5, None, ALU.mult).then_inc(qb_ready, 1)
            prepare_mask(0, 0, 1)
            for g in range(4):
                move_k(0, 0, g, bank[4 + g])
            for k in range(KC):
                move_v(0, 0, k, bank[1 + k])
            dve.wait_ge(att_in, 16 * 8)
            def add_x(j):
                dve.wait_ge(proj_ready, 2 * j + 2)
                v.tensor_tensor(h1[0:L, 2 * j:2 * j + 2, :], bank[j][0:L, :].rearrange("p (b d) -> p b d", b=2),
                                xb[0:L, 2 * j:2 * j + 2, :], ALU.add).then_inc(h1_ready, 1)

            layer_norm(h1, h1_ready, 2, add_x, x1, 0, x1_ready)
            for hf in range(2):
                dve.wait_ge(x1t_ready, 4 * hf + 4)
                v.tensor_copy(x1t[:, 1, hf * HT:(hf + 1) * HT], bank[6 + hf][:, 0:HT]).then_inc(x1t_moved, 1)
            dve.wait_ge(qb_ready, 1)
            for hf in range(2):
                for g in range(2, 4):
                    dve.wait_ge(qp_ready, 4 * hf + g + 1)
                    v.tensor_scalar(q_s[:, g, hf * HT:(hf + 1) * HT], bank[4 * hf + g][:, 0:HT], DK ** -0.5,
                                    q_bias[:, g:g + 1], ALU.mult, ALU.add).then_inc(q_moved, 1)
            dve.wait_ge(q_moved, 4)
            dve.wait_ge(q_copied, 4)
            for h in range(4):
                maximum(0, 0, h)
            batch(0, 0, 1, first=True)
            with dve.Fori(0, B // 2 - 1) as i:
                batch(i * 2 + 1, 1, i + 2)
                batch(i * 2 + 2, 0, i + 2)
            batch(B - 1, 1, None, last=True)
            divide(B - 1)

            def move_turned(dst, ready, moved):
                for hf in range(2):
                    dve.wait_ge(ready, 4 * hf + 4)
                    v.tensor_copy(dst[:, 1, hf * HT:(hf + 1) * HT], bank[2 + hf][:, 0:HT]).then_inc(moved, 1)

            move_turned(at_t, att_t_ready, att_moved)
            dve.wait_ge(x1b_ready, 1)
            def add_x1(j):
                dve.wait_ge(wo_ready, 2 * j + 2)
                v.tensor_tensor(h1[0:L, 2 * j:2 * j + 2, :], bank[4 + j][0:L, :].rearrange("p (b d) -> p b d", b=2),
                                xb[0:L, 2 * j:2 * j + 2, :], ALU.add).then_inc(h2_ready, 1)

            layer_norm(h1, h2_ready, 2, add_x1, x2, 1, x2_ready)
            move_turned(x2t, x2t_ready, x2t_moved)
            dve.wait_ge(lg_ready, 1)
            logits = bank[4][0:L, 0:B * E].rearrange("p (b e) -> p b e", b=B)
            v.tensor_reduce(top_logit[0:L, :], logits, AX.X, ALU.max).then_inc(top, 1)
            dve.wait_ge(top, 1)
            v.tensor_tensor(lg[0:L], logits, spread(top_logit[0:L, :], 2, E), ALU.is_equal).then_inc(top, 1)
            dve.wait_ge(top, 2)
            v.tensor_tensor(lg[0:L], lg[0:L], spread(tie_rank[0:L, :], 1, B), ALU.mult).then_inc(top, 1)
            dve.wait_ge(top, 3)
            v.tensor_reduce(top_rank[0:L, :], lg[0:L], AX.X, ALU.max).then_inc(top, 1)
            dve.wait_ge(top, 4)
            v.tensor_tensor(onehot[0:L], lg[0:L], spread(top_rank[0:L, :], 2, E), ALU.is_equal).then_inc(top, 1)
            def by(ap, n=B):
                return ap.rearrange("p (b e) -> p b e", b=n)

            step = [0]

            def after(ins):
                ins.then_inc(route_step, 1)
                step[0] += 1
                dve.wait_ge(route_step, step[0])

            dve.wait_ge(count_ready, 2)
            after(v.tensor_copy(r_tot, bank[6][:, 0:B * E]))
            v.tensor_reduce(r_cnt, by(r_tot).rearrange("p b e -> p e b"), AX.X, ALU.add).then_inc(route_step, 1)
            v.memset(r_pre[:, 0:E], 0.0).then_inc(route_step, 1)
            step[0] += 2
            dve.wait_ge(route_step, step[0])
            after(v.tensor_tensor(by(r_cmp, E), spread(r_cnt, 2, E), spread(tile_start, 1, E), ALU.is_gt))
            after(v.tensor_reduce(r_tiles, by(r_cmp, E), AX.X, ALU.add))
            after(v.tensor_tensor(by(r_tri, E), spread(r_tiles, 1, E), by(before_e, E), ALU.mult))
            after(v.tensor_reduce(r_base, by(r_tri, E), AX.X, ALU.add))
            for b in range(1, B):
                after(v.tensor_tensor(r_pre[:, b * E:(b + 1) * E], r_pre[:, (b - 1) * E:b * E], r_tot[:, (b - 1) * E:b * E], ALU.add))
            after(v.scalar_tensor_tensor(by(r_pre), spread(r_base, 1, B), float(P), by(r_pre), ALU.mult, ALU.add))
            after(v.tensor_tensor(r_pos[0:L, :], bank[5][0:L, 0:B * E], r_pre[0:L, :], ALU.add))
            after(v.tensor_tensor(by(r_pos)[0:L], by(r_pos)[0:L], onehot[0:L], ALU.mult))
            after(v.tensor_reduce(r_slot[0:L, :], by(r_pos)[0:L], AX.X, ALU.add))
            v.tensor_copy(slot_i[0:L, :], r_slot[0:L, :]).then_inc(route_ready, 1)

            for k in range(8):
                f, hf = k // 2, k % 2
                dve.wait_ge(up_ready, k + 1)
                dve.wait_ge(silu_ready, k + 1)
                v.tensor_tensor(hid[:, f, hf * HT:(hf + 1) * HT], bank[2 + k % 2][:, 0:HT], gate[:, k % 2, :],
                                ALU.mult).then_inc(hid_ready, 1)
                if k == 1:
                    after(v.tensor_tensor(r_end, r_base, r_tiles, ALU.add))
                    after(v.tensor_tensor(by(r_end_cmp, NT), spread(r_end, 1, NT), spread(tile_no, 2, E), ALU.is_le))
                    after(v.tensor_reduce(r_tile, by(r_end_cmp, NT), AX.X, ALU.add))
                    after(v.tensor_scalar(r_tile, r_tile, float(E - 1), None, ALU.min))
                    after(v.tensor_tensor(r_tile, r_tile, digit, ALU.mult))
                    after(v.tensor_reduce(r_cnt[:, 0:2], r_tile.rearrange("p (k u) -> p u k", u=2), AX.X, ALU.add))
                    v.tensor_copy(expert_i[:, :], r_cnt[:, 0:2]).then_inc(route_ready, 1)
            for b in range(B):
                dve.wait_ge(down_ready, b + 1)
                v.tensor_tensor(acc[0:L, b, :], bank[4 + b % 2][0:L, 0:DM], x2[0:L, b, :], ALU.add).then_inc(acc_ready, 1)

            def routed_tile(par, j):
                dve.wait_ge(ru_ready, LEAD + j + 1)
                dve.wait_ge(rsilu_ready, LEAD + j + 1)
                dve.wait_ge(rht_ready, LEAD + j - 1)
                v.tensor_tensor(hid_r[par], bank[2 + par][:, :], silu_r[par], ALU.mult).then_inc(rhid_ready, 1)
                dve.wait_ge(rht_ready, LEAD + j + 1)
                dve.wait_ge(ry_ready, LEAD + j - 1)
                v.tensor_copy(hid_t[par], bank[4][:, :]).then_inc(rht_moved, 1)

            with dve.Fori(0, NT // 2) as i:
                routed_tile(0, i * 2)
                routed_tile(1, i * 2 + 1)
            for b in range(B + 1):
                if b < B:
                    dve.wait_ge(back_in[b], 16)
                    v.tensor_tensor(acc[0:L, b, :], acc[0:L, b, :], att[0:L, b, :], ALU.add).then_inc(sum_ready, 1)
                if b > 0:
                    dve.wait_ge(std_ready, 2 + b)
                    v.reciprocal(stat[0:L, 159 + b:160 + b], stat[0:L, 63 + b:64 + b]).then_inc(inv_std_ready, 1)
                if b < B:
                    dve.wait_ge(sum_ready, b + 1)
                    v.bn_stats(stat[0:L, 6 * b:6 * b + 6], acc[0:L, b, :]).then_inc(stats_ready, 1)
                if b > 0:
                    dve.wait_ge(inv_std_ready, b)
                    v.tensor_scalar(h1[0:L, b - 1, :], acc[0:L, b - 1, :], mean_var[:, b - 1, 0:1],
                                    stat[0:L, 159 + b:160 + b], ALU.subtract, ALU.mult).then_inc(y_ready, 1)
                if b < B:
                    dve.wait_ge(stats_ready, b + 1)
                    v.bn_aggr(mean_var[:, b, :], stat[0:L, 6 * b:6 * b + 6]).then_inc(var_ready, 1)

        @block.scalar
        def _(act):
            a = nc.scalar.activation
            act.wait_ge(pre_in, 64)
            for c in range(C):
                act.wait_ge(conv_step, (c + 1) * W)
                a(x_a[:, 0:L, c, :], conv[:, c % 2, :].rearrange("p (t b) -> p t b", b=B), ACT.Silu,
                  bias=vecs[:, 0, c:c + 1]).then_inc(x_ready, 1)
            for hf in range(2):
                for c in range(C):
                    act.wait_ge(dt_ready, hf * C + c + 1)
                    a(sp_a_of[hf].rearrange("p (t c b) -> p t c b", c=C, b=B)[:, :, c, :],
                      bank[c][:, 0:HT].rearrange("p (t b) -> p t b", b=B), ACT.Identity,
                      bias=vecs[:, 1, c:c + 1]).then_inc(sp_act, 1)
            act.wait_ge(sp_act, 2 * C)
            act.wait_ge(xz_ready, 2 * C)
            act.wait_ge(conv_step, C * W)
            act.wait_ge(x_ready, C)
            act.wait_ge(kq_ready, 4)
            for hf in range(2):
                a(sp_e[hf], sp_a_of[hf], ACT.Abs).then_inc(sp_act, 1)
            for hf in range(2):
                act.wait_ge(sp_act, 2 * C + hf + 1)
                a(sp_e[hf], sp_e[hf], ACT.Exp, scale=-1.0).then_inc(sp_act, 1)
            for hf in range(2):
                act.wait_ge(sp_dve, hf + 1)
                a(sp_l[hf], sp_u_of[hf], ACT.Ln).then_inc(sp_act, 1)
            for n in range(2 * C):
                c, hf = n // 2, n % 2
                act.wait_ge(xz_ready, 2 * C + n + 1)
                a(z_a[:, hf * HL:(hf + 1) * HL, c, :], bank[n % 4][:, 0:HT].rearrange("p (t b) -> p t b", b=B),
                  ACT.Silu).then_inc(z_done, 1)
            act.wait_ge(zeroed, 12)
            act.wait_ge(base_ready, 1)
            with act.Fori(0, L // TURN) as i:
                a(dummy, cols[:, 12:13], ACT.Sqrt)
                for u in range(TURN):
                    t = i * TURN + u
                    act.wait_ge(trace_ready, t + 1)
                    a(root, trace, ACT.Sqrt).then_inc(root_ready, 1)
                    act.wait_ge(s_ready, t + 1)
                    act.wait_ge(base_ready, t + 1)
                    nc.scalar.copy(s_b[:, :, :].rearrange("p c n -> p (c n)"), bank[6][:, :]).then_inc(sb_ready, 1)
                    act.wait_ge(mt_ready, t + 1)
                    nc.scalar.copy(m_b[:, :, :].rearrange("p c n -> p (c n)"), bank[7][:, :]).then_inc(mb_ready, 1)
            act.wait_ge(s_ready, L + 1)
            act.wait_ge(base_ready, L + 1)
            nc.scalar.copy(s_b[:, :, :].rearrange("p c n -> p (c n)"), bank[6][:, :]).then_inc(sb_ready, 1)

            def deviation(n):
                act.wait_ge(ln, n * 17 + 16)
                a(stat[0:L, 64:72], stat[0:L, 48:64].rearrange("p (b v) -> p b v", b=B)[:, :, 1], ACT.Sqrt,
                  bias=eps_ln[0:L, :]).then_inc(std_ready, 1)

            def move_turned(dst, ready, moved, first_bank):
                for hf in range(2):
                    act.wait_ge(ready, 4 * hf + 4)
                    nc.scalar.copy(dst[:, 0, hf * HT:(hf + 1) * HT], bank[first_bank + hf][:, 0:HT]).then_inc(moved, 1)

            def copy_values(b):
                act.wait_ge(pv_ready, LEAD + b * 4 + 4)
                act.wait_ge(ot_ready, LEAD + b)
                nc.scalar.copy(o_raw.rearrange("p g q -> p (g q)"), bank[5][:, 0:4 * L]).then_inc(o_copied, 1)

            def exponent(b, g, h, fresh=False):
                hh = 4 * g + h
                act.wait_ge(max_ready, LEAD + b * H + (hh + 1))
                if not fresh:
                    act.wait_ge(pt_ready, LEAD + b * H + (hh - 3))
                a(prob[h][0:L, :], bank[hh % 3][0:L, 0:S2], ACT.Exp, bias=row_max[g % 2][0:L, h:h + 1]).then_inc(exp_ready, 1)

            def copy_probs(b, g, h):
                act.wait_ge(pt_ready, LEAD + b * H + (4 * g + h + 1))
                act.wait_ge(pv_ready, LEAD + b * 4 + (g - 1))
                nc.scalar.copy(prob_t[g % 2][0:KW, :, h * L:(h + 1) * L],
                               bank[3 + h % 2][0:KW, 0:KC * L].rearrange("p (k q) -> p k q", k=KC)).then_inc(pt_copied, 1)

            def batch(b, first=False, last=False):
                for g in range(4):
                    for h in range(4):
                        if h % 2 == 1:
                            copy_probs(b, g, h)
                        if g < 3:
                            exponent(b, g + 1, h)
                        elif not last:
                            exponent(b + 1, 0, h)
                        if g == 0 and h == 2 and not first:
                            copy_values(b - 1)

            deviation(0)
            move_turned(x1t, x1t_ready, x1t_copied, 4)
            act.wait_ge(qb_ready, 1)
            for hf in range(2):
                for g in range(2):
                    act.wait_ge(qp_ready, 4 * hf + g + 1)
                    a(q_s[:, g, hf * HT:(hf + 1) * HT], bank[4 * hf + g][:, 0:HT], ACT.Identity,
                      bias=q_bias[:, g:g + 1], scale=DK ** -0.5).then_inc(q_copied, 1)
            for h in range(4):
                exponent(0, 0, h, fresh=True)
            batch(0, first=True)
            with act.Fori(1, B - 1) as b:
                batch(b)
            batch(B - 1, last=True)
            copy_values(B - 1)
            move_turned(at_t, att_t_ready, att_copied, 0)
            deviation(1)
            move_turned(x2t, x2t_ready, x2t_copied, 0)
            act.wait_ge(top, 1)
            a(score[0:L, :], top_logit[0:L, :], ACT.Sigmoid).then_inc(score_ready, 1)
            act.wait_ge(x2_ready, B)
            act.wait_ge(score_ready, 1)
            for b in range(B):
                a(xs[0:L, b, :], x2[0:L, b, :], ACT.Copy, scale=score[0:L, b:b + 1]).then_inc(xs_ready, 1)

            for k in range(8):
                act.wait_ge(gate_ready, k + 1)
                if k >= 2:
                    act.wait_ge(hid_ready, k - 1)
                a(gate[:, k % 2, :], bank[k % 2][:, 0:HT], ACT.Silu).then_inc(silu_ready, 1)

            def move_rows(par, j):
                act.wait_ge(turned, LEAD + j + 1)
                act.wait_ge(ru_ready, LEAD + j - 1)
                nc.scalar.copy(rows_t[par], bank[7][:, 0:DM]).then_inc(turned_moved, 1)

            def silu_rows(par, j):
                act.wait_ge(rg_ready, LEAD + j + 1)
                act.wait_ge(rhid_ready, LEAD + j - 1)
                a(silu_r[par], bank[par][:, :], ACT.Silu).then_inc(rsilu_ready, 1)

            def move_out(par, j, stored):
                act.wait_ge(ry_ready, LEAD + j + 1)
                if stored is not None:
                    act.wait_ge(tile_out[par], 16 * stored)
                nc.scalar.copy(y_r[par], bank[5 + par][:, 0:DM]).then_inc(ry_moved, 1)

            move_rows(0, 0)
            silu_rows(0, 0)
            move_rows(1, 1)
            silu_rows(1, 1)
            move_rows(0, 2)
            move_out(0, 0, None)
            silu_rows(0, 2)
            move_rows(1, 3)
            move_out(1, 1, None)
            with act.Fori(1, NT // 2 - 1) as i:
                silu_rows(1, i * 2 + 1)
                move_rows(0, i * 2 + 2)
                move_out(0, i * 2, i)
                silu_rows(0, i * 2 + 2)
                move_rows(1, i * 2 + 3)
                move_out(1, i * 2 + 1, i)
            silu_rows(1, NT - 1)
            move_out(0, NT - 2, NT // 2 - 1)
            move_out(1, NT - 1, NT // 2 - 1)
            for b in range(B):
                act.wait_ge(var_ready, b + 1)
                a(stat[0:L, 64 + b:65 + b], stat[0:L, 49 + 2 * b:50 + 2 * b], ACT.Sqrt, bias=eps_ln[0:L, :]).then_inc(std_ready, 1)

        @block.gpsimd
        def _(pool):
            pool.wait_ge(zeroed, 12)
            pool.wait_ge(ks_in[0], 16)
            pool.wait_ge(row_moved, 4)
            pool.wait_ge(tab, 8)

            def gate_y(s):
                def row(table, r):
                    return table[:, bass.ds(r, 1)].rearrange("p o c b -> p (o c) b")

                pool.wait_ge(gated, LEAD + s)
                nc.gpsimd.tensor_tensor(y_now[:, :, :], row(x_a, s), spread(vecs[:, 2, :], 2, B), ALU.mult).then_inc(dx_ready, 1)
                pool.wait_ge(y_saved, LEAD + s + 3)
                pool.wait_ge(dx_ready, s + 1)
                nc.gpsimd.tensor_tensor(y_now[:, :, :], y_now[:, :, :], row(y_a, s + 2), ALU.add).then_inc(ydx_ready, 1)
                pool.wait_ge(ydx_ready, s + 1)
                nc.gpsimd.tensor_tensor(row(z_a, s), y_now[:, :, :], row(z_a, s), ALU.mult).then_inc(gated, 1)

            def two_steps(i, first=False):
                for par in range(2):
                    t = i * 2 + par
                    pool.wait_ge(w_ready, LEAD + i * 2)
                    pool.wait_ge(base_ready, i * 2 + 1)
                    nc.gpsimd.tensor_copy(now[par][:, 0:REC], rec[:, bass.ds(t, 1), :].rearrange("p o f -> p (o f)")).then_inc(now_ready, 1)
                    pool.wait_ge(g_ready, t + 1)
                    pool.wait_ge(ma0_ready, LEAD + t)
                    nc.gpsimd.tensor_tensor(outer[:, :, :].rearrange("p c (n b) -> p c n b", b=B),
                                            spread(g_a, 2, N),
                                            spread(ks_all[:, bass.ds(t, 1), :].rearrange("p o (n b) -> p (o n) b", b=B), 1, C),
                                            ALU.mult).then_inc(outer_ready, 1)
                    pool.wait_ge(outer_ready, t + 1)
                    pool.wait_ge(mg_ready, t + 1)
                    flat_m = m_g[:, 1:C, 0:N, :].rearrange("p c n b -> p c (n b)")
                    nc.gpsimd.tensor_tensor(flat_m, flat_m, outer[:, 1:C, :], ALU.add).then_inc(ma_ready, 1)
                    if not first:
                        gate_y(t - 2)

            two_steps(0, first=True)
            pool.wait_ge(ks_in[1], 3 * 16)
            with pool.Fori(1, L // 2) as i:
                two_steps(i)
            gate_y(L - 2)
            gate_y(L - 1)
            pool.wait_ge(now_ready, L)
            for par in range(2):
                nc.gpsimd.memset(v_t[par][:, :, :, DK:], 1.0).then_inc(cleared, 1)

            def q_blocks(b, g, fresh=False):
                if not fresh:
                    pool.wait_ge(sc_ready, LEAD + b * H + 4 * (g - 1))
                nc.gpsimd.tensor_tensor(q_bd[g % 2], spread(q_s[:, g, bass.ds(b * L, L)], 1, 4),
                                        spread(head_rows, 2, L), ALU.mult).then_inc(qbd_ready, 1)

            def batch(b, last=False):
                for g in range(4):
                    if g < 2:
                        q_blocks(b, g + 2)
                    elif not last:
                        q_blocks(b + 1, g - 2)

            pool.wait_ge(q_moved, 4)
            pool.wait_ge(q_copied, 4)
            q_blocks(0, 0, fresh=True)
            q_blocks(0, 1, fresh=True)
            batch(0)
            with pool.Fori(1, B - 1) as b:
                batch(b)
            batch(B - 1, last=True)
            pool.wait_ge(x1_ready, B)
            nc.gpsimd.tensor_tensor(xb[0:L], x1[0:L], spread(bias_rows[0:L, 1, :], 1, B), ALU.add).then_inc(x1b_ready, 1)
            pool.wait_ge(rows_zero, 16)
            pool.wait_ge(route_ready, 1)
            for b in range(B):
                pool.wait_ge(xs_ready, b + 1)
                pool.indirect_dma_start(rows_dram, bass.IndirectOffsetOnAxis(ap=slot_i[0:L, b:b + 1], axis=0),
                                        xs[0:L, b, :], None).then_inc(rows_out, 16)
            pool.wait_ge(rows_out, 16 * B)

            def load_rows(par, j):
                pool.dma_start(rows_in[par], rows_dram[bass.ds(j * P, P), :]).then_inc(rows_in_ready[par], 16)

            def store_rows(par, j):
                pool.wait_ge(ry_moved, LEAD + j + 1)
                pool.dma_start(out_dram[bass.ds(j * P, P), :], y_r[par]).then_inc(tile_out[par], 16)

            load_rows(0, 0)
            load_rows(1, 1)
            with pool.Fori(0, NT // 2 - 1) as i:
                pool.wait_ge(turned, LEAD + i * 2 + 1)
                load_rows(0, i * 2 + 2)
                pool.wait_ge(turned, LEAD + i * 2 + 2)
                load_rows(1, i * 2 + 3)
                store_rows(0, i * 2)
                store_rows(1, i * 2 + 1)
            store_rows(0, NT - 2)
            store_rows(1, NT - 1)
            for par in range(2):
                pool.wait_ge(tile_out[par], 16 * (NT // 2))
            for b in range(B):
                pool.indirect_dma_start(att[0:L, b, :], None, out_dram,
                                        bass.IndirectOffsetOnAxis(ap=slot_i[0:L, b:b + 1], axis=0)).then_inc(back_in[b], 16)


def _constants():
    f = np.float32
    p = np.arange(P)
    small = np.zeros((P, 64), f)
    small[:, 0:8] = (p[:, None] % B == np.arange(B))
    small[:, 8:12] = (p[:, None] // 32 == np.arange(4))
    small[:, 16:32] = (p[:, None] // B == np.arange(N))
    small[:, 32:48] = NS_A * small[:, 16:32]
    mask_row = p % 32 == DK
    small[:, 48] = np.where(mask_row, NEG, 1.0)
    small[:, 49] = np.where(mask_row, -NEG, 0.0)
    small[:, 50] = EPS
    small[:, 52:60] = E - np.arange(E)
    route = np.zeros((P, 112), f)
    route[:, 96:96 + NT] = E ** (np.arange(NT) // 2)
    route[:, 0:64] = (np.arange(E)[None, :] < np.arange(E)[:, None]).reshape(-1)
    route[:, 64:72] = P * np.arange(E)
    route[:, 72:72 + NT] = np.arange(NT)
    gain = np.float64(BETA) ** -np.arange(L)
    block = (p[:, None] % B == p[None, :] % B).astype(f)
    used = p[:, None] % 32 < B
    row_of = 32 * (np.arange(C * B) // B) + np.arange(C * B) % B
    pick = np.concatenate([p[:, None] == row_of, p[:, None] == row_of + B], 1).astype(f)
    return {
        "c_ident": np.eye(P, dtype=f), "c_neg": -np.eye(P, dtype=f), "c_ones": np.ones((P, P), f),
        "c_block": block, "c_small": small, "c_bmask": block.reshape(P, N, B),
        "c_pick": pick, "c_spread": (used & (p[:, None] % 32 == p[None, :] % B)).astype(f),
        "c_tile": (used & (p[:, None] % 32 == np.arange(B))).astype(f),
        "c_route": route, "c_earlier": (p[:, None] < np.arange(L)).astype(f), "c_zero": np.zeros((NT * P, DM), f),
        "c_gain": np.broadcast_to(gain, (P, L)).astype(f),
    }


def _chunks(w, n=P):
    return w.reshape(-1, n, w.shape[-1]).transpose(1, 0, 2)


def _pad_heads(w):
    out = np.zeros((H, 32) + w.shape[1:], w.dtype)
    out[:, :DK] = w.reshape((H, DK) + w.shape[1:])
    return out.reshape((H * 32,) + w.shape[1:])


def _expert(gate, up, down):
    return np.concatenate([_chunks(w.T).reshape(P, -1) for w in (gate, up, down)], axis=1)


def kernel(**inputs):
    import concourse.bacc as bacc
    from concourse.bass_utils import run_bass_kernel_spmd as run

    i = {k.replace("L0_", ""): np.asarray(a) for k, a in inputs.items()}
    x = i["x"]
    xp = i["attn_x_proj_w"]
    bq, bk = _pad_heads(i["xattn_bq"]), _pad_heads(i["xattn_bk"])
    bq.reshape(H, 32)[:, DK] = DK ** 0.5
    bk.reshape(H, 32)[:, DK] = 1.0
    arrays = {
        "x": x,
        "xt": _chunks(x.transpose(2, 1, 0).reshape(DM, T)),
        "w_in": _chunks(i["attn_in_proj_w"].T),
        "conv_w": _chunks(i["attn_conv_w"].reshape(DI, W)),
        "vecs": np.stack([i[k].reshape(C, P).T for k in ("attn_conv_b", "attn_dt_head_b", "attn_D")], 1),
        "w_lo": _chunks(xp[0:R].T),
        "w_k": _chunks(np.repeat(xp[R:R + N].T, B, axis=1)),
        "w_q": _chunks(np.repeat(xp[R + N:].T, B, axis=1)),
        "w_dt": i["attn_dt_head_w"].T,
        "w_out": _chunks(i["attn_out_proj_w"].T),
        "bias_qk": np.stack([bq.reshape(4, P).T, bk.reshape(4, P).T], 1),
        "bias_rows": np.broadcast_to(np.stack([i["xattn_bv"], i["xattn_bo"]]), (P, 2, DM)),
        "wq": _chunks(_pad_heads(i["xattn_Wq"]).T),
        "wk": _chunks(_pad_heads(i["xattn_Wk"]).T),
        "wv": _chunks(i["xattn_Wv"].T),
        "wo": _chunks(i["xattn_Wo"].T),
        "w_gate": _chunks(i["ffn_gate_w"].T),
        "ctx_t": i["ctx_1024"].transpose(0, 2, 1).reshape(B, MC, P, S2).transpose(0, 2, 1, 3),
        "mask": i["mask_Bx1xS2_ik0"].reshape(B, S2),
        "w_shared": _expert(i["ffn_shared_gate"], i["ffn_shared_up"], i["ffn_shared_down"]),
        "w_r": np.stack([_expert(*w) for w in zip(i["ffn_r_gate"], i["ffn_r_up"], i["ffn_r_down"])]),
        **_constants(),
    }
    nc = bacc.Bacc("TRN2", target_bir_lowering=False, num_devices=1)
    sent, io = {}, {}
    for name, a in arrays.items():
        a = np.ascontiguousarray(a)
        sent[f"in_{name}"] = a
        io[name] = nc.dram_tensor(f"in_{name}", a.shape, mybir.dt.from_np(a.dtype), kind="ExternalInput").ap()
    out = nc.dram_tensor("out_0", (B, L, DM), F32, kind="ExternalOutput").ap()
    decoder_kernel(nc, io, out)
    r = run(nc, [sent], core_ids=[0])
    return r.results[0]["out_0"]
```
